# Optimizing a Trainium2 kernel written in Bass

```python
import numpy as np
import jax
import jax.numpy as jnp

def _softmax(x, axis=-1):
    return jax.nn.softmax(x, axis=axis)

def _gelu(x):
    return jax.nn.gelu(x, approximate=True)

def _silu(x):
    return jax.nn.silu(x)

def _sigmoid(x):
    return jax.nn.sigmoid(x)

def _layernorm(x, axis=-1, eps=1e-05):
    m = jnp.mean(x, axis=axis, keepdims=True)
    v = jnp.var(x, axis=axis, keepdims=True)
    return (x - m) / jnp.sqrt(v + eps)

def _scatter_add(tgt, idx, src, axis=0):
    return tgt.at[idx].add(src)

def _segment_sum(src, seg, n):
    return jax.ops.segment_sum(src, seg, n)
kernel_name = 'mk_decoder_preln_d1_seqx_r4_c7528b'

def setup_inputs(seed: int=0):
    np.random.seed(seed)
    _w = jnp.asarray

    def _rec_inputs():
        import jax
        import jax.numpy as jnp
        _rk = jax.random.key(seed)
        x = -0.0002928 + 1 * jax.random.normal(jax.random.fold_in(_rk, 1), (4, 1024, 256), jnp.float32)
        _lenS = 1024 - jax.random.randint(jax.random.fold_in(_rk, 7), (4,), 0, max(1, 1024 // 4) + 1, jnp.int32)
        _lenS2 = 77 - jax.random.randint(jax.random.fold_in(_rk, 8), (4,), 0, max(1, 77 // 4) + 1, jnp.int32)
        _ctx_1024P = jax.random.normal(jax.random.fold_in(_rk, 11), (4, 16, 256), jnp.float32)
        _ctx_1024c = jax.random.dirichlet(jax.random.fold_in(_rk, 511), 0.3 * jnp.ones((16,), jnp.float32), (4, 77))
        _ctx_1024t = jnp.einsum('bsk,bkd->bsd', _ctx_1024c, _ctx_1024P)
        _ctx_1024t = _ctx_1024t * jax.lax.rsqrt(jnp.mean(jnp.square(_ctx_1024t)) + 1e-12) * 0.953939
        ctx_1024 = -1.39393e-06 + 0.999914 * (_ctx_1024t + 0.3 * jax.random.normal(jax.random.fold_in(_rk, 611), (4, 77, 256), jnp.float32))
        _validS = jnp.arange(1024)[None, :] < _lenS[:, None]
        _validS2 = jnp.arange(77)[None, :] < _lenS2[:, None]
        _causal = jnp.tril(jnp.ones((1024, 1024), dtype=bool))
        mask_BxSxS2_bk1 = jnp.broadcast_to(_validS2[:, None, :], (4, 1024, 77))
        return (x, ctx_1024, mask_BxSxS2_bk1)
    x, ctx_1024, mask_BxSxS2_bk1 = _rec_inputs()

    def _L0_attn_setup():
        import jax, jax.numpy as jnp
        import numpy as np
        D_MODEL = 256
        N_HEADS = 16
        HEAD_DIM = D_MODEL // N_HEADS
        MAX_SHIFT = HEAD_DIM // 2
        BATCH, SEQ = (2, 512)

        def _forward(x, Wq, bq, Wk, bk, Wv, bv, Wo, bo, W_cross, shift_weights, gate):
            b, s, _ = x.shape
            H, hd = (W_cross.shape[0], W_cross.shape[1])
            ms = shift_weights.shape[1]
            Q = (x @ Wq.T + bq).reshape(b, s, H, hd)
            K = (x @ Wk.T + bk).reshape(b, s, H, hd)
            V = (x @ Wv.T + bv).reshape(b, s, H, hd)
            Qt = jnp.einsum('bqhf,hfg->bqhg', Q, W_cross)
            scores_cross = jnp.einsum('bqhd,bkhd->bhqk', Qt, K)
            f = jnp.arange(hd)[:, None]
            g = jnp.arange(hd)[None, :]
            tau = g - f
            valid = (tau >= 0) & (tau < ms)
            M = jnp.where(valid[None], shift_weights[:, jnp.clip(tau, 0, ms - 1)], 0.0)
            K_mixed = jnp.einsum('hfg,bkhg->bkhf', M, K)
            scores_conv = jnp.einsum('bqhf,bkhf->bhqk', Q, K_mixed)
            gt = jax.nn.sigmoid(gate).reshape(1, H, 1, 1)
            scale = hd ** (-0.5)
            scores = (gt * scores_cross + (1.0 - gt) * scores_conv) * scale
            causal = jnp.tril(jnp.ones((s, s), dtype=bool))
            scores = jnp.where(causal[None, None], scores, -jnp.inf)
            attn = jax.nn.softmax(scores, axis=-1)
            out = jnp.einsum('bhqk,bkhd->bqhd', attn, V).reshape(b, s, H * hd)
            return out @ Wo.T + bo
        key = jax.random.key(seed)
        ks = jax.random.split(key, 12)
        s = 0.02
        x = jax.random.normal(ks[0], (BATCH, SEQ, D_MODEL), dtype=jnp.float32)
        Wq = jax.random.normal(ks[1], (D_MODEL, D_MODEL), dtype=jnp.float32) * s
        bq = jnp.zeros((D_MODEL,), jnp.float32)
        Wk = jax.random.normal(ks[2], (D_MODEL, D_MODEL), dtype=jnp.float32) * s
        bk = jnp.zeros((D_MODEL,), jnp.float32)
        Wv = jax.random.normal(ks[3], (D_MODEL, D_MODEL), dtype=jnp.float32) * s
        bv = jnp.zeros((D_MODEL,), jnp.float32)
        Wo = jax.random.normal(ks[4], (D_MODEL, D_MODEL), dtype=jnp.float32) * s
        bo = jnp.zeros((D_MODEL,), jnp.float32)
        eye = jnp.broadcast_to(jnp.eye(HEAD_DIM, dtype=jnp.float32), (N_HEADS, HEAD_DIM, HEAD_DIM))
        W_cross = eye + 0.01 * jax.random.normal(ks[5], (N_HEADS, HEAD_DIM, HEAD_DIM), dtype=jnp.float32)
        decay = jnp.exp(-jnp.arange(MAX_SHIFT, dtype=jnp.float32) / (MAX_SHIFT / 4.0))
        shift_weights = jnp.broadcast_to(decay, (N_HEADS, MAX_SHIFT)).copy()
        gate = jnp.zeros((N_HEADS,), jnp.float32)
        return {'x': x, 'Wq': Wq, 'bq': bq, 'Wk': Wk, 'bk': bk, 'Wv': Wv, 'bv': bv, 'Wo': Wo, 'bo': bo, 'W_cross': W_cross, 'shift_weights': shift_weights, 'gate': gate}
    _L0_attn_all = _L0_attn_setup()
    _L0_attn_in = {k: v for k, v in _L0_attn_all.items() if k in ('Wq', 'bq', 'Wk', 'bk', 'Wv', 'bv', 'Wo', 'bo', 'W_cross', 'shift_weights', 'gate')}
    del _L0_attn_all

    def _L0_xattn_setup():
        import jax, jax.numpy as jnp
        import numpy as np
        EMBED_DIM = 256
        HEAD = 16
        DK = EMBED_DIM // HEAD
        B, S = (2, 512)
        NEG = -1000000000.0
        key = jax.random.key(seed)
        ks = jax.random.split(key, 8)
        d = {'query': jax.random.normal(ks[0], (B, S, EMBED_DIM), jnp.float32), 'key': jax.random.normal(ks[1], (B, S, EMBED_DIM), jnp.float32), 'value': jax.random.normal(ks[2], (B, S, EMBED_DIM), jnp.float32), 'masked': jax.random.randint(ks[3], (B, S, S), 0, 2).astype(bool), 'Wq': jax.random.normal(ks[4], (EMBED_DIM, EMBED_DIM), jnp.float32) / np.sqrt(EMBED_DIM), 'Wk': jax.random.normal(ks[5], (EMBED_DIM, EMBED_DIM), jnp.float32) / np.sqrt(EMBED_DIM), 'Wv': jax.random.normal(ks[6], (EMBED_DIM, EMBED_DIM), jnp.float32) / np.sqrt(EMBED_DIM), 'Wo': jax.random.normal(ks[7], (EMBED_DIM, EMBED_DIM), jnp.float32) / np.sqrt(EMBED_DIM)}
        return d
    _L0_xattn_all = _L0_xattn_setup()
    _L0_xattn_in = {k: v for k, v in _L0_xattn_all.items() if k in ('Wq', 'Wk', 'Wv', 'Wo')}
    del _L0_xattn_all

    def _L0_ffn_setup():
        import jax, jax.numpy as jnp
        import numpy as np
        DIM = 256
        HIDDEN = 768
        SCALE = 1.0 / 127.0

        def _dequant(w_int, dtype):
            return w_int.astype(dtype) * jnp.asarray(SCALE, dtype)
        key = jax.random.key(seed)
        k_x, k_g, k_u, k_d = jax.random.split(key, 4)
        x = jax.random.normal(k_x, (4, 512, DIM), dtype=jnp.float32)
        w_gate = jax.random.randint(k_g, (HIDDEN, DIM), -127, 128, dtype=jnp.int32)
        w_up = jax.random.randint(k_u, (HIDDEN, DIM), -127, 128, dtype=jnp.int32)
        w_down = jax.random.randint(k_d, (DIM, HIDDEN), -127, 128, dtype=jnp.int32)
        return {'x': x, 'w_gate': w_gate, 'w_up': w_up, 'w_down': w_down}
    _L0_ffn_all = _L0_ffn_setup()
    _L0_ffn_in = {k: v for k, v in _L0_ffn_all.items() if k in ('w_gate', 'w_up', 'w_down')}
    del _L0_ffn_all
    return {'x': x, 'ctx_1024': ctx_1024, 'mask_BxSxS2_bk1': mask_BxSxS2_bk1, 'L0_attn_Wq': _L0_attn_in['Wq'], 'L0_attn_bq': _L0_attn_in['bq'], 'L0_attn_Wk': _L0_attn_in['Wk'], 'L0_attn_bk': _L0_attn_in['bk'], 'L0_attn_Wv': _L0_attn_in['Wv'], 'L0_attn_bv': _L0_attn_in['bv'], 'L0_attn_Wo': _L0_attn_in['Wo'], 'L0_attn_bo': _L0_attn_in['bo'], 'L0_attn_W_cross': _L0_attn_in['W_cross'], 'L0_attn_shift_weights': _L0_attn_in['shift_weights'], 'L0_attn_gate': _L0_attn_in['gate'], 'L0_xattn_Wq': _L0_xattn_in['Wq'], 'L0_xattn_Wk': _L0_xattn_in['Wk'], 'L0_xattn_Wv': _L0_xattn_in['Wv'], 'L0_xattn_Wo': _L0_xattn_in['Wo'], 'L0_ffn_w_gate': _L0_ffn_in['w_gate'], 'L0_ffn_w_up': _L0_ffn_in['w_up'], 'L0_ffn_w_down': _L0_ffn_in['w_down']}

def reference(x, ctx_1024, mask_BxSxS2_bk1, L0_attn_Wq, L0_attn_bq, L0_attn_Wk, L0_attn_bk, L0_attn_Wv, L0_attn_bv, L0_attn_Wo, L0_attn_bo, L0_attn_W_cross, L0_attn_shift_weights, L0_attn_gate, L0_xattn_Wq, L0_xattn_Wk, L0_xattn_Wv, L0_xattn_Wo, L0_ffn_w_gate, L0_ffn_w_up, L0_ffn_w_down):
    import jax
    import jax.numpy as jnp

    def _L0_attn_ref(x, Wq, bq, Wk, bk, Wv, bv, Wo, bo, W_cross, shift_weights, gate):
        import jax, jax.numpy as jnp
        import numpy as np
        D_MODEL = 256
        N_HEADS = 16
        HEAD_DIM = D_MODEL // N_HEADS
        MAX_SHIFT = HEAD_DIM // 2
        BATCH, SEQ = (2, 512)

        def _forward(x, Wq, bq, Wk, bk, Wv, bv, Wo, bo, W_cross, shift_weights, gate):
            b, s, _ = x.shape
            H, hd = (W_cross.shape[0], W_cross.shape[1])
            ms = shift_weights.shape[1]
            Q = (x @ Wq.T + bq).reshape(b, s, H, hd)
            K = (x @ Wk.T + bk).reshape(b, s, H, hd)
            V = (x @ Wv.T + bv).reshape(b, s, H, hd)
            Qt = jnp.einsum('bqhf,hfg->bqhg', Q, W_cross)
            scores_cross = jnp.einsum('bqhd,bkhd->bhqk', Qt, K)
            f = jnp.arange(hd)[:, None]
            g = jnp.arange(hd)[None, :]
            tau = g - f
            valid = (tau >= 0) & (tau < ms)
            M = jnp.where(valid[None], shift_weights[:, jnp.clip(tau, 0, ms - 1)], 0.0)
            K_mixed = jnp.einsum('hfg,bkhg->bkhf', M, K)
            scores_conv = jnp.einsum('bqhf,bkhf->bhqk', Q, K_mixed)
            gt = jax.nn.sigmoid(gate).reshape(1, H, 1, 1)
            scale = hd ** (-0.5)
            scores = (gt * scores_cross + (1.0 - gt) * scores_conv) * scale
            causal = jnp.tril(jnp.ones((s, s), dtype=bool))
            scores = jnp.where(causal[None, None], scores, -jnp.inf)
            attn = jax.nn.softmax(scores, axis=-1)
            out = jnp.einsum('bhqk,bkhd->bqhd', attn, V).reshape(b, s, H * hd)
            return out @ Wo.T + bo
        return _forward(x, Wq, bq, Wk, bk, Wv, bv, Wo, bo, W_cross, shift_weights, gate)

    def _L0_xattn_ref(query, key, value, masked, Wq, Wk, Wv, Wo):
        import jax, jax.numpy as jnp
        import numpy as np
        EMBED_DIM = 256
        HEAD = 16
        DK = EMBED_DIM // HEAD
        B, S = (2, 512)
        NEG = -1000000000.0

        def split_heads(x):
            b, s, _ = x.shape
            return x.reshape(b, s, HEAD, DK).transpose(0, 2, 1, 3)
        q = split_heads(query @ Wq)
        k = split_heads(key @ Wk)
        v = split_heads(value @ Wv)
        scale = 1.0 / jnp.sqrt(jnp.asarray(DK, q.dtype))
        scores = jnp.einsum('bhqd,bhkd->bhqk', q, k) * scale
        scores = jnp.where(masked[:, None, :, :], NEG, scores)
        attn = jax.nn.softmax(scores, axis=-1)
        out = jnp.einsum('bhqk,bhkd->bhqd', attn, v)
        out = out.transpose(0, 2, 1, 3).reshape(query.shape[0], -1, EMBED_DIM)
        return out @ Wo

    def _L0_ffn_ref(x, w_gate, w_up, w_down):
        import jax, jax.numpy as jnp
        import numpy as np
        DIM = 256
        HIDDEN = 768
        SCALE = 1.0 / 127.0

        def _dequant(w_int, dtype):
            return w_int.astype(dtype) * jnp.asarray(SCALE, dtype)
        wg = _dequant(w_gate, x.dtype)
        wu = _dequant(w_up, x.dtype)
        wd = _dequant(w_down, x.dtype)
        gate = jnp.einsum('bsd,hd->bsh', x, wg)
        up = jnp.einsum('bsd,hd->bsh', x, wu)
        h = jax.nn.silu(gate) * up
        return jnp.einsum('bsh,dh->bsd', h, wd)
    x = x + _L0_attn_ref(_layernorm(x, axis=-1), L0_attn_Wq, L0_attn_bq, L0_attn_Wk, L0_attn_bk, L0_attn_Wv, L0_attn_bv, L0_attn_Wo, L0_attn_bo, L0_attn_W_cross, L0_attn_shift_weights, L0_attn_gate)
    x = x + _L0_xattn_ref(_layernorm(x, axis=-1), ctx_1024, ctx_1024, mask_BxSxS2_bk1, L0_xattn_Wq, L0_xattn_Wk, L0_xattn_Wv, L0_xattn_Wo)
    x = x + _L0_ffn_ref(_layernorm(x, axis=-1), L0_ffn_w_gate, L0_ffn_w_up, L0_ffn_w_down)
    return x

_drawn_inputs = setup_inputs


def setup_inputs(seed=0):
    import zlib

    import numpy as np

    out = dict(_drawn_inputs(seed))
    spreads = {'L0_attn_bq': (0.0, 0.8),
     'L0_attn_bk': (0.0, 0.8),
     'L0_attn_bv': (0.0, 0.1),
     'L0_attn_bo': (0.0, 0.1),
     'L0_attn_gate': (0.0, 0.8)}
    factors = {'L0_attn_Wq': 8.0,
     'L0_attn_Wk': 8.0,
     'L0_attn_Wv': 4.687,
     'L0_attn_W_cross': 8.0,
     'L0_attn_shift_weights': 8.0}
    for name, (base, spread) in spreads.items():
        noise = np.random.default_rng([zlib.crc32(name.encode()), seed]).standard_normal(out[name].shape)
        drawn = base * np.exp(spread * noise) if base else spread * noise
        out[name] = jnp.asarray(drawn.astype(out[name].dtype))
    for name, factor in factors.items():
        out[name] = (out[name] * factor).astype(out[name].dtype)
    return out
```

```python
from contextlib import ExitStack

import concourse.bass as bass
from concourse import mybir

F32 = mybir.dt.float32
BF16 = mybir.dt.bfloat16
I32 = mybir.dt.int32
U8 = mybir.dt.uint8
ALU = mybir.AluOpType
ACT = mybir.ActivationFunctionType
AX = mybir.AxisListType.X

P = 128
NEG = -1.0e30
EPS = 1e-5
HG = 4
Q_PARTS = (0, 0, 1, 1, 0, 2)
K_PARTS = (0, 1, 0, 1, 2, 0)
MX_BANKS, ST_BANKS, PV_BANKS = (0, 1, 2), (3, 4, 5), (6, 7)


def program(nc, x, ctxt, mask, Wq, bq, Wk, bk, Wv, bv, Wo, bo, W_cross, shift_w, gate,
            xWq, xWk, xWv, xWo, w_gate, w_up, w_down, out):
    B, S, D = x.shape
    S2 = ctxt.shape[1]
    H, HD = W_cross.shape[0], W_cross.shape[1]
    MS = shift_w.shape[1]
    HID = w_gate.shape[0]
    KT = D // P
    HT = HID // P
    CH = 512
    J = CH // P
    G = B * H // HG
    GB = H // HG
    HP = P // HD
    SK = 96
    R = len(Q_PARTS) * HD
    RM = R + 2
    VW = 2 * HD
    SCALE = float(HD) ** -0.5
    WSCALE = 1.0 / 127.0
    NCH = B * S // CH
    assert (D, HD, S, S2 <= SK, HG * VW, NCH) == (256, 16, 1024, True, P, 2 * B)

    def dram(name, shape, dt):
        return nc.dram_tensor(name, shape, dt, kind="Internal").ap()

    qk3 = dram("qk3", (2, 3, G, HG * HD, S), BF16)
    vs = dram("vs", (G, S, HG * VW), F32)
    od = dram("od", (G, HG, 2, HD, S), F32)
    x1s = dram("x1s", (NCH, P, J, D), F32)
    xqs = dram("xqs", (R, G * HG, S), BF16)
    xk3 = dram("xk3", (3, G * HG, HD, SK), BF16)
    xks = dram("xks", (R, G * HG, SK), BF16)
    xvs = dram("xvs", (G, SK, HG * VW), F32)
    mts = dram("mts", (G, SK, S), BF16)
    rdn = dram("rdn", (G * HG, S), F32)
    rdn2 = dram("rdn2", (G * HG, S), F32)
    od2 = dram("od2", (G, HG, 2, HD, S), F32)

    xv = x.rearrange("b (h j p) d -> (b h) p j d", j=J, p=P)
    ov = out.rearrange("b (h j p) d -> (b h) p j d", j=J, p=P)
    mv = mask.rearrange("b (h j p) k -> (b h) p j k", j=J, p=P)

    root = ExitStack()
    with root:
        scope = [root]

        def sb(name, shape, dt=F32):
            return scope[0].enter_context(nc.sbuf_tensor(name, shape, dt))

        def sem(name):
            return scope[0].enter_context(nc.semaphore(name))

        bank = [root.enter_context(nc.psum_tensor(f"bank{i}", [P, 512], F32)) for i in range(8)]
        s_phase = sem("s_phase")

        def barrier(eng, n):
            eng.drain().then_inc(s_phase, 1)
            eng.wait_ge(s_phase, 5 * n)

        ident = sb("ident", [P, P])
        identb = sb("identb", [P, P], BF16)
        tri_q = sb("tri_q", [P, HG, P], BF16)
        tri_k = sb("tri_k", [P, HG, P], BF16)
        negid = sb("negid", [SK, HG, SK], BF16)
        wq_t = sb("wq_t", [P, KT, D])
        wk_t = sb("wk_t", [P, KT, D])
        wv_t = sb("wv_t", [P, KT, D])
        wo_t = sb("wo_t", [P, KT, D])
        xwq = sb("xwq", [P, KT, D])
        xwo = sb("xwo", [P, KT, D])
        qkb = sb("qkb", [P, 2, KT])
        bv_b = sb("bv_b", [P, H, HD])
        bo_b = sb("bo_b", [P, D])
        wg_t = sb("wg_t", [P, KT, HID])
        wu_t = sb("wu_t", [P, KT, HID])
        wd_t = sb("wd_t", [P, HT, D])
        mhalf = sb("mhalf", [P, J])

        with ExitStack() as st:
            scope[0] = st
            n_q = sb("n_q", [P, KT, D])
            n_k = sb("n_k", [P, KT, D])
            n_v = sb("n_v", [P, KT, D])
            n_o = sb("n_o", [P, KT, D])
            ig = sb("ig", [P, HT, D], I32)
            iu = sb("iu", [P, HT, D], I32)
            idn = sb("idn", [P, KT, HID], I32)
            fg = sb("fg", [P, HT, D])
            fu = sb("fu", [P, HT, D])
            fd = sb("fd", [P, KT, HID])
            xwk = sb("xwk", [P, KT, D])
            xwv = sb("xwv", [P, KT, D])
            bq_c = sb("bq_c", [P, KT])
            wc = sb("wc", [P, KT, HD])
            sw = sb("sw", [P, KT, MS])
            gt = sb("gt", [P, KT])
            ge = sb("ge", [P, KT])
            gs = sb("gs", [P, 2, KT])
            blk = sb("blk", [P, P])
            tau = sb("tau", [P, MS, P])
            mm_ = sb("mm_", [P, KT, P])
            ablk = sb("ablk", [P, KT, P])
            cn = sb("cn", [S2, B, D])
            c_t = sb("c_t", [P, KT, B, S2])
            k3 = sb("k3", [P, KT, 3, B, SK], BF16)
            kr = sb("kr", [P, B, S2])
            vx = sb("vx", [SK, B, H, VW])
            trif = sb("trif", [P, 2, P])

            s_in = sem("w_in")
            s_in2 = sem("w_in2")
            s_g = sem("w_g")
            s_v = sem("w_v")
            s_a = sem("w_a")
            s_ab = sem("w_ab")
            s_f = sem("w_f")
            s_t = sem("w_t")
            s_e = sem("w_e")
            s_k = sem("w_k")
            s_kh = sem("w_kh")
            s_vx = sem("w_vx")
            s_out = sem("w_out")
            s_stk = sem("w_stk")

            def cols(a):
                return a.rearrange("(t p) -> p t", p=P)

            N_IN, N_IN2 = 5 + 2 + 2 * KT + 4, 8
            jobs = []

            def turned(src, dst, nk, no):
                for k in range(nk):
                    for o in range(0, no, 4):
                        n = min(4, no - o)
                        jobs.append(([src[:, o + i, k * P:(k + 1) * P] for i in range(n)],
                                     dst[:, k, o * P:(o + n) * P]))

            turned(n_k, wk_t, KT, KT)
            turned(n_v, wv_t, KT, KT)
            turned(n_o, wo_t, KT, KT)
            n_small = len(jobs)
            turned(fg, wg_t, KT, HT)
            turned(fu, wu_t, KT, HT)
            turned(fd, wd_t, HT, KT)
            NJ = len(jobs)
            N_FOLD = NJ + KT
            N_BIAS = N_FOLD + 1
            N_CTX = N_BIAS + KT
            N_XK = N_CTX + KT
            NB = 8

            block = st.enter_context(nc.Block())

            @block.sync
            def _(sp):
                for dst, src in ((n_q, Wq), (n_k, Wk), (n_v, Wv), (n_o, Wo)):
                    sp.dma_start(dst[:], src.rearrange("(t p) n -> p t n", p=P)).then_inc(s_in, 16)
                sp.dma_start(wc[:], W_cross.rearrange("(t h) f g -> (h f) t g", t=KT)).then_inc(s_in, 16)
                with nc.allow_non_contiguous_dma(reason="biases on partitions, a few hundred words"):
                    sp.dma_start(bq_c[:], cols(bq)).then_inc(s_in, 16)
                    sp.dma_start(qkb[:, 1, :], cols(bk)).then_inc(s_in, 16)
                    for t in range(KT):
                        hs = slice(t * HP, (t + 1) * HP)
                        sp.dma_start(sw[:, t, :], shift_w[hs, None, :].to_broadcast([HP, HD, MS])).then_inc(s_in, 16)
                        sp.dma_start(gt[:, t:t + 1],
                                     gate[hs].rearrange("(h a b) -> h a b", a=1, b=1).to_broadcast([HP, HD, 1])).then_inc(s_in, 16)
                sp.dma_start(bv_b[:], bv.rearrange("(a n) -> a n", a=1).to_broadcast([P, D])).then_inc(s_in, 16)
                sp.dma_start(bo_b[:], bo.rearrange("(a n) -> a n", a=1).to_broadcast([P, D])).then_inc(s_in, 16)
                sp.dma_start(xwq[:], xWq.rearrange("(t p) n -> p t n", p=P)).then_inc(s_in, 16)
                sp.dma_start(xwo[:], xWo.rearrange("(t p) n -> p t n", p=P)).then_inc(s_in, 16)
                for dst, src in ((ig, w_gate), (iu, w_up), (idn, w_down), (xwk, xWk), (xwv, xWv)):
                    sp.dma_start(dst[:], src.rearrange("(t p) n -> p t n", p=P)).then_inc(s_in2, 16)
                sp.dma_start(cn[:], ctxt.rearrange("b s d -> s b d")).then_inc(s_in2, 16)
                sp.wait_ge(s_k, 3 * KT)
                for t in range(KT):
                    for b in range(B):
                        sp.dma_start(
                            xk3[:, b * H + HP * t:b * H + HP * (t + 1)].rearrange("c h r k -> (h r) c k"),
                            k3[:, t, :, b, :]).then_inc(s_out, 16)
                sp.wait_ge(s_vx, 1 + B)
                for b in range(B):
                    sp.dma_start(xvs[b * GB:(b + 1) * GB].rearrange("g k c -> k g c"),
                                 vx[:, b].rearrange("k h c -> k (h c)").rearrange("k (g c) -> k g c", g=GB)).then_inc(s_out, 16)
                sp.wait_ge(s_in, 16 * N_IN)
                sp.wait_ge(s_in2, 16 * 6)
                sp.wait_ge(s_out, 16 * (KT * B + B))
                for slot, part in enumerate(K_PARTS):
                    sp.dma_start(xks[HD * slot:HD * (slot + 1)],
                                 xk3[part].rearrange("h r k -> r h k")).then_inc(s_stk, 16)
                sp.wait_ge(s_stk, 16 * len(K_PARTS))
                barrier(sp, 1)

            @block.gpsimd
            def _(g):
                nc.gpsimd.memset(ident[:], 0.0).then_inc(s_g, 1)
                nc.gpsimd.memset(trif[:], 0.0).then_inc(s_g, 1)
                nc.gpsimd.memset(blk[:], 1.0).then_inc(s_g, 1)
                nc.gpsimd.memset(tau[:], 0.0).then_inc(s_g, 1)
                g.wait_ge(s_g, 4)
                nc.gpsimd.affine_select(out=ident[:], in_=ident[:], compare_op=ALU.not_equal, fill=1.0,
                                        base=0, pattern=[[-1, P]], channel_multiplier=1).then_inc(s_g, 1)
                nc.gpsimd.affine_select(out=blk[:], in_=blk[:], compare_op=ALU.is_ge, fill=0.0,
                                        base=0, pattern=[[-HD, HP], [0, HD]], channel_multiplier=1).then_inc(s_g, 1)
                g.wait_ge(s_g, 6)
                nc.gpsimd.affine_select(out=blk[:], in_=blk[:], compare_op=ALU.is_ge, fill=0.0,
                                        base=HD - 1, pattern=[[HD, HP], [0, HD]], channel_multiplier=-1).then_inc(s_g, 1)
                nc.gpsimd.affine_select(out=tau[:], in_=tau[:], compare_op=ALU.not_equal, fill=1.0,
                                        base=0, pattern=[[-1, MS], [1, P]], channel_multiplier=-1).then_inc(s_g, 1)
                nc.gpsimd.affine_select(out=trif[:, 0, :], in_=trif[:, 0, :], compare_op=ALU.is_ge, fill=NEG,
                                        base=0, pattern=[[-1, P]], channel_multiplier=1).then_inc(s_g, 1)
                nc.gpsimd.affine_select(out=trif[:, 1, :], in_=trif[:, 1, :], compare_op=ALU.is_ge, fill=NEG,
                                        base=0, pattern=[[1, P]], channel_multiplier=-1).then_inc(s_g, 1)
                nc.gpsimd.memset(mhalf[:], -0.5)
                nc.gpsimd.memset(k3[:], 0.0).then_inc(s_g, 1)
                nc.gpsimd.memset(vx[:], 0.0).then_inc(s_g, 1)
                g.wait_ge(s_g, 12)
                nc.gpsimd.memset(vx[:, :, :, HD:VW], 1.0).then_inc(s_g, 1)
                for h in range(HG):
                    nc.gpsimd.tensor_copy(tri_q[:, h, :], trif[:, 0, :])
                    nc.gpsimd.tensor_copy(tri_k[:, h, :], trif[:, 1, :])
                    nc.gpsimd.tensor_scalar(negid[:, h, :], ident[0:SK, 0:SK], NEG, None, ALU.mult)
                nc.gpsimd.tensor_copy(identb[:], ident[:])
                barrier(g, 1)

            @block.vector
            def _(v):
                v.wait_ge(s_in, 16 * N_IN)
                v.wait_ge(s_a, 1)
                nc.vector.tensor_scalar(ge[:], ge[:], 1.0, None, ALU.add).then_inc(s_v, 1)
                v.wait_ge(s_v, 1)
                nc.vector.reciprocal(ge[:], ge[:]).then_inc(s_v, 1)
                v.wait_ge(s_v, 2)
                nc.vector.tensor_scalar(gs[:, 0, :], ge[:], SCALE, None, ALU.mult).then_inc(s_v, 1)
                nc.vector.tensor_scalar(gs[:, 1, :], ge[:], -SCALE, SCALE, ALU.mult, ALU.add).then_inc(s_v, 1)
                v.wait_ge(s_g, 10)
                n = 4
                for t in range(KT):
                    v.wait_ge(s_v, n)
                    nc.vector.tensor_scalar(mm_[:, t, :], tau[:, 0, :], sw[:, t, 0:1], None, ALU.mult).then_inc(s_v, 1)
                    n += 1
                    for s in range(1, MS):
                        v.wait_ge(s_v, n)
                        nc.vector.scalar_tensor_tensor(mm_[:, t, :], tau[:, s, :], sw[:, t, s:s + 1],
                                                       mm_[:, t, :], ALU.mult, ALU.add).then_inc(s_v, 1)
                        n += 1
                    v.wait_ge(s_v, n)
                    nc.vector.tensor_scalar(mm_[:, t, :], mm_[:, t, :], gs[:, 1, t:t + 1], None, ALU.mult).then_inc(s_v, 1)
                    n += 1
                    v.wait_ge(s_v, n)
                    nc.vector.scalar_tensor_tensor(
                        ablk[:, t, :].rearrange("p (h g) -> p h g", h=HP),
                        wc[:, t:t + 1, :].to_broadcast([P, HP, HD]), gs[:, 0, t:t + 1],
                        mm_[:, t, :].rearrange("p (h g) -> p h g", h=HP), ALU.mult, ALU.add).then_inc(s_v, 1)
                    n += 1
                    v.wait_ge(s_v, n)
                    nc.vector.tensor_tensor(ablk[:, t, :], ablk[:, t, :], blk[:], ALU.mult).then_inc(s_ab, 1)
                v.wait_ge(s_in2, 16 * 6)
                for f, i in ((fg, ig), (fu, iu), (fd, idn)):
                    nc.vector.tensor_scalar(f[:], i[:], WSCALE, None, ALU.mult).then_inc(s_f, 1)
                v.wait_ge(s_g, 13)
                for t in range(KT):
                    ps = bank[(N_CTX + t) % NB][:, 0:B * S2].rearrange("p (b s) -> p b s", b=B)
                    v.wait_ge(s_kh, t + 1)
                    if t:
                        v.wait_ge(s_k, 3 * t)
                    nc.vector.tensor_tensor(kr[:], ps, k3[:, t, 0, :, 0:S2], ALU.subtract).then_inc(s_k, 1)
                    v.wait_ge(s_k, 3 * t + 1)
                    nc.vector.tensor_copy(k3[:, t, 1, :, 0:S2], kr[:]).then_inc(s_k, 1)
                    v.wait_ge(s_k, 3 * t + 2)
                    nc.vector.tensor_tensor(k3[:, t, 2, :, 0:S2], kr[:], k3[:, t, 1, :, 0:S2], ALU.subtract).then_inc(s_k, 1)
                barrier(v, 1)

            @block.scalar
            def _(a):
                a.wait_ge(s_in, 16 * N_IN)
                nc.scalar.activation(ge[:], gt[:], ACT.Exp, scale=-1.0).then_inc(s_a, 1)

                def empty(n, dst, src, **kw):
                    a.wait_ge(s_t, n + 1)
                    nc.scalar.activation(dst, src, ACT.Identity, **kw).then_inc(s_e, 1)

                for n, (blocks, dst) in enumerate(jobs):
                    empty(n, dst, bank[n % NB][:, 0:len(blocks) * P])
                for k in range(KT):
                    empty(NJ + k, wq_t[:, k, :], bank[(NJ + k) % NB][:, 0:D])
                empty(N_FOLD, qkb[:, 0, :], bank[N_FOLD % NB][:, 0:KT])
                for k in range(KT):
                    empty(N_BIAS + k, c_t[:, k], bank[(N_BIAS + k) % NB][:, 0:B * S2].rearrange("p (b s) -> p b s", b=B))
                a.wait_ge(s_g, 13)
                for t in range(KT):
                    a.wait_ge(s_t, N_CTX + t + 1)
                    nc.scalar.activation(k3[:, t, 0, :, 0:S2],
                                         bank[(N_CTX + t) % NB][:, 0:B * S2].rearrange("p (b s) -> p b s", b=B),
                                         ACT.Identity).then_inc(s_kh, 1)
                nc.scalar.activation(gt[0:1, 0:1], gt[0:1, 0:1], ACT.Identity).then_inc(s_vx, 1)
                for b in range(B):
                    n = N_XK + b
                    a.wait_ge(s_t, n + 1)
                    nc.scalar.activation(vx[0:S2, b, :, 0:HD],
                                         bank[n % NB][0:S2, 0:D].rearrange("p (h d) -> p h d", h=H),
                                         ACT.Identity).then_inc(s_vx, 1)
                barrier(a, 1)

            @block.tensor
            def _(t_):
                t_.wait_ge(s_in, 16 * N_IN)
                t_.wait_ge(s_g, 5)

                def free(n):
                    if n >= NB:
                        t_.wait_ge(s_e, n - NB + 1)

                for n, (blocks, dst) in enumerate(jobs):
                    free(n)
                    if n >= n_small:
                        t_.wait_ge(s_f, 3)
                    for i, b_ in enumerate(blocks):
                        m = nc.tensor.transpose(bank[n % NB][:, i * P:(i + 1) * P], b_, ident[:])
                    m.then_inc(s_t, 1)
                t_.wait_ge(s_ab, KT)
                for k in range(KT):
                    free(NJ + k)
                    for o in range(KT):
                        m = nc.tensor.matmul(bank[(NJ + k) % NB][:, o * P:(o + 1) * P],
                                             n_q[:, o, k * P:(k + 1) * P], ablk[:, o, :], start=True, stop=True)
                    m.then_inc(s_t, 1)
                free(N_FOLD)
                for o in range(KT):
                    m = nc.tensor.matmul(bank[N_FOLD % NB][:, o:o + 1], ablk[:, o, :], bq_c[:, o:o + 1],
                                         start=True, stop=True)
                m.then_inc(s_t, 1)
                t_.wait_ge(s_in2, 16 * 6)
                for k in range(KT):
                    free(N_BIAS + k)
                    for b in range(B):
                        m = nc.tensor.transpose(bank[(N_BIAS + k) % NB][:, b * S2:(b + 1) * S2],
                                                cn[:, b, k * P:(k + 1) * P], ident[0:S2, 0:S2])
                    m.then_inc(s_t, 1)
                t_.wait_ge(s_e, N_CTX)
                for o in range(KT):
                    for k in range(KT):
                        m = nc.tensor.matmul(bank[(N_CTX + o) % NB][:, 0:B * S2],
                                             xwk[:, k, o * P:(o + 1) * P],
                                             c_t[:, k].rearrange("p b s -> p (b s)"),
                                             start=(k == 0), stop=(k == KT - 1))
                    m.then_inc(s_t, 1)
                for b in range(B):
                    for k in range(KT):
                        m = nc.tensor.matmul(bank[(N_XK + b) % NB][0:S2, 0:D], c_t[:, k, b, :], xwv[:, k, :],
                                             start=(k == 0), stop=(k == KT - 1))
                    m.then_inc(s_t, 1)
                barrier(t_, 1)

        def again(b):
            return not (isinstance(b, int) and b == B - 1)

        def sweep(eng, chunk):
            with eng.Fori(0, B - 1) as b:
                chunk(b, 0, True)
                chunk(b, 1, True)
            chunk(B - 1, 0, True)
            chunk(B - 1, 1, False)

        def moments(v, s_sum, c, src, stat, mom, ve):
            for j in range(J):
                nc.vector.bn_stats(stat[:, j], src[:, j]).then_inc(s_sum, 1)
            v.wait_ge(s_sum, NSUM * c + J)
            even, odd = stat[:, :, 1], stat[:, :, 4]
            nc.vector.tensor_tensor(mom[:, 1], even, odd, ALU.add).then_inc(s_sum, 1)
            nc.vector.tensor_tensor(mom[:, 2], even, odd, ALU.subtract).then_inc(s_sum, 1)
            nc.vector.tensor_tensor(mom[:, 3], stat[:, :, 2], stat[:, :, 5], ALU.add).then_inc(s_sum, 1)
            v.wait_ge(s_sum, NSUM * c + J + 3)
            nc.vector.tensor_scalar(mom[:, 0], mom[:, 1], 0.5, None, ALU.mult).then_inc(s_sum, 1)
            nc.vector.scalar_tensor_tensor(mom[:, 4], mom[:, 2], 0.25, mom[:, 2], ALU.mult, ALU.mult).then_inc(s_sum, 1)
            nc.vector.tensor_scalar(mom[:, 5], mom[:, 3], 1.0 / D, EPS, ALU.mult, ALU.add).then_inc(s_sum, 1)
            v.wait_ge(s_sum, NSUM * c + J + 6)
            nc.vector.tensor_tensor(ve, mom[:, 4], mom[:, 5], ALU.add).then_inc(s_sum, 1)

        NSUM = J + 7

        with ExitStack() as st:
            scope[0] = st
            xin = sb("a_xin", [P, 2, J, D])
            stat = sb("a_stat", [P, 2, J, 6])
            mom = sb("a_mom", [P, 2, 6, J])
            ve = sb("a_ve", [P, 2, J])
            rstd = sb("a_rstd", [P, 2, J])
            xn = sb("a_xn", [P, 2, J, D])
            xnt = sb("a_xnt", [P, 2, KT, CH])
            parts = sb("a_parts", [P, 2, 4, 3, CH], BF16)
            rest = sb("a_rest", [P, 4, CH])
            vst = sb("a_vst", [P, 2, J, H, VW])

            ld = [sem(f"a_ld{u}") for u in range(2)]
            s_sum = sem("a_sum")
            s_pow = sem("a_pow")
            s_xn = sem("a_xn_")
            s_tr = sem("a_tr")
            s_xt = sem("a_xt")
            s_qk = sem("a_qk")
            s_hi = sem("a_hi")
            s_r = sem("a_r")
            s_m = sem("a_m")
            s_lo = sem("a_lo")
            so = [sem(f"a_so{u}") for u in range(2)]
            s_vm = sem("a_vm")
            s_ve = sem("a_ve_")
            vo = [sem(f"a_vo{u}") for u in range(2)]
            s_one = sem("a_one")
            QKB, VB = (2, 3, 4, 5), (6, 7)

            block = st.enter_context(nc.Block())

            @block.sync
            def _(sp):
                sp.sem_inc(s_xn, 2 * J)
                sp.sem_inc(s_tr, 4)
                sp.sem_inc(s_xt, 2)
                sp.sem_inc(s_r, 4)
                sp.sem_inc(s_lo, 4)
                sp.sem_inc(s_vm, 4)
                sp.sem_inc(s_ve, 2)
                for u in range(2):
                    sp.sem_inc(so[u], 64)
                    sp.sem_inc(vo[u], 64)
                for u in range(2):
                    sp.dma_start(xin[:, u], xv[u]).then_inc(ld[u], 16)

                def chunk(b, u, more, load):
                    c = 2 * b + u
                    for n in range(4):
                        sp.wait_ge(s_lo, 4 + 4 * c + n + 1)
                        sp.dma_start(
                            qk3[n // 2, :, bass.ds(b * GB + 2 * (n % 2), 2), :, u * CH:(u + 1) * CH]
                            .rearrange("c g r t -> (g r) c t"),
                            parts[:, u, n]).then_inc(so[u], 16)
                    sp.wait_ge(s_ve, 2 + 2 * c + 2)
                    for j in range(J):
                        sp.dma_start(
                            vs[bass.ds(b * GB, GB), (u * J + j) * P:(u * J + j + 1) * P, :].rearrange("g p c -> p g c"),
                            vst[:, u, j].rearrange("p h c -> p (h c)").rearrange("p (g c) -> p g c", g=GB)).then_inc(vo[u], 16)
                    if load:
                        sp.wait_ge(s_xn, 2 * J + J * c + J)
                        sp.dma_start(xin[:, u], xv[bass.ds(c + 2, 1)].rearrange("a p j d -> (a p) j d")).then_inc(ld[u], 16)

                with sp.Fori(0, B - 1) as b:
                    chunk(b, 0, True, True)
                    chunk(b, 1, True, True)
                chunk(B - 1, 0, True, False)
                chunk(B - 1, 1, False, False)
                for u in range(2):
                    sp.wait_ge(so[u], 64 * (B + 1))
                    sp.wait_ge(vo[u], 64 * (B + 1))
                barrier(sp, 2)

            @block.vector
            def _(v):
                nc.vector.memset(vst[:].rearrange("p u j h c -> p (u j h) c")[:, :, HD:VW], 1.0)

                def stats(b, u):
                    c = 2 * b + u
                    v.wait_ge(ld[u], 16 * (b + 1))
                    moments(v, s_sum, c, xin[:, u], stat[:, u], mom[:, u], ve[:, u])

                def normalise(b, u):
                    c = 2 * b + u
                    v.wait_ge(s_pow, c + 1)
                    v.wait_ge(s_tr, 2 * c + 2)
                    for j in range(J):
                        nc.vector.tensor_scalar(xn[:, u, j], xin[:, u, j], mom[:, u, 0, j:j + 1], rstd[:, u, j:j + 1],
                                                ALU.subtract, ALU.mult).then_inc(s_xn, 1)

                def split(b, u, n):
                    c = 2 * b + u
                    v.wait_ge(s_hi, 4 * c + n + 1)
                    v.wait_ge(s_lo, 4 * c + n + 1)
                    nc.vector.scalar_tensor_tensor(rest[:, n], bank[QKB[n]][:], qkb[:, n // 2, n % 2:n % 2 + 1],
                                                   parts[:, u, n, 0], ALU.add, ALU.subtract).then_inc(s_r, 1)
                    v.wait_ge(s_r, 4 + 4 * c + n + 1)
                    nc.vector.tensor_copy(parts[:, u, n, 1], rest[:, n]).then_inc(s_m, 1)

                def chunk(b, u, more):
                    c = 2 * b + u
                    nb, nu = b + u, 1 - u
                    split(b, u, 0)
                    split(b, u, 1)
                    if more:
                        stats(nb, nu)
                    split(b, u, 2)
                    split(b, u, 3)
                    if more:
                        normalise(nb, nu)
                    v.wait_ge(vo[u], 64 * (b + 1))
                    for w in range(2):
                        v.wait_ge(s_vm, 4 + 2 * c + w + 1)
                        for i in range(2):
                            m = nc.vector.tensor_tensor(
                                vst[:, u, 2 * w + i, :, 0:HD],
                                bank[VB[w]][:, i * D:(i + 1) * D].rearrange("p (h d) -> p h d", h=H),
                                bv_b[:], ALU.add)
                        m.then_inc(s_ve, 1)

                stats(0, 0)
                normalise(0, 0)
                sweep(v, chunk)
                barrier(v, 2)

            @block.gpsimd
            def _(g):
                def power(b, u):
                    c = 2 * b + u
                    g.wait_ge(s_sum, NSUM * (c + 1))
                    g.wait_ge(s_xn, J * c + J)
                    nc.gpsimd.tensor_tensor(rstd[:, u], ve[:, u], mhalf[:], ALU.pow).then_inc(s_pow, 1)

                def low(b, u, n):
                    c = 2 * b + u
                    g.wait_ge(s_m, 4 * c + n + 1)
                    nc.gpsimd.tensor_tensor(parts[:, u, n, 2], rest[:, n], parts[:, u, n, 1],
                                            ALU.subtract).then_inc(s_lo, 1)

                def chunk(b, u, more):
                    low(b, u, 0)
                    low(b, u, 1)
                    if more:
                        power(b + u, 1 - u)
                    low(b, u, 2)
                    low(b, u, 3)

                power(0, 0)
                sweep(g, chunk)
                barrier(g, 2)

            @block.scalar
            def _(a):
                def turned(b, u):
                    c = 2 * b + u
                    a.wait_ge(s_vm, 2 * c + 2)
                    for k in range(KT):
                        a.wait_ge(s_tr, 4 + 2 * c + k + 1)
                        nc.scalar.activation(xnt[:, u, k], bank[k][:], ACT.Identity).then_inc(s_xt, 1)

                def chunk(b, u, more):
                    c = 2 * b + u
                    a.wait_ge(so[u], 64 * (b + 1))
                    for n in range(4):
                        a.wait_ge(s_qk, 4 * c + n + 1)
                        nc.scalar.activation(parts[:, u, n, 0], bank[QKB[n]][:], ACT.Identity,
                                             bias=qkb[:, n // 2, n % 2:n % 2 + 1]).then_inc(s_hi, 1)
                    if more:
                        turned(b + u, 1 - u)

                turned(0, 0)
                sweep(a, chunk)
                barrier(a, 2)

            @block.tensor
            def _(t):
                def turn(b, u):
                    c = 2 * b + u
                    t.wait_ge(s_xn, 2 * J + J * c + J)
                    for k in range(KT):
                        t.wait_ge(s_xt, 2 * c + k + 1)
                        for j in range(J):
                            m = nc.tensor.transpose(bank[k][:, j * P:(j + 1) * P],
                                                    xn[:, u, j, k * P:(k + 1) * P], ident[:])
                        m.then_inc(s_tr, 1)

                def values(b, u, w):
                    c = 2 * b + u
                    t.wait_ge(s_ve, 2 * c + w + 1)
                    for i in range(2):
                        for k in range(KT):
                            m = nc.tensor.matmul(bank[VB[w]][:, i * D:(i + 1) * D],
                                                 xnt[:, u, k, (2 * w + i) * P:(2 * w + i + 1) * P], wv_t[:, k, :],
                                                 start=(k == 0), stop=(k == KT - 1))
                    m.then_inc(s_vm, 1)

                def chunk(b, u, more):
                    c = 2 * b + u
                    t.wait_ge(s_xt, 2 + 2 * c + 2)
                    for n in range(4):
                        t.wait_ge(s_r, 4 * c + n + 1)
                        w_ = (wq_t, wk_t)[n // 2]
                        for k in range(KT):
                            m = nc.tensor.matmul(bank[QKB[n]][:], w_[:, k, (n % 2) * P:(n % 2 + 1) * P],
                                                 xnt[:, u, k], start=(k == 0), stop=(k == KT - 1))
                        m.then_inc(s_qk, 1)
                    values(b, u, 0)
                    if more:
                        turn(b + u, 1 - u)
                    values(b, u, 1)

                turn(0, 0)
                sweep(t, chunk)
                barrier(t, 2)

        def attention(stage, name, causal, ahead, load_qk, n_qk, v_src, m_src, o_dst):
            KW = S if causal else SK
            KP = P if causal else SK
            NKT = S // P if causal else 1
            NPS = 12
            mx_units = []
            for half in range(2):
                for r in range(4):
                    if not causal:
                        mx_units.append((half, half, r, 0, HG, 0, KW, False))
                        continue
                    if half:
                        mx_units += [(half, 1, r, h, 1, 0, 512, False) for h in range(HG)]
                    hb = HG // (r + 1)
                    mx_units += [(half, 2 * half, r, h, hb, half * 512, (r + 1) * P, True)
                                 for h in range(0, HG, hb)]
            n_half = sum(1 for m in mx_units if m[0] == 0)
            st_units, sets = [], []
            for half in range(2):
                kts = range(4 * half + 4) if causal else range(1)
                for kt in kts:
                    diag = causal and kt >= 4 * half
                    q0 = (kt % 4) * P if diag else 0
                    n = 512 - q0
                    hb = max(1, (512 // n) // 2 * 2)
                    first = len(st_units)
                    st_units += [(half, kt, h, hb, q0, n, diag) for h in range(0, HG, hb)]
                    sets.append((half, kt, first, len(st_units), kt == kts[0], kt == kts[-1], q0, n, hb))
            NST = len(st_units)
            half_end = [max(s[3] for s in sets if s[0] == h) for h in range(2)]
            ring = [("m", i) for i in range(len(mx_units))]
            ring.insert(min(n_half + 6, len(ring)), ("t", 0))
            ring.append(("t", 1))
            NMX = len(ring)
            NC = 3 if causal else 2
            LAG = 3
            LATE = 2 if causal else 0

            def reused(u, count, slots):
                last = max(w for w in range(count) if w % slots == u % slots) if u < slots else None
                return slots - count + last + 1 if u < slots else u + 1

            plan, at = [], 0
            for u in range(NST):
                plan.append(("s", u))
                plan += [("p", s) for s, x in enumerate(sets) if x[3] - 1 == u - LAG]
                if u == LATE:
                    plan.append(("r", NMX - 1, ahead - 1))
                upto = max(0, u - LATE + 1) * (NMX - 1) // (NST - LATE)
                plan += [("r", n, ahead) for n in range(at, upto)]
                at = upto
            plan += [("p", s) for s, x in enumerate(sets) if x[3] - 1 > NST - 1 - LAG]
            with ExitStack() as st:
                scope[0] = st
                stq = sb(name + "stq", [P, GB, 2, HG, 512], BF16)
                stk = sb(name + "stk", [P, GB, HG, KW], BF16)
                va = sb(name + "va", [KP, GB, NKT, HG * VW])
                prob = sb(name + "prob", [KP, NPS, 512])
                u_ = sb(name + "u", [P, 2, S])
                pm = sb(name + "pm", [P, 3, HG, 4])
                mxv = sb(name + "mxv", [P, HG * 4])
                mt = sb(name + "mt", [P, 2, 2, HG * 4], BF16)
                mrow = sb(name + "mrow", [2 * HG * 4, 2, 2, P], BF16)
                mk = None if causal else sb(name + "mk", [SK, GB, S], BF16)

                ld = [sem(f"{name}ld{i}") for i in range(GB)]
                s_set = sem(name + "s_set")
                s_mxf = sem(name + "s_mxf")
                s_mxe = sem(name + "s_mxe")
                s_cmb = sem(name + "s_cmb")
                s_mt = sem(name + "s_mt")
                md = [[sem(f"{name}md{i}{c}") for c in range(2)] for i in range(2)]
                s_st = sem(name + "s_st")
                s_ex = sem(name + "s_ex")
                s_pv = sem(name + "s_pv")
                s_u = sem(name + "s_u")
                us = [sem(f"{name}us{i}") for i in range(2)]
                NLD = n_qk + 1 + (0 if causal else 1)

                block = st.enter_context(nc.Block())

                def steps(eng, step):
                    with eng.Fori(0, B - 1) as b:
                        for i in range(GB):
                            step(b, i, GB)
                    for i in range(GB):
                        step(B - 1, i, GB - 1 - i)

                def after(b, i, n):
                    return b + (i + n) // GB, (i + n) % GB

                @block.sync
                def _(sp):
                    sp.sem_inc(s_mxe, 3)
                    sp.sem_inc(s_ex, 3)
                    sp.sem_inc(s_pv, NPS)
                    sp.sem_inc(s_u, 2)
                    for i in range(2):
                        sp.sem_inc(us[i], 16)

                    def load(b, i):
                        g = b * GB + i
                        load_qk(sp, g, stq[:, i], stk[:, i], ld[i])
                        sp.dma_start(va[:, i], v_src[bass.ds(g, 1)].rearrange("a (n p) c -> (a p) n c", p=KP)).then_inc(ld[i], 16)
                        if m_src is not None:
                            sp.dma_start(mk[:, i], m_src[bass.ds(g, 1)].rearrange("a k t -> (a k) t")).then_inc(ld[i], 16)

                    def maxima(b, i, c):
                        sp.wait_ge(s_mxe, 3 + (b * GB + i) * NMX + ring.index(("t", c)) + 1)
                        for t in range(2):
                            sp.dma_start(stq[R + t:R + t + 1, i, c].rearrange("a h q -> a (h q)"),
                                         mrow[16 * t:16 * (t + 1), i % 2, c]).then_inc(md[i % 2][c], 16)

                    for i in range(GB - 1):
                        load(0, i)
                    for i in range(ahead):
                        maxima(0, i, 0)
                        if i < ahead - 1:
                            maxima(0, i, 1)

                    def step(b, i, left):
                        g = b * GB + i
                        if left >= ahead - 1:
                            maxima(*after(b, i, ahead - 1), 1)
                        if left >= GB - 1:
                            sp.wait_ge(s_pv, NPS + g * NST)
                            load(*after(b, i, GB - 1))
                        if left >= ahead:
                            maxima(*after(b, i, ahead), 0)
                        sp.wait_ge(s_u, 2 + 2 * g + 2)
                        sp.dma_start(o_dst[bass.ds(g, 1)].rearrange("a h w r t -> (a h w r) t"),
                                     u_[:, i % 2]).then_inc(us[i % 2], 16)

                    steps(sp, step)
                    for i in range(2):
                        sp.wait_ge(us[i], 16 * (G // 2 + 1))
                    barrier(sp, stage)

                @block.gpsimd
                def _(g):
                    barrier(g, stage)

                @block.vector
                def _(v):
                    nc.vector.memset(stk[R:RM], -1.0).then_inc(s_set, 1)

                    def item(b, i, n):
                        g = b * GB + i
                        kind, m = ring[n]
                        src = bank[MX_BANKS[n % 3]]
                        v.wait_ge(s_mxf, g * NMX + n + 1)
                        if kind == "t":
                            nc.vector.tensor_copy(mrow[:, i % 2, m], src[0:32, 0:P // 2].bitcast(BF16)).then_inc(s_mxe, 1)
                            return
                        half, k, r, h0, hb, _, w, _ = mx_units[m]
                        nc.vector.tensor_reduce(pm[:, k, h0:h0 + hb, r],
                                                src[:, 0:hb * w].rearrange("p (h w) -> p h w", h=hb),
                                                AX, ALU.max).then_inc(s_mxe, 1)
                        if m == n_half - 1 or m == len(mx_units) - 1:
                            parts_of_max(g, half, n)

                    def parts_of_max(g, c, n):
                        v.wait_ge(s_mxe, 3 + g * NMX + n + 1)
                        m = pm[:, c].rearrange("p h r -> p (h r)")
                        if causal and c:
                            nc.vector.tensor_tensor(mxv[:], m, pm[:, 2].rearrange("p h r -> p (h r)"),
                                                    ALU.max).then_inc(s_cmb, 1)
                            v.wait_ge(s_cmb, NC * g + 2)
                            m = mxv[:]
                        nc.vector.tensor_copy(mt[:, c, 0], m).then_inc(s_cmb, 1)
                        v.wait_ge(s_cmb, NC * g + (NC if c else 1))
                        nc.vector.tensor_tensor(mt[:, c, 1], m, mt[:, c, 0], ALU.subtract).then_inc(s_mt, 1)

                    def step(b, i, left):
                        if left >= ahead - 1:
                            item(*after(b, i, ahead - 1), NMX - 1)
                        if left >= ahead:
                            for n in range(NMX - 1):
                                item(*after(b, i, ahead), n)

                    for n in range(ahead * NMX - 1):
                        item(0, n // NMX, n % NMX)
                    steps(v, step)
                    barrier(v, stage)

                @block.scalar
                def _(a):
                    def outputs(b, i, c):
                        g = b * GB + i
                        if c == 0:
                            a.wait_ge(us[i % 2], 16 * (2 * b + i // 2 + 1))
                        a.wait_ge(s_pv, NPS + g * NST + half_end[c])
                        nc.scalar.activation(u_[:, i % 2, c * 512:(c + 1) * 512], bank[PV_BANKS[c]][:],
                                             ACT.Identity).then_inc(s_u, 1)

                    def step(b, i, left):
                        g = b * GB + i
                        for u, (half, kt, h0, hb, q0, n, diag) in enumerate(st_units):
                            a.wait_ge(s_st, g * NST + u + 1)
                            a.wait_ge(s_pv, g * NST + reused(u, NST, NPS))
                            nc.scalar.activation(prob[:, u % NPS, 0:hb * n], bank[ST_BANKS[u % 3]][0:KP, 0:hb * n],
                                                 ACT.Exp).then_inc(s_ex, 1)
                            if u == min(half_end[0] + LAG + 2, NST - 2):
                                outputs(b, i, 0)
                        outputs(b, i, 1)

                    steps(a, step)
                    barrier(a, stage)

                @block.tensor
                def _(t):
                    def item(b, i, n):
                        g = b * GB + i
                        kind, m = ring[n]
                        dst = bank[MX_BANKS[n % 3]]
                        if n == 0:
                            t.wait_ge(ld[i], 16 * NLD * (b + 1))
                        t.wait_ge(s_mxe, g * NMX + reused(n, NMX, 3))
                        if kind == "t":
                            t.wait_ge(s_mt, 2 * g + m + 1)
                            nc.tensor.transpose(dst[0:32, 0:P // 2].bitcast(BF16),
                                                mt[:, m].rearrange("p t m -> p (t m)"), identb[:]).then_inc(s_mxf, 1)
                            return
                        half, k, r, h0, hb, k0, w, diag = mx_units[m]
                        qt = 4 * half + r
                        for h in range(hb):
                            mm = nc.tensor.matmul(dst[:, h * w:(h + 1) * w],
                                                  stq[0:R, i, half, h0 + h, r * P:(r + 1) * P],
                                                  stk[0:R, i, h0 + h, k0:k0 + w],
                                                  start=(h == 0), stop=(causal and not diag), skip_group_check=True)
                        if not causal:
                            mm = nc.tensor.matmul(dst[:, 0:hb * w], mk[:, i, qt * P:(qt + 1) * P],
                                                  negid[:].rearrange("k h l -> k (h l)"),
                                                  start=False, stop=True, skip_group_check=True)
                        elif diag:
                            mm = nc.tensor.matmul(dst[:, 0:hb * w].rearrange("p (h w) -> p h w", h=hb)[:, :, w - P:w],
                                                  identb[:], tri_q[:, 0:hb], start=False, stop=True,
                                                  skip_group_check=True)
                        mm.then_inc(s_mxf, 1)

                    def scores(b, i, u):
                        g = b * GB + i
                        half, kt, h0, hb, q0, n, diag = st_units[u]
                        if u == 0 or u == half_end[0]:
                            t.wait_ge(md[i % 2][half], 32 * (2 * b + i // 2 + 1))
                        t.wait_ge(s_ex, g * NST + reused(u, NST, 3))
                        dst = bank[ST_BANKS[u % 3]]
                        q = half * 512 + q0
                        for h in range(hb):
                            mm = nc.tensor.matmul(dst[0:KP, h * n:(h + 1) * n],
                                                  stk[0:RM, i, h0 + h, kt * KP:(kt + 1) * KP],
                                                  stq[0:RM, i, half, h0 + h, q0:q0 + n],
                                                  start=(h == 0), stop=(causal and not diag), skip_group_check=True)
                        if not causal:
                            mm = nc.tensor.matmul(dst[0:KP, 0:n], negid[:, 0], mk[:, i, q:q + n],
                                                  start=False, stop=True, skip_group_check=True)
                        elif diag:
                            mm = nc.tensor.matmul(dst[:, 0:hb * n].rearrange("p (h n) -> p h n", h=hb)[:, :, 0:P],
                                                  identb[:], tri_k[:, 0:hb], start=False, stop=True,
                                                  skip_group_check=True)
                        mm.then_inc(s_st, 1)

                    def products(b, i, s):
                        g = b * GB + i
                        half, kt, first, end, fresh, last, q0, n, hb = sets[s]
                        if fresh:
                            t.wait_ge(s_u, 2 * g + half + 1)
                        t.wait_ge(s_ex, 3 + g * NST + end)
                        for h in range(HG):
                            mm = nc.tensor.matmul(bank[PV_BANKS[half]][h * VW:(h + 1) * VW, q0:512],
                                                  va[:, i, kt, h * VW:(h + 1) * VW],
                                                  prob[:, (first + h // hb) % NPS, (h % hb) * n:(h % hb + 1) * n],
                                                  start=fresh, stop=last)
                            if h % hb == hb - 1:
                                mm.then_inc(s_pv, 1)

                    def step(b, i, left):
                        for what in plan:
                            if what[0] == "s":
                                scores(b, i, what[1])
                            elif what[0] == "p":
                                products(b, i, what[1])
                            elif left >= what[2]:
                                item(*after(b, i, what[2]), what[1])

                    t.wait_ge(s_set, 1)
                    for n in range(ahead * NMX - 1):
                        item(0, n // NMX, n % NMX)
                    steps(t, step)
                    barrier(t, stage)

        def load_self(sp, g, stq, stk, ld):
            for slot, part in enumerate(Q_PARTS):
                for c in range(2):
                    sp.dma_start(stq[HD * slot:HD * (slot + 1), c],
                                 qk3[0, part, bass.ds(g, 1), :, c * 512:(c + 1) * 512]
                                 .rearrange("a (h r) t -> (a r) h t", h=HG)).then_inc(ld, 16)
            for slot, part in enumerate(K_PARTS):
                sp.dma_start(stk[HD * slot:HD * (slot + 1)],
                             qk3[1, part, bass.ds(g, 1)].rearrange("a (h r) t -> (a r) h t", h=HG)).then_inc(ld, 16)

        def load_cross(sp, g, stq, stk, ld):
            for c in range(2):
                sp.dma_start(stq[0:R, c], xqs[:, bass.ds(g * HG, HG), c * 512:(c + 1) * 512]).then_inc(ld, 16)
            sp.dma_start(stk[0:R], xks[:, bass.ds(g * HG, HG)]).then_inc(ld, 16)

        attention(3, "self_", True, 1, load_self, 2 * len(Q_PARTS) + len(K_PARTS), vs, None, od)

        def chunk_loads(sp, o_src, r_src, b, u, oin, din, ld):
            for k in range(KT):
                sp.dma_start(oin[:, u, k], o_src[bass.ds(b * GB + 2 * k, 2), :, 0, :, u * CH:(u + 1) * CH]
                             .rearrange("g h r t -> (g h) r t")).then_inc(ld, 16)
                sp.dma_start(din[:, u, k], r_src[bass.ds(b * H + HP * k, HP), None, u * CH:(u + 1) * CH]
                             .to_broadcast([HP, HD, CH])).then_inc(ld, 16)

        with ExitStack() as st:
            scope[0] = st
            oin = sb("c_oin", [P, 2, KT, CH])
            din = sb("c_din", [P, 2, KT, CH])
            den = sb("c_den", [P, CH])
            xin = sb("c_xin", [P, 2, J, D])
            min_ = sb("c_min", [P, 2, J, S2], U8)
            x1 = sb("c_x1", [P, 2, J, D])
            stat = sb("c_stat", [P, 2, J, 6])
            mom = sb("c_mom", [P, 2, 6, J])
            ve = sb("c_ve", [P, 2, J])
            rstd = sb("c_rstd", [P, 2, J])
            allm = sb("c_allm", [P, 2, J])
            live = sb("c_live", [P, 2, J])
            meff = sb("c_meff", [P, 2, J, SK], BF16)
            xn = sb("c_xn", [P, 2, J, D])
            xnt = sb("c_xnt", [P, 2, KT, CH])
            parts = sb("c_parts", [P, 2, KT, 3, CH], BF16)
            rest = sb("c_rest", [P, KT, CH])
            mtr = sb("c_mtr", [SK, 2, CH], BF16)

            ld = [sem(f"c_ld{u}") for u in range(2)]
            s_den = sem("c_den_")
            s_rd = sem("c_rd")
            s_on = sem("c_on")
            s_xb = sem("c_xb")
            s_op = sem("c_op")
            s_x1 = sem("c_x1_")
            x1o = [sem(f"c_x1o{u}") for u in range(2)]
            s_sum = sem("c_sum")
            s_pow = sem("c_pow")
            s_all = sem("c_all")
            s_sc = sem("c_sc")
            s_me = sem("c_me")
            s_xn = sem("c_xn_")
            s_mtp = sem("c_mtp")
            s_mts = sem("c_mts")
            mo = [sem(f"c_mo{u}") for u in range(2)]
            s_tr = sem("c_tr")
            s_xt = sem("c_xt")
            s_q = sem("c_q")
            s_hi = sem("c_hi")
            s_r = sem("c_r")
            s_m = sem("c_m")
            s_lo = sem("c_lo")
            so = [sem(f"c_so{u}") for u in range(2)]
            OB, TB, QB, MB = (0, 1), (2, 3), (4, 5), 6
            NSO = 16 * KT * len(Q_PARTS)

            block = st.enter_context(nc.Block())

            @block.sync
            def _(sp):
                for s_, n in ((s_on, 2), (s_op, 4), (s_x1, 2), (s_me, 4), (s_xn, 8), (s_mtp, 2), (s_mts, 1),
                              (s_tr, 4), (s_xt, 2), (s_q, 4), (s_r, 2), (s_lo, 2)):
                    sp.sem_inc(s_, n)
                for u in range(2):
                    sp.sem_inc(x1o[u], 16)
                    sp.sem_inc(mo[u], 64)
                    sp.sem_inc(so[u], NSO)

                def load(b, u):
                    c = 2 * b + u
                    chunk_loads(sp, od, rdn, b, u, oin, din, ld[u])
                    sp.dma_start(xin[:, u], xv[bass.ds(c, 1)].rearrange("a p j d -> (a p) j d")).then_inc(ld[u], 16)
                    sp.dma_start(min_[:, u], mv[bass.ds(c, 1)].rearrange("a p j k -> (a p) j k")).then_inc(ld[u], 16)

                sp.dma_start(den[:], od[:, :, 1, 0].rearrange("g h (c t) -> (g h) c t", c=2)).then_inc(s_den, 16)
                sp.wait_ge(s_rd, 1)
                sp.dma_start(rdn.rearrange("h (c t) -> (h c) t", c=2), den[:]).then_inc(s_den, 16)
                sp.wait_ge(s_den, 32)
                load(0, 0)
                load(0, 1)

                def chunk(b, u, more):
                    c = 2 * b + u
                    sp.wait_ge(s_x1, 2 + 2 * c + 2)
                    sp.dma_start(x1s[bass.ds(c, 1)].rearrange("a p j d -> (a p) j d"), x1[:, u]).then_inc(x1o[u], 16)
                    if again(b):
                        sp.wait_ge(s_me, 4 + 4 * c + 4)
                        load(b + 1, u)
                    sp.wait_ge(s_mts, 1 + c + 1)
                    sp.dma_start(mts[bass.ds(b * GB, GB), :, u * CH:(u + 1) * CH].rearrange("g k t -> k g t"),
                                 mtr[:, u:u + 1].to_broadcast([SK, GB, CH])).then_inc(mo[u], 64)
                    for n in range(KT):
                        sp.wait_ge(s_lo, 2 + 2 * c + n + 1)
                        for slot, part in enumerate(Q_PARTS):
                            sp.dma_start(xqs[HD * slot:HD * (slot + 1), bass.ds(b * H + HP * n, HP), u * CH:(u + 1) * CH]
                                         .rearrange("r h t -> h r t"), parts[:, u, n, part]).then_inc(so[u], 16)

                sweep(sp, chunk)
                for u in range(2):
                    sp.wait_ge(x1o[u], 16 * (B + 1))
                    sp.wait_ge(mo[u], 64 * (B + 1))
                    sp.wait_ge(so[u], NSO * (B + 1))
                barrier(sp, 4)

            @block.gpsimd
            def _(g):
                def quotients(b, u):
                    c = 2 * b + u
                    g.wait_ge(ld[u], 96 * (b + 1))
                    nc.gpsimd.tensor_tensor(oin[:, u], oin[:, u], din[:, u], ALU.mult).then_inc(s_on, 1)
                    nc.gpsimd.tensor_tensor(xin[:, u], xin[:, u], bo_b[:, None, :].to_broadcast([P, J, D]),
                                            ALU.add).then_inc(s_xb, 1)

                def power(b, u):
                    c = 2 * b + u
                    g.wait_ge(s_sum, NSUM * (c + 1))
                    g.wait_ge(s_xn, J * c + J)
                    nc.gpsimd.tensor_tensor(rstd[:, u], ve[:, u], mhalf[:], ALU.pow).then_inc(s_pow, 1)

                def low(b, u, n):
                    c = 2 * b + u
                    g.wait_ge(s_m, 2 * c + n + 1)
                    nc.gpsimd.tensor_tensor(parts[:, u, n, 2], rest[:, n], parts[:, u, n, 1],
                                            ALU.subtract).then_inc(s_lo, 1)

                def chunk(b, u, more):
                    if more:
                        power(b + u, 1 - u)
                    low(b, u, 0)
                    low(b, u, 1)
                    if again(b):
                        quotients(b + 1, u)

                quotients(0, 0)
                quotients(0, 1)
                power(0, 0)
                sweep(g, chunk)
                barrier(g, 4)

            @block.vector
            def _(v):
                for u in range(2):
                    nc.vector.memset(meff[:, u, :, S2:SK], 1.0)
                v.wait_ge(s_den, 16)
                nc.vector.reciprocal(den[:], den[:]).then_inc(s_rd, 1)

                def masks(b, u):
                    c = 2 * b + u
                    v.wait_ge(ld[u], 96 * (b + 1))
                    v.wait_ge(s_mtp, c + 1)
                    nc.vector.tensor_reduce(allm[:, u], min_[:, u], AX, ALU.min).then_inc(s_all, 1)
                    v.wait_ge(s_all, 2 * c + 1)
                    nc.vector.tensor_scalar(live[:, u], allm[:, u], -1.0, 1.0, ALU.mult, ALU.add).then_inc(s_all, 1)
                    v.wait_ge(s_all, 2 * c + 2)
                    for j in range(J):
                        nc.vector.tensor_scalar(meff[:, u, j, 0:S2], min_[:, u, j], live[:, u, j:j + 1], None,
                                                ALU.mult).then_inc(s_me, 1)

                def sums(b, u):
                    c = 2 * b + u
                    v.wait_ge(s_xb, c + 1)
                    v.wait_ge(x1o[u], 16 * (b + 1))
                    for w in range(2):
                        v.wait_ge(s_op, 4 + 2 * c + w + 1)
                        nc.vector.tensor_tensor(x1[:, u, 2 * w:2 * w + 2].rearrange("p j d -> p (j d)"), bank[OB[w]][:],
                                                xin[:, u, 2 * w:2 * w + 2].rearrange("p j d -> p (j d)"),
                                                ALU.add).then_inc(s_x1, 1)
                    v.wait_ge(s_x1, 2 + 2 * c + 2)
                    moments(v, s_sum, c, x1[:, u], stat[:, u], mom[:, u], ve[:, u])

                def normalise(b, u):
                    c = 2 * b + u
                    v.wait_ge(s_pow, c + 1)
                    nc.vector.tensor_tensor(rstd[:, u], rstd[:, u], live[:, u], ALU.mult).then_inc(s_sc, 1)
                    v.wait_ge(s_sc, c + 1)
                    v.wait_ge(s_tr, 2 * c + 2)
                    for j in range(J):
                        nc.vector.tensor_scalar(xn[:, u, j], x1[:, u, j], mom[:, u, 0, j:j + 1], rstd[:, u, j:j + 1],
                                                ALU.subtract, ALU.mult).then_inc(s_xn, 1)

                def split(b, u, n):
                    c = 2 * b + u
                    v.wait_ge(s_hi, 2 * c + n + 1)
                    v.wait_ge(s_lo, 2 * c + n + 1)
                    nc.vector.scalar_tensor_tensor(rest[:, n], bank[QB[n]][:], SCALE,
                                                   parts[:, u, n, 0], ALU.mult, ALU.subtract).then_inc(s_r, 1)
                    v.wait_ge(s_r, 2 + 2 * c + n + 1)
                    nc.vector.tensor_copy(parts[:, u, n, 1], rest[:, n]).then_inc(s_m, 1)

                def chunk(b, u, more):
                    nb, nu = b + u, 1 - u
                    if more:
                        sums(nb, nu)
                    split(b, u, 0)
                    if more:
                        normalise(nb, nu)
                    split(b, u, 1)
                    if again(b):
                        masks(b + 1, u)

                masks(0, 0)
                masks(0, 1)
                sums(0, 0)
                normalise(0, 0)
                sweep(v, chunk)
                barrier(v, 4)

            @block.scalar
            def _(a):
                def turned(b, u):
                    c = 2 * b + u
                    a.wait_ge(s_q, 2 * c + 2)
                    for k in range(KT):
                        a.wait_ge(s_tr, 4 + 2 * c + k + 1)
                        nc.scalar.activation(xnt[:, u, k], bank[TB[k]][:], ACT.Identity).then_inc(s_xt, 1)
                    a.wait_ge(s_mtp, 2 + c + 1)
                    a.wait_ge(mo[u], 64 * (b + 1))
                    nc.scalar.activation(mtr[:, u], bank[MB][0:SK, 0:CH // 2].bitcast(BF16), ACT.Identity).then_inc(s_mts, 1)

                def chunk(b, u, more):
                    c = 2 * b + u
                    a.wait_ge(so[u], NSO * (b + 1))
                    for n in range(KT):
                        a.wait_ge(s_q, 4 + 2 * c + n + 1)
                        nc.scalar.activation(parts[:, u, n, 0], bank[QB[n]][:], ACT.Identity, scale=SCALE).then_inc(s_hi, 1)
                    if more:
                        turned(b + u, 1 - u)

                turned(0, 0)
                sweep(a, chunk)
                barrier(a, 4)

            @block.tensor
            def _(t):
                def project(b, u):
                    c = 2 * b + u
                    t.wait_ge(s_on, 2 + c + 1)
                    for w in range(2):
                        t.wait_ge(s_x1, 2 * c + w + 1)
                        for i in range(2):
                            for k in range(KT):
                                mm = nc.tensor.matmul(bank[OB[w]][:, i * D:(i + 1) * D],
                                                      oin[:, u, k, (2 * w + i) * P:(2 * w + i + 1) * P], wo_t[:, k],
                                                      start=(k == 0), stop=(k == KT - 1))
                        mm.then_inc(s_op, 1)

                def turn(b, u):
                    c = 2 * b + u
                    t.wait_ge(s_xn, 8 + 4 * c + 4)
                    for k in range(KT):
                        t.wait_ge(s_xt, 2 * c + k + 1)
                        for j in range(J):
                            mm = nc.tensor.transpose(bank[TB[k]][:, j * P:(j + 1) * P],
                                                     xn[:, u, j, k * P:(k + 1) * P], ident[:])
                        mm.then_inc(s_tr, 1)
                    t.wait_ge(s_me, 4 + 4 * c + 4)
                    t.wait_ge(s_mts, c + 1)
                    for j in range(J):
                        mm = nc.tensor.transpose(bank[MB][0:SK, j * P // 2:(j + 1) * P // 2].bitcast(BF16),
                                                 meff[:, u, j], identb[:])
                    mm.then_inc(s_mtp, 1)

                def chunk(b, u, more):
                    c = 2 * b + u
                    if more:
                        project(b + u, 1 - u)
                    t.wait_ge(s_xt, 2 + 2 * c + 2)
                    for n in range(KT):
                        t.wait_ge(s_r, 2 * c + n + 1)
                        for k in range(KT):
                            mm = nc.tensor.matmul(bank[QB[n]][:], xwq[:, k, n * P:(n + 1) * P], xnt[:, u, k],
                                                  start=(k == 0), stop=(k == KT - 1))
                        mm.then_inc(s_q, 1)
                    if more:
                        turn(b + u, 1 - u)

                project(0, 0)
                turn(0, 0)
                sweep(t, chunk)
                barrier(t, 4)

        attention(5, "cross_", False, 2, load_cross, 3, xvs, mts, od2)

        with ExitStack() as st:
            scope[0] = st
            oin = sb("e_oin", [P, 2, KT, CH])
            din = sb("e_din", [P, 2, KT, CH])
            den = sb("e_den", [P, CH])
            xin = sb("e_xin", [P, 2, J, D])
            x2 = sb("e_x2", [P, 2, J, D])
            yo = sb("e_yo", [P, 2, J, D])
            stat = sb("e_stat", [P, 2, J, 6])
            mom = sb("e_mom", [P, 2, 6, J])
            ve = sb("e_ve", [P, 2, J])
            rstd = sb("e_rstd", [P, 2, J])
            xn = sb("e_xn", [P, 2, J, D])
            xnt = sb("e_xnt", [P, 2, KT, CH])
            sg = sb("e_sg", [P, 2, CH])
            ht = sb("e_ht", [P, HT, CH])

            ld = [sem(f"e_ld{u}") for u in range(2)]
            s_den = sem("e_den_")
            s_rd = sem("e_rd")
            s_on = sem("e_on")
            s_op = sem("e_op")
            s_x2 = sem("e_x2_")
            s_sum = sem("e_sum")
            s_pow = sem("e_pow")
            s_xn = sem("e_xn_")
            s_tr = sem("e_tr")
            s_xt = sem("e_xt")
            s_gu = sem("e_gu")
            s_sg = sem("e_sg_")
            s_h = sem("e_h")
            s_y = sem("e_y")
            s_yo = sem("e_yo_")
            yd = [sem(f"e_yd{u}") for u in range(2)]
            OB, TB = (0, 1), (2, 3)

            block = st.enter_context(nc.Block())

            @block.sync
            def _(sp):
                for s_, n in ((s_on, 2), (s_op, 4), (s_xn, 8), (s_tr, 4), (s_xt, 2), (s_gu, 12), (s_sg, 2),
                              (s_h, 2), (s_y, 2), (s_yo, 4)):
                    sp.sem_inc(s_, n)
                for u in range(2):
                    sp.sem_inc(yd[u], 16)

                def load(b, u):
                    c = 2 * b + u
                    chunk_loads(sp, od2, rdn2, b, u, oin, din, ld[u])
                    sp.dma_start(xin[:, u], x1s[bass.ds(c, 1)].rearrange("a p j d -> (a p) j d")).then_inc(ld[u], 16)

                sp.dma_start(den[:], od2[:, :, 1, 0].rearrange("g h (c t) -> (g h) c t", c=2)).then_inc(s_den, 16)
                sp.wait_ge(s_rd, 1)
                sp.dma_start(rdn2.rearrange("h (c t) -> (h c) t", c=2), den[:]).then_inc(s_den, 16)
                sp.wait_ge(s_den, 32)
                load(0, 0)
                load(0, 1)

                def chunk(b, u, more):
                    c = 2 * b + u
                    if again(b):
                        sp.wait_ge(s_x2, 2 * c + 2)
                        load(b + 1, u)
                    sp.wait_ge(s_yo, 4 + 2 * c + 2)
                    sp.dma_start(ov[bass.ds(c, 1)].rearrange("a p j d -> (a p) j d"), yo[:, u]).then_inc(yd[u], 16)

                sweep(sp, chunk)
                for u in range(2):
                    sp.wait_ge(yd[u], 16 * (B + 1))
                barrier(sp, 6)

            @block.gpsimd
            def _(g):
                def quotients(b, u):
                    c = 2 * b + u
                    g.wait_ge(ld[u], 80 * (b + 1))
                    nc.gpsimd.tensor_tensor(oin[:, u], oin[:, u], din[:, u], ALU.mult).then_inc(s_on, 1)

                def power(b, u):
                    c = 2 * b + u
                    g.wait_ge(s_sum, NSUM * (c + 1))
                    g.wait_ge(s_xn, J * c + J)
                    nc.gpsimd.tensor_tensor(rstd[:, u], ve[:, u], mhalf[:], ALU.pow).then_inc(s_pow, 1)

                def chunk(b, u, more):
                    if more:
                        power(b + u, 1 - u)
                    if again(b):
                        quotients(b + 1, u)

                quotients(0, 0)
                quotients(0, 1)
                power(0, 0)
                sweep(g, chunk)
                barrier(g, 6)

            @block.vector
            def _(v):
                def sums(b, u):
                    c = 2 * b + u
                    for w in range(2):
                        v.wait_ge(s_op, 4 + 2 * c + w + 1)
                        nc.vector.tensor_tensor(x2[:, u, 2 * w:2 * w + 2].rearrange("p j d -> p (j d)"), bank[OB[w]][:],
                                                xin[:, u, 2 * w:2 * w + 2].rearrange("p j d -> p (j d)"),
                                                ALU.add).then_inc(s_x2, 1)
                    v.wait_ge(s_x2, 2 * c + 2)
                    moments(v, s_sum, c, x2[:, u], stat[:, u], mom[:, u], ve[:, u])

                def normalise(b, u):
                    c = 2 * b + u
                    v.wait_ge(s_pow, c + 1)
                    v.wait_ge(s_tr, 2 * c + 2)
                    for j in range(J):
                        nc.vector.tensor_scalar(xn[:, u, j], x2[:, u, j], mom[:, u, 0, j:j + 1], rstd[:, u, j:j + 1],
                                                ALU.subtract, ALU.mult).then_inc(s_xn, 1)

                def hidden(b, u, h):
                    c = 2 * b + u
                    if h == 0:
                        v.wait_ge(s_y, 2 * c + 2)
                    v.wait_ge(s_sg, 2 + HT * c + h + 1)
                    nc.vector.tensor_tensor(ht[:, h], bank[5 + 2 * (h % 2)][:], sg[:, h % 2], ALU.mult).then_inc(s_h, 1)

                def chunk(b, u, more):
                    c = 2 * b + u
                    nb, nu = b + u, 1 - u
                    hidden(b, u, 0)
                    hidden(b, u, 1)
                    hidden(b, u, 2)
                    if more:
                        sums(nb, nu)
                    hidden(b, u, 3)
                    hidden(b, u, 4)
                    if more:
                        normalise(nb, nu)
                    hidden(b, u, 5)
                    v.wait_ge(yd[u], 16 * (b + 1))
                    for w in range(2):
                        v.wait_ge(s_y, 2 + 2 * c + w + 1)
                        nc.vector.tensor_tensor(yo[:, u, 2 * w:2 * w + 2].rearrange("p j d -> p (j d)"), bank[OB[w]][:],
                                                x2[:, u, 2 * w:2 * w + 2].rearrange("p j d -> p (j d)"),
                                                ALU.add).then_inc(s_yo, 1)

                v.wait_ge(s_den, 16)
                nc.vector.reciprocal(den[:], den[:]).then_inc(s_rd, 1)
                sums(0, 0)
                normalise(0, 0)
                sweep(v, chunk)
                barrier(v, 6)

            @block.scalar
            def _(a):
                def turned(b, u):
                    c = 2 * b + u
                    a.wait_ge(s_gu, HT * c + HT)
                    for k in range(KT):
                        a.wait_ge(s_tr, 4 + 2 * c + k + 1)
                        nc.scalar.activation(xnt[:, u, k], bank[TB[k]][:], ACT.Identity).then_inc(s_xt, 1)

                def chunk(b, u, more):
                    c = 2 * b + u
                    for h in range(HT):
                        a.wait_ge(s_gu, 2 * HT + HT * c + h + 1)
                        a.wait_ge(s_h, HT * c + h + 1)
                        nc.scalar.activation(sg[:, h % 2], bank[4 + 2 * (h % 2)][:], ACT.Silu).then_inc(s_sg, 1)
                    if more:
                        turned(b + u, 1 - u)

                turned(0, 0)
                sweep(a, chunk)
                barrier(a, 6)

            @block.tensor
            def _(t):
                def project(b, u):
                    c = 2 * b + u
                    t.wait_ge(s_on, 2 + c + 1)
                    t.wait_ge(s_yo, 2 * c + 2)
                    for w in range(2):
                        for i in range(2):
                            for k in range(KT):
                                mm = nc.tensor.matmul(bank[OB[w]][:, i * D:(i + 1) * D],
                                                      oin[:, u, k, (2 * w + i) * P:(2 * w + i + 1) * P], xwo[:, k],
                                                      start=(k == 0), stop=(k == KT - 1))
                        mm.then_inc(s_op, 1)

                def turn(b, u):
                    c = 2 * b + u
                    t.wait_ge(s_xn, 8 + 4 * c + 4)
                    for k in range(KT):
                        t.wait_ge(s_xt, 2 * c + k + 1)
                        for j in range(J):
                            mm = nc.tensor.transpose(bank[TB[k]][:, j * P:(j + 1) * P],
                                                     xn[:, u, j, k * P:(k + 1) * P], ident[:])
                        mm.then_inc(s_tr, 1)

                def gate_up(b, u, h):
                    c = 2 * b + u
                    t.wait_ge(s_h, HT * c + h + 1)
                    for w_, o in ((wg_t, 4), (wu_t, 5)):
                        for k in range(KT):
                            mm = nc.tensor.matmul(bank[o + 2 * (h % 2)][:], w_[:, k, h * P:(h + 1) * P], xnt[:, u, k],
                                                  start=(k == 0), stop=(k == KT - 1))
                    mm.then_inc(s_gu, 1)

                def down(b, u, more):
                    c = 2 * b + u
                    t.wait_ge(s_h, 2 + HT * (c + 1))
                    if more:
                        t.wait_ge(s_x2, 2 * (c + 1) + 2)
                    for w in range(2):
                        for i in range(2):
                            for h in range(HT):
                                mm = nc.tensor.matmul(bank[OB[w]][:, i * D:(i + 1) * D],
                                                      ht[:, h, (2 * w + i) * P:(2 * w + i + 1) * P], wd_t[:, h],
                                                      start=(h == 0), stop=(h == HT - 1))
                        mm.then_inc(s_y, 1)

                def chunk(b, u, more):
                    c = 2 * b + u
                    t.wait_ge(s_xt, 2 + 2 * c + 2)
                    gate_up(b, u, 0)
                    gate_up(b, u, 1)
                    if more:
                        project(b + u, 1 - u)
                    for h in range(2, HT):
                        gate_up(b, u, h)
                    if more:
                        turn(b + u, 1 - u)
                    down(b, u, more)

                project(0, 0)
                turn(0, 0)
                sweep(t, chunk)
                barrier(t, 6)


_INS = ["x", "ctx_1024", "mask_BxSxS2_bk1", "L0_attn_Wq", "L0_attn_bq", "L0_attn_Wk", "L0_attn_bk",
        "L0_attn_Wv", "L0_attn_bv", "L0_attn_Wo", "L0_attn_bo", "L0_attn_W_cross",
        "L0_attn_shift_weights", "L0_attn_gate", "L0_xattn_Wq", "L0_xattn_Wk", "L0_xattn_Wv",
        "L0_xattn_Wo", "L0_ffn_w_gate", "L0_ffn_w_up", "L0_ffn_w_down"]


def kernel(**inputs):
    import numpy as np
    import concourse.bacc as bacc
    from concourse.bass_utils import run_bass_kernel_spmd

    nc = bacc.Bacc("TRN2", target_bir_lowering=False, num_devices=1)
    arrays, args = {}, []
    for name in _INS:
        a = np.ascontiguousarray(inputs[name])
        arrays[name] = a
        args.append(nc.dram_tensor(name, a.shape, mybir.dt.from_np(a.dtype), kind="ExternalInput").ap())
    out = nc.dram_tensor("out", inputs["x"].shape, F32, kind="ExternalOutput").ap()
    program(nc, *args, out)
    r = run_bass_kernel_spmd(nc, [arrays], core_ids=[0])
    return r.results[0]["out"]
```

```python
from contextlib import ExitStack

import concourse.bass as bass
from concourse import mybir

F32 = mybir.dt.float32
F32R = mybir.dt.float32r
BF16 = mybir.dt.bfloat16
I32 = mybir.dt.int32
U8 = mybir.dt.uint8
ALU = mybir.AluOpType
ACT = mybir.ActivationFunctionType
AX = mybir.AxisListType.X

P = 128
NEG = -1.0e30
EPS = 1e-5
HG = 4
Q_PARTS = (0, 0, 1, 1, 0, 2)
K_PARTS = (0, 1, 0, 1, 2, 0)
MX_BANKS, ST_BANKS, PV_BANKS = (0, 1, 2), (3, 4, 5), (6, 7)


def program(nc, x, ctxt, mask, Wq, bq, Wk, bk, Wv, bv, Wo, bo, W_cross, shift_w, gate,
            xWq, xWk, xWv, xWo, w_gate, w_up, w_down, out):
    B, S, D = x.shape
    S2 = ctxt.shape[1]
    H, HD = W_cross.shape[0], W_cross.shape[1]
    MS = shift_w.shape[1]
    HID = w_gate.shape[0]
    KT = D // P
    HT = HID // P
    CH = 512
    J = CH // P
    G = B * H // HG
    GB = H // HG
    HP = P // HD
    SK = 96
    R = len(Q_PARTS) * HD
    RM = R + 2
    VW = 2 * HD
    SCALE = float(HD) ** -0.5
    WSCALE = 1.0 / 127.0
    NCH = B * S // CH
    assert (D, HD, S, S2 <= SK, HG * VW, NCH) == (256, 16, 1024, True, P, 2 * B)

    def dram(name, shape, dt):
        return nc.dram_tensor(name, shape, dt, kind="Internal").ap()

    qk3 = dram("qk3", (2, 3, G, HG * HD, S), BF16)
    vs = dram("vs", (G, P, S // P, HG * VW), F32)
    od = dram("od", (G, HG, 2, HD, S), F32)
    x1s = dram("x1s", (NCH, P, J, D), F32)
    xqs = dram("xqs", (R, G * HG, S), BF16)
    xk3 = dram("xk3", (3, G * HG, HD, SK), BF16)
    xks = dram("xks", (R, G * HG, SK), BF16)
    xvs = dram("xvs", (G, SK, 1, HG * VW), F32)
    mts = dram("mts", (G, SK, S), BF16)
    rdn = dram("rdn", (G * HG, S), F32)
    rdn2 = dram("rdn2", (G * HG, S), F32)
    od2 = dram("od2", (G, HG, 2, HD, S), F32)

    xv = x.rearrange("b (h j p) d -> (b h) p j d", j=J, p=P)
    ov = out.rearrange("b (h j p) d -> (b h) p j d", j=J, p=P)
    mv = mask.rearrange("b (h j p) k -> (b h) p j k", j=J, p=P)

    root = ExitStack()
    with root:
        scope = [root]

        def sb(name, shape, dt=F32):
            return scope[0].enter_context(nc.sbuf_tensor(name, shape, dt))

        def sem(name):
            return scope[0].enter_context(nc.semaphore(name))

        bank = [root.enter_context(nc.psum_tensor(f"bank{i}", [P, 512], F32)) for i in range(8)]
        s_phase = sem("s_phase")

        def barrier(eng, n):
            eng.drain().then_inc(s_phase, 1)
            eng.wait_ge(s_phase, 5 * n)

        ident = sb("ident", [P, P])
        identb = sb("identb", [P, P], BF16)
        tri_q = sb("tri_q", [P, HG, P], BF16)
        tri_k = sb("tri_k", [P, HG, P], BF16)
        negid = sb("negid", [SK, HG, SK], BF16)
        wq_t = sb("wq_t", [P, 2, KT, D], F32R)
        wk_t = sb("wk_t", [P, 2, KT, D], F32R)
        wv_t = sb("wv_t", [P, 2, KT, D], F32R)
        wo_t = sb("wo_t", [P, KT, D])
        xwq = sb("xwq", [P, KT, D])
        xwo = sb("xwo", [P, KT, D])
        qkb = sb("qkb", [P, 2, KT])
        bv_b = sb("bv_b", [P, H, HD])
        bo_b = sb("bo_b", [P, D])
        wg_t = sb("wg_t", [P, 2, KT, HID], F32R)
        wu_t = sb("wu_t", [P, 2, KT, HID], F32R)
        wd_t = sb("wd_t", [P, 2, HT, D], F32R)
        mhalf = sb("mhalf", [P, J])

        with ExitStack() as st:
            scope[0] = st
            n_q = sb("n_q", [P, KT, D])
            n_k = sb("n_k", [P, KT, D])
            n_v = sb("n_v", [P, KT, D])
            n_o = sb("n_o", [P, KT, D])
            ig = sb("ig", [P, HT, D], I32)
            iu = sb("iu", [P, HT, D], I32)
            idn = sb("idn", [P, KT, HID], I32)
            fg = sb("fg", [P, HT, D])
            fu = sb("fu", [P, HT, D])
            fd = sb("fd", [P, KT, HID])
            xwk = sb("xwk", [P, KT, D])
            xwv = sb("xwv", [P, KT, D])
            bq_c = sb("bq_c", [P, KT])
            wc = sb("wc", [P, KT, HD])
            sw = sb("sw", [P, KT, MS])
            gt = sb("gt", [P, KT])
            ge = sb("ge", [P, KT])
            gs = sb("gs", [P, 2, KT])
            blk = sb("blk", [P, P])
            tau = sb("tau", [P, MS, P])
            mm_ = sb("mm_", [P, KT, P])
            ablk = sb("ablk", [P, KT, P])
            cn = sb("cn", [S2, B, D])
            c_t = sb("c_t", [P, KT, B, S2])
            k3 = sb("k3", [P, KT, 3, B, SK], BF16)
            kr = sb("kr", [P, B, S2])
            vx = sb("vx", [SK, B, H, VW])
            trif = sb("trif", [P, 2, P])

            s_in = sem("w_in")
            s_in2 = sem("w_in2")
            s_g = sem("w_g")
            s_v = sem("w_v")
            s_a = sem("w_a")
            s_ab = sem("w_ab")
            s_f = sem("w_f")
            s_t = sem("w_t")
            s_e = sem("w_e")
            s_el = sem("w_el")
            s_k = sem("w_k")
            s_kh = sem("w_kh")
            s_vx = sem("w_vx")
            s_out = sem("w_out")
            s_stk = sem("w_stk")

            def cols(a):
                return a.rearrange("(t p) -> p t", p=P)

            N_IN, N_IN2 = 5 + 2 + 2 * KT + 4, 8
            jobs = []

            def turned(src, dst, nk, no):
                for k in range(nk):
                    for o in range(0, no, 4):
                        n = min(4, no - o)
                        jobs.append(([src[:, o + i, k * P:(k + 1) * P] for i in range(n)],
                                     [d[:, k, o * P:(o + n) * P] for d in dst]))

            def both(w):
                return w[:, 0], w[:, 1]

            turned(n_k, both(wk_t), KT, KT)
            turned(n_v, both(wv_t), KT, KT)
            turned(n_o, (wo_t,), KT, KT)
            n_small = len(jobs)
            turned(fg, both(wg_t), KT, HT)
            turned(fu, both(wu_t), KT, HT)
            turned(fd, both(wd_t), HT, KT)
            NJ = len(jobs)
            cut = [n for n in range(NJ + KT) if n >= NJ or len(jobs[n][1]) == 2]
            N_FOLD = NJ + KT
            N_BIAS = N_FOLD + 1
            N_CTX = N_BIAS + KT
            N_XK = N_CTX + KT
            NB = 8

            block = st.enter_context(nc.Block())

            @block.sync
            def _(sp):
                for dst, src in ((n_q, Wq), (n_k, Wk), (n_v, Wv), (n_o, Wo)):
                    sp.dma_start(dst[:], src.rearrange("(t p) n -> p t n", p=P)).then_inc(s_in, 16)
                sp.dma_start(wc[:], W_cross.rearrange("(t h) f g -> (h f) t g", t=KT)).then_inc(s_in, 16)
                with nc.allow_non_contiguous_dma(reason="biases on partitions, a few hundred words"):
                    sp.dma_start(bq_c[:], cols(bq)).then_inc(s_in, 16)
                    sp.dma_start(qkb[:, 1, :], cols(bk)).then_inc(s_in, 16)
                    for t in range(KT):
                        hs = slice(t * HP, (t + 1) * HP)
                        sp.dma_start(sw[:, t, :], shift_w[hs, None, :].to_broadcast([HP, HD, MS])).then_inc(s_in, 16)
                        sp.dma_start(gt[:, t:t + 1],
                                     gate[hs].rearrange("(h a b) -> h a b", a=1, b=1).to_broadcast([HP, HD, 1])).then_inc(s_in, 16)
                sp.dma_start(bv_b[:], bv.rearrange("(a n) -> a n", a=1).to_broadcast([P, D])).then_inc(s_in, 16)
                sp.dma_start(bo_b[:], bo.rearrange("(a n) -> a n", a=1).to_broadcast([P, D])).then_inc(s_in, 16)
                sp.dma_start(xwq[:], xWq.rearrange("(t p) n -> p t n", p=P)).then_inc(s_in, 16)
                sp.dma_start(xwo[:], xWo.rearrange("(t p) n -> p t n", p=P)).then_inc(s_in, 16)
                for dst, src in ((ig, w_gate), (iu, w_up), (idn, w_down), (xwk, xWk), (xwv, xWv)):
                    sp.dma_start(dst[:], src.rearrange("(t p) n -> p t n", p=P)).then_inc(s_in2, 16)
                sp.dma_start(cn[:], ctxt.rearrange("b s d -> s b d")).then_inc(s_in2, 16)
                sp.wait_ge(s_k, 3 * KT)
                for t in range(KT):
                    for b in range(B):
                        sp.dma_start(
                            xk3[:, b * H + HP * t:b * H + HP * (t + 1)].rearrange("c h r k -> (h r) c k"),
                            k3[:, t, :, b, :]).then_inc(s_out, 16)
                sp.wait_ge(s_vx, 1 + B)
                for b in range(B):
                    sp.dma_start(xvs[b * GB:(b + 1) * GB].rearrange("g k a c -> (k a) g c"),
                                 vx[:, b].rearrange("k h c -> k (h c)").rearrange("k (g c) -> k g c", g=GB)).then_inc(s_out, 16)
                sp.wait_ge(s_in, 16 * N_IN)
                sp.wait_ge(s_in2, 16 * 6)
                sp.wait_ge(s_out, 16 * (KT * B + B))
                for slot, part in enumerate(K_PARTS):
                    sp.dma_start(xks[HD * slot:HD * (slot + 1)],
                                 xk3[part].rearrange("h r k -> r h k")).then_inc(s_stk, 16)
                sp.wait_ge(s_stk, 16 * len(K_PARTS))
                barrier(sp, 1)

            @block.gpsimd
            def _(g):
                nc.gpsimd.memset(ident[:], 0.0).then_inc(s_g, 1)
                nc.gpsimd.memset(trif[:], 0.0).then_inc(s_g, 1)
                nc.gpsimd.memset(blk[:], 1.0).then_inc(s_g, 1)
                nc.gpsimd.memset(tau[:], 0.0).then_inc(s_g, 1)
                g.wait_ge(s_g, 4)
                nc.gpsimd.affine_select(out=ident[:], in_=ident[:], compare_op=ALU.not_equal, fill=1.0,
                                        base=0, pattern=[[-1, P]], channel_multiplier=1).then_inc(s_g, 1)
                nc.gpsimd.affine_select(out=blk[:], in_=blk[:], compare_op=ALU.is_ge, fill=0.0,
                                        base=0, pattern=[[-HD, HP], [0, HD]], channel_multiplier=1).then_inc(s_g, 1)
                g.wait_ge(s_g, 6)
                nc.gpsimd.affine_select(out=blk[:], in_=blk[:], compare_op=ALU.is_ge, fill=0.0,
                                        base=HD - 1, pattern=[[HD, HP], [0, HD]], channel_multiplier=-1).then_inc(s_g, 1)
                nc.gpsimd.affine_select(out=tau[:], in_=tau[:], compare_op=ALU.not_equal, fill=1.0,
                                        base=0, pattern=[[-1, MS], [1, P]], channel_multiplier=-1).then_inc(s_g, 1)
                nc.gpsimd.affine_select(out=trif[:, 0, :], in_=trif[:, 0, :], compare_op=ALU.is_ge, fill=NEG,
                                        base=0, pattern=[[-1, P]], channel_multiplier=1).then_inc(s_g, 1)
                nc.gpsimd.affine_select(out=trif[:, 1, :], in_=trif[:, 1, :], compare_op=ALU.is_ge, fill=NEG,
                                        base=0, pattern=[[1, P]], channel_multiplier=-1).then_inc(s_g, 1)
                nc.gpsimd.memset(mhalf[:], -0.5)
                nc.gpsimd.memset(k3[:], 0.0).then_inc(s_g, 1)
                nc.gpsimd.memset(vx[:], 0.0).then_inc(s_g, 1)
                g.wait_ge(s_g, 12)
                nc.gpsimd.memset(vx[:, :, :, HD:VW], 1.0).then_inc(s_g, 1)
                for h in range(HG):
                    nc.gpsimd.tensor_copy(tri_q[:, h, :], trif[:, 0, :])
                    nc.gpsimd.tensor_copy(tri_k[:, h, :], trif[:, 1, :])
                    nc.gpsimd.tensor_scalar(negid[:, h, :], ident[0:SK, 0:SK], NEG, None, ALU.mult)
                nc.gpsimd.tensor_copy(identb[:], ident[:])
                barrier(g, 1)

            @block.vector
            def _(v):
                made = [0]

                def low(upto):
                    for n in cut[made[0]:upto]:
                        v.wait_ge(s_e, n + 1)
                        if n < NJ:
                            blocks, (hi, lo) = jobs[n]
                            w = len(blocks) * P
                        else:
                            hi, lo, w = wq_t[:, 0, n - NJ], wq_t[:, 1, n - NJ], D
                        nc.vector.tensor_tensor(lo, bank[n % NB][:, 0:w], hi.bitcast(F32), ALU.subtract).then_inc(s_el, 1)
                    made[0] = upto

                v.wait_ge(s_in, 16 * N_IN)
                v.wait_ge(s_a, 1)
                nc.vector.tensor_scalar(ge[:], ge[:], 1.0, None, ALU.add).then_inc(s_v, 1)
                v.wait_ge(s_v, 1)
                nc.vector.reciprocal(ge[:], ge[:]).then_inc(s_v, 1)
                v.wait_ge(s_v, 2)
                nc.vector.tensor_scalar(gs[:, 0, :], ge[:], SCALE, None, ALU.mult).then_inc(s_v, 1)
                nc.vector.tensor_scalar(gs[:, 1, :], ge[:], -SCALE, SCALE, ALU.mult, ALU.add).then_inc(s_v, 1)
                v.wait_ge(s_g, 10)
                n = 4
                for t in range(KT):
                    v.wait_ge(s_v, n)
                    nc.vector.tensor_scalar(mm_[:, t, :], tau[:, 0, :], sw[:, t, 0:1], None, ALU.mult).then_inc(s_v, 1)
                    n += 1
                    for s in range(1, MS):
                        v.wait_ge(s_v, n)
                        nc.vector.scalar_tensor_tensor(mm_[:, t, :], tau[:, s, :], sw[:, t, s:s + 1],
                                                       mm_[:, t, :], ALU.mult, ALU.add).then_inc(s_v, 1)
                        n += 1
                    v.wait_ge(s_v, n)
                    nc.vector.tensor_scalar(mm_[:, t, :], mm_[:, t, :], gs[:, 1, t:t + 1], None, ALU.mult).then_inc(s_v, 1)
                    n += 1
                    v.wait_ge(s_v, n)
                    nc.vector.scalar_tensor_tensor(
                        ablk[:, t, :].rearrange("p (h g) -> p h g", h=HP),
                        wc[:, t:t + 1, :].to_broadcast([P, HP, HD]), gs[:, 0, t:t + 1],
                        mm_[:, t, :].rearrange("p (h g) -> p h g", h=HP), ALU.mult, ALU.add).then_inc(s_v, 1)
                    n += 1
                    v.wait_ge(s_v, n)
                    nc.vector.tensor_tensor(ablk[:, t, :], ablk[:, t, :], blk[:], ALU.mult).then_inc(s_ab, 1)
                v.wait_ge(s_in2, 16 * 6)
                for f, i in ((fg, ig), (fu, iu), (fd, idn)):
                    nc.vector.tensor_scalar(f[:], i[:], WSCALE, None, ALU.mult).then_inc(s_f, 1)
                low(len(cut))
                v.wait_ge(s_g, 13)
                for t in range(KT):
                    ps = bank[(N_CTX + t) % NB][:, 0:B * S2].rearrange("p (b s) -> p b s", b=B)
                    v.wait_ge(s_kh, t + 1)
                    if t:
                        v.wait_ge(s_k, 3 * t)
                    nc.vector.tensor_tensor(kr[:], ps, k3[:, t, 0, :, 0:S2], ALU.subtract).then_inc(s_k, 1)
                    v.wait_ge(s_k, 3 * t + 1)
                    nc.vector.tensor_copy(k3[:, t, 1, :, 0:S2], kr[:]).then_inc(s_k, 1)
                    v.wait_ge(s_k, 3 * t + 2)
                    nc.vector.tensor_tensor(k3[:, t, 2, :, 0:S2], kr[:], k3[:, t, 1, :, 0:S2], ALU.subtract).then_inc(s_k, 1)
                barrier(v, 1)

            @block.scalar
            def _(a):
                a.wait_ge(s_in, 16 * N_IN)
                nc.scalar.activation(ge[:], gt[:], ACT.Exp, scale=-1.0).then_inc(s_a, 1)

                def empty(n, dst, src, **kw):
                    a.wait_ge(s_t, n + 1)
                    nc.scalar.activation(dst, src, ACT.Identity, **kw).then_inc(s_e, 1)

                for n, (blocks, dst) in enumerate(jobs):
                    empty(n, dst[0], bank[n % NB][:, 0:len(blocks) * P])
                for k in range(KT):
                    empty(NJ + k, wq_t[:, 0, k, :], bank[(NJ + k) % NB][:, 0:D])
                empty(N_FOLD, qkb[:, 0, :], bank[N_FOLD % NB][:, 0:KT])
                for k in range(KT):
                    empty(N_BIAS + k, c_t[:, k], bank[(N_BIAS + k) % NB][:, 0:B * S2].rearrange("p (b s) -> p b s", b=B))
                a.wait_ge(s_g, 13)
                for t in range(KT):
                    a.wait_ge(s_t, N_CTX + t + 1)
                    nc.scalar.activation(k3[:, t, 0, :, 0:S2],
                                         bank[(N_CTX + t) % NB][:, 0:B * S2].rearrange("p (b s) -> p b s", b=B),
                                         ACT.Identity).then_inc(s_kh, 1)
                nc.scalar.activation(gt[0:1, 0:1], gt[0:1, 0:1], ACT.Identity).then_inc(s_vx, 1)
                for b in range(B):
                    n = N_XK + b
                    a.wait_ge(s_t, n + 1)
                    nc.scalar.activation(vx[0:S2, b, :, 0:HD],
                                         bank[n % NB][0:S2, 0:D].rearrange("p (h d) -> p h d", h=H),
                                         ACT.Identity).then_inc(s_vx, 1)
                barrier(a, 1)

            @block.tensor
            def _(t_):
                t_.wait_ge(s_in, 16 * N_IN)
                t_.wait_ge(s_g, 5)

                def free(n):
                    if n >= NB:
                        t_.wait_ge(s_e, n - NB + 1)
                        if n - NB in cut:
                            t_.wait_ge(s_el, cut.index(n - NB) + 1)

                for n, (blocks, dst) in enumerate(jobs):
                    free(n)
                    if n >= n_small:
                        t_.wait_ge(s_f, 3)
                    for i, b_ in enumerate(blocks):
                        m = nc.tensor.transpose(bank[n % NB][:, i * P:(i + 1) * P], b_, ident[:])
                    m.then_inc(s_t, 1)
                t_.wait_ge(s_ab, KT)
                for k in range(KT):
                    free(NJ + k)
                    for o in range(KT):
                        m = nc.tensor.matmul(bank[(NJ + k) % NB][:, o * P:(o + 1) * P],
                                             n_q[:, o, k * P:(k + 1) * P], ablk[:, o, :], start=True, stop=True)
                    m.then_inc(s_t, 1)
                free(N_FOLD)
                for o in range(KT):
                    m = nc.tensor.matmul(bank[N_FOLD % NB][:, o:o + 1], ablk[:, o, :], bq_c[:, o:o + 1],
                                         start=True, stop=True)
                m.then_inc(s_t, 1)
                t_.wait_ge(s_in2, 16 * 6)
                for k in range(KT):
                    free(N_BIAS + k)
                    for b in range(B):
                        m = nc.tensor.transpose(bank[(N_BIAS + k) % NB][:, b * S2:(b + 1) * S2],
                                                cn[:, b, k * P:(k + 1) * P], ident[0:S2, 0:S2])
                    m.then_inc(s_t, 1)
                t_.wait_ge(s_e, N_CTX)
                t_.wait_ge(s_el, len(cut))
                for o in range(KT):
                    for k in range(KT):
                        m = nc.tensor.matmul(bank[(N_CTX + o) % NB][:, 0:B * S2],
                                             xwk[:, k, o * P:(o + 1) * P],
                                             c_t[:, k].rearrange("p b s -> p (b s)"),
                                             start=(k == 0), stop=(k == KT - 1))
                    m.then_inc(s_t, 1)
                for b in range(B):
                    for k in range(KT):
                        m = nc.tensor.matmul(bank[(N_XK + b) % NB][0:S2, 0:D], c_t[:, k, b, :], xwv[:, k, :],
                                             start=(k == 0), stop=(k == KT - 1))
                    m.then_inc(s_t, 1)
                barrier(t_, 1)

        def again(b):
            return not (isinstance(b, int) and b == B - 1)

        def sweep(eng, chunk, peeled=1):
            with eng.Fori(0, B - peeled) as b:
                chunk(b, 0, True)
                chunk(b, 1, True)
            for b in range(B - peeled, B):
                chunk(b, 0, True)
                chunk(b, 1, b < B - 1)

        def moments(v, s_sum, c, src, stat, mom, ve, which=(0, 1)):
            if 0 in which:
                for j in range(J):
                    nc.vector.bn_stats(stat[:, j], src[:, j]).then_inc(s_sum, 1)
            if 1 not in which:
                return
            v.wait_ge(s_sum, NSUM * c + J)
            even, odd = stat[:, :, 1], stat[:, :, 4]
            nc.vector.tensor_tensor(mom[:, 1], even, odd, ALU.add).then_inc(s_sum, 1)
            nc.vector.tensor_tensor(mom[:, 2], even, odd, ALU.subtract).then_inc(s_sum, 1)
            nc.vector.tensor_tensor(mom[:, 3], stat[:, :, 2], stat[:, :, 5], ALU.add).then_inc(s_sum, 1)
            v.wait_ge(s_sum, NSUM * c + J + 3)
            nc.vector.tensor_scalar(mom[:, 0], mom[:, 1], 0.5, None, ALU.mult).then_inc(s_sum, 1)
            nc.vector.scalar_tensor_tensor(mom[:, 4], mom[:, 2], 0.25, mom[:, 2], ALU.mult, ALU.mult).then_inc(s_sum, 1)
            nc.vector.tensor_scalar(mom[:, 5], mom[:, 3], 1.0 / D, EPS, ALU.mult, ALU.add).then_inc(s_sum, 1)
            v.wait_ge(s_sum, NSUM * c + J + 6)
            nc.vector.tensor_tensor(ve, mom[:, 4], mom[:, 5], ALU.add).then_inc(s_sum, 1)

        NSUM = J + 7

        def cut_products(dst, terms):
            n = 0
            for a, b in terms:
                for i, j in ((0, 0), (0, 1), (1, 0)):
                    mm = nc.tensor.matmul(dst, a[:, i], b[:, j], start=(n == 0), stop=(n == 3 * len(terms) - 1))
                    n += 1
            return mm

        with ExitStack() as st:
            scope[0] = st
            xin = sb("a_xin", [P, 2, J, D])
            stat = sb("a_stat", [P, 2, J, 6])
            mom = sb("a_mom", [P, 2, 6, J])
            ve = sb("a_ve", [P, 2, J])
            rstd = sb("a_rstd", [P, 2, J])
            xn = sb("a_xn", [P, 2, J, D])
            xnt = sb("a_xnt", [P, 2, 2, KT, CH], F32R)
            parts = sb("a_parts", [P, 2, 4, 3, CH], BF16)
            rest = sb("a_rest", [P, 4, CH])
            vst = sb("a_vst", [P, 2, GB, J, HG, VW])

            ld = [sem(f"a_ld{u}") for u in range(2)]
            s_sum = sem("a_sum")
            s_pow = sem("a_pow")
            s_xn = sem("a_xn_")
            s_tr = sem("a_tr")
            s_xh = sem("a_xh")
            s_xt = sem("a_xt")
            s_qk = sem("a_qk")
            s_hi = sem("a_hi")
            s_r = sem("a_r")
            s_m = sem("a_m")
            s_lo = sem("a_lo")
            so = [sem(f"a_so{u}") for u in range(2)]
            s_vm = sem("a_vm")
            s_ve = sem("a_ve_")
            vo = [sem(f"a_vo{u}") for u in range(2)]
            s_one = sem("a_one")
            QKB, VB = (2, 3, 4, 5), (6, 7)

            block = st.enter_context(nc.Block())

            @block.sync
            def _(sp):
                sp.sem_inc(s_xn, 2 * J)
                sp.sem_inc(s_tr, 4)
                sp.sem_inc(s_xt, 2)
                sp.sem_inc(s_r, 4)
                sp.sem_inc(s_lo, 4)
                sp.sem_inc(s_vm, 4)
                sp.sem_inc(s_ve, 2)
                for u in range(2):
                    sp.sem_inc(so[u], 64)
                    sp.sem_inc(vo[u], 16)
                for u in range(2):
                    sp.dma_start(xin[:, u], xv[u]).then_inc(ld[u], 16)

                sp.wait_ge(s_xn, 2 * J + J)
                sp.dma_start(xin[:, 0], xv[2]).then_inc(ld[0], 16)

                def chunk(b, u, more):
                    c = 2 * b + u
                    if not isinstance(b, int) or c + 3 < NCH:
                        sp.wait_ge(s_xn, 2 * J + J * (c + 1) + J)
                        sp.dma_start(xin[:, 1 - u], xv[bass.ds(c + 3, 1)].rearrange("a p j d -> (a p) j d")).then_inc(ld[1 - u], 16)
                    for n in range(4):
                        sp.wait_ge(s_lo, 4 + 4 * c + n + 1)
                        sp.dma_start(
                            qk3[n // 2, :, bass.ds(b * GB + 2 * (n % 2), 2), :, u * CH:(u + 1) * CH]
                            .rearrange("c g r t -> (g r) c t"),
                            parts[:, u, n]).then_inc(so[u], 16)
                    sp.wait_ge(s_ve, 2 + 2 * c + 2)
                    sp.dma_start(vs[bass.ds(b * GB, GB), :, u * J:(u + 1) * J, :].rearrange("g p j c -> p g (j c)"),
                                 vst[:, u].rearrange("p g j h c -> p g (j h c)")).then_inc(vo[u], 16)

                sweep(sp, chunk, 2)
                for u in range(2):
                    sp.wait_ge(so[u], 64 * (B + 1))
                    sp.wait_ge(vo[u], 16 * (B + 1))
                barrier(sp, 2)

            @block.vector
            def _(v):
                nc.vector.memset(vst[:].rearrange("p u g j h c -> p (u g j h) c")[:, :, HD:VW], 1.0)

                def stats(b, u):
                    c = 2 * b + u
                    v.wait_ge(ld[u], 16 * (b + 1))
                    moments(v, s_sum, c, xin[:, u], stat[:, u], mom[:, u], ve[:, u])

                def normalise(b, u):
                    c = 2 * b + u
                    v.wait_ge(s_pow, c + 1)
                    v.wait_ge(s_tr, 2 * c + 2)
                    for j in range(J):
                        nc.vector.tensor_scalar(xn[:, u, j], xin[:, u, j], mom[:, u, 0, j:j + 1], rstd[:, u, j:j + 1],
                                                ALU.subtract, ALU.mult).then_inc(s_xn, 1)

                def turned_low(b, u):
                    c = 2 * b + u
                    for k in range(KT):
                        v.wait_ge(s_xh, 2 * c + k + 1)
                        nc.vector.tensor_tensor(xnt[:, u, 1, k], bank[k][:], xnt[:, u, 0, k].bitcast(F32),
                                                ALU.subtract).then_inc(s_xt, 1)

                def split(b, u, n):
                    c = 2 * b + u
                    v.wait_ge(s_hi, 4 * c + n + 1)
                    v.wait_ge(s_lo, 4 * c + n + 1)
                    nc.vector.scalar_tensor_tensor(rest[:, n], bank[QKB[n]][:], qkb[:, n // 2, n % 2:n % 2 + 1],
                                                   parts[:, u, n, 0], ALU.add, ALU.subtract).then_inc(s_r, 1)

                def chunk(b, u, more):
                    c = 2 * b + u
                    nb, nu = b + u, 1 - u
                    if more:
                        normalise(nb, nu)
                    split(b, u, 0)
                    split(b, u, 1)
                    if more:
                        turned_low(nb, nu)
                    if again(b):
                        stats(b + 1, u)
                    split(b, u, 2)
                    split(b, u, 3)
                    v.wait_ge(vo[u], 16 * (b + 1))
                    for w in range(2):
                        v.wait_ge(s_vm, 4 + 2 * c + w + 1)
                        for i in range(2):
                            m = nc.vector.tensor_tensor(
                                vst[:, u, :, 2 * w + i, :, 0:HD],
                                bank[VB[w]][:, i * D:(i + 1) * D].rearrange("p (g h d) -> p g h d", g=GB, h=HG),
                                bv_b[:].rearrange("p (g h) d -> p g h d", g=GB), ALU.add)
                        m.then_inc(s_ve, 1)

                stats(0, 0)
                normalise(0, 0)
                stats(0, 1)
                turned_low(0, 0)
                sweep(v, chunk)
                barrier(v, 2)

            @block.gpsimd
            def _(g):
                def power(b, u):
                    c = 2 * b + u
                    g.wait_ge(s_sum, NSUM * (c + 1))
                    g.wait_ge(s_xn, J * c + J)
                    nc.gpsimd.tensor_tensor(rstd[:, u], ve[:, u], mhalf[:], ALU.pow).then_inc(s_pow, 1)

                def low(b, u, n):
                    c = 2 * b + u
                    g.wait_ge(s_m, 4 * c + n + 1)
                    nc.gpsimd.tensor_tensor(parts[:, u, n, 2], rest[:, n], parts[:, u, n, 1],
                                            ALU.subtract).then_inc(s_lo, 1)

                def chunk(b, u, more):
                    low(b, u, 0)
                    low(b, u, 1)
                    if again(b):
                        power(b + 1, u)
                    low(b, u, 2)
                    low(b, u, 3)

                power(0, 0)
                power(0, 1)
                sweep(g, chunk)
                barrier(g, 2)

            @block.scalar
            def _(a):
                def turned(b, u):
                    c = 2 * b + u
                    a.wait_ge(s_vm, 2 * c + 2)
                    for k in range(KT):
                        a.wait_ge(s_tr, 4 + 2 * c + k + 1)
                        nc.scalar.activation(xnt[:, u, 0, k], bank[k][:], ACT.Identity).then_inc(s_xh, 1)

                def high(b, u, n):
                    a.wait_ge(s_qk, 4 * (2 * b + u) + n + 1)
                    nc.scalar.activation(parts[:, u, n, 0], bank[QKB[n]][:], ACT.Identity,
                                         bias=qkb[:, n // 2, n % 2:n % 2 + 1]).then_inc(s_hi, 1)

                def middle(b, u, n):
                    a.wait_ge(s_r, 4 + 4 * (2 * b + u) + n + 1)
                    nc.scalar.activation(parts[:, u, n, 1], rest[:, n], ACT.Identity).then_inc(s_m, 1)

                def chunk(b, u, more):
                    c = 2 * b + u
                    a.wait_ge(so[u], 64 * (b + 1))
                    high(b, u, 0)
                    high(b, u, 1)
                    middle(b, u, 0)
                    if more:
                        turned(b + u, 1 - u)
                    high(b, u, 2)
                    middle(b, u, 1)
                    high(b, u, 3)
                    middle(b, u, 2)
                    middle(b, u, 3)

                turned(0, 0)
                sweep(a, chunk)
                barrier(a, 2)

            @block.tensor
            def _(t):
                def turn(b, u):
                    c = 2 * b + u
                    t.wait_ge(s_xn, 2 * J + J * c + J)
                    for k in range(KT):
                        t.wait_ge(s_xt, 2 * c + k + 1)
                        for j in range(J):
                            m = nc.tensor.transpose(bank[k][:, j * P:(j + 1) * P],
                                                    xn[:, u, j, k * P:(k + 1) * P], ident[:])
                        m.then_inc(s_tr, 1)

                def values(b, u, w):
                    c = 2 * b + u
                    t.wait_ge(s_ve, 2 * c + w + 1)
                    for i in range(2):
                        tok = slice((2 * w + i) * P, (2 * w + i + 1) * P)
                        m = cut_products(bank[VB[w]][:, i * D:(i + 1) * D],
                                         [(xnt[:, u, :, k, tok], wv_t[:, :, k]) for k in range(KT)])
                    m.then_inc(s_vm, 1)

                def chunk(b, u, more):
                    c = 2 * b + u
                    t.wait_ge(s_xt, 2 + 2 * c + 2)
                    for n in range(4):
                        t.wait_ge(s_r, 4 * c + n + 1)
                        w_ = (wq_t, wk_t)[n // 2]
                        m = cut_products(bank[QKB[n]][:],
                                         [(w_[:, :, k, (n % 2) * P:(n % 2 + 1) * P], xnt[:, u, :, k]) for k in range(KT)])
                        m.then_inc(s_qk, 1)
                        if n == 1 and more:
                            turn(b + u, 1 - u)
                    values(b, u, 0)
                    values(b, u, 1)

                turn(0, 0)
                sweep(t, chunk)
                barrier(t, 2)

        def attention(stage, name, causal, ahead, load_qk, n_qk, v_src, m_src, o_dst):
            KW = S if causal else SK
            KP = P if causal else SK
            NKT = S // P if causal else 1
            NPS = 12
            mx_units = []
            for half in range(2):
                for r in range(4):
                    if not causal:
                        mx_units.append((half, half, r, 0, HG, 0, KW, False))
                        continue
                    if half:
                        mx_units += [(half, 1, r, h, 1, 0, 512, False) for h in range(HG)]
                    hb = HG // (r + 1)
                    mx_units += [(half, 2 * half, r, h, hb, half * 512, (r + 1) * P, True)
                                 for h in range(0, HG, hb)]
            n_half = sum(1 for m in mx_units if m[0] == 0)
            st_units, sets = [], []
            for half in range(2):
                kts = range(4 * half + 4) if causal else range(1)
                for kt in kts:
                    diag = causal and kt >= 4 * half
                    q0 = (kt % 4) * P if diag else 0
                    n = 512 - q0
                    hb = max(1, (512 // n) // 2 * 2)
                    first = len(st_units)
                    st_units += [(half, kt, h, hb, q0, n, diag) for h in range(0, HG, hb)]
                    sets.append((half, kt, first, len(st_units), kt == kts[0], kt == kts[-1], q0, n, hb))
            NST = len(st_units)
            half_end = [max(s[3] for s in sets if s[0] == h) for h in range(2)]
            ring = [("m", i) for i in range(len(mx_units))]
            ring.insert(min(n_half + 6, len(ring)), ("t", 0))
            ring.append(("t", 1))
            NMX = len(ring)
            NC = 3 if causal else 2
            LAG = 3
            LATE = 2 if causal else 0

            def reused(u, count, slots):
                last = max(w for w in range(count) if w % slots == u % slots) if u < slots else None
                return slots - count + last + 1 if u < slots else u + 1

            plan, at = [], 0
            for u in range(NST):
                plan.append(("s", u))
                plan += [("p", s) for s, x in enumerate(sets) if x[3] - 1 == u - LAG]
                if u == LATE:
                    plan.append(("r", NMX - 1, ahead - 1))
                upto = max(0, u - LATE + 1) * (NMX - 1) // (NST - LATE)
                plan += [("r", n, ahead) for n in range(at, upto)]
                at = upto
            plan += [("p", s) for s, x in enumerate(sets) if x[3] - 1 > NST - 1 - LAG]
            with ExitStack() as st:
                scope[0] = st
                stq = sb(name + "stq", [P, GB, 2, HG, 512], BF16)
                stk = sb(name + "stk", [P, GB, HG, KW], BF16)
                va = sb(name + "va", [KP, GB, NKT, HG * VW])
                prob = sb(name + "prob", [KP, NPS, 512])
                u_ = sb(name + "u", [P, 2, S])
                pm = sb(name + "pm", [P, 3, HG, 4])
                mxv = sb(name + "mxv", [P, HG * 4])
                mt = sb(name + "mt", [P, 2, 2, HG * 4], BF16)
                mrow = sb(name + "mrow", [2 * HG * 4, 2, 2, P], BF16)
                mk = None if causal else sb(name + "mk", [SK, GB, S], BF16)

                ld = [sem(f"{name}ld{i}") for i in range(GB)]
                s_set = sem(name + "s_set")
                s_mxf = sem(name + "s_mxf")
                s_mxe = sem(name + "s_mxe")
                s_cmb = sem(name + "s_cmb")
                s_mt = sem(name + "s_mt")
                md = [[sem(f"{name}md{i}{c}") for c in range(2)] for i in range(2)]
                s_st = sem(name + "s_st")
                s_ex = sem(name + "s_ex")
                s_pv = sem(name + "s_pv")
                s_u = sem(name + "s_u")
                us = [sem(f"{name}us{i}") for i in range(2)]
                NLD = n_qk + 1 + (0 if causal else 1)

                block = st.enter_context(nc.Block())

                def steps(eng, step):
                    with eng.Fori(0, B - 1) as b:
                        for i in range(GB):
                            step(b, i, GB)
                    for i in range(GB):
                        step(B - 1, i, GB - 1 - i)

                def after(b, i, n):
                    return b + (i + n) // GB, (i + n) % GB

                @block.sync
                def _(sp):
                    sp.sem_inc(s_mxe, 3)
                    sp.sem_inc(s_ex, 3)
                    sp.sem_inc(s_pv, NPS)
                    sp.sem_inc(s_u, 2)
                    for i in range(2):
                        sp.sem_inc(us[i], 16)

                    def load(b, i):
                        g = b * GB + i
                        load_qk(sp, g, stq[:, i], stk[:, i], ld[i])
                        sp.dma_start(va[:, i], v_src[bass.ds(g, 1)].rearrange("a p n c -> (a p) n c")).then_inc(ld[i], 16)
                        if m_src is not None:
                            sp.dma_start(mk[:, i], m_src[bass.ds(g, 1)].rearrange("a k t -> (a k) t")).then_inc(ld[i], 16)

                    def maxima(b, i, c):
                        sp.wait_ge(s_mxe, 3 + (b * GB + i) * NMX + ring.index(("t", c)) + 1)
                        for t in range(2):
                            sp.dma_start(stq[R + t:R + t + 1, i, c].rearrange("a h q -> a (h q)"),
                                         mrow[16 * t:16 * (t + 1), i % 2, c]).then_inc(md[i % 2][c], 16)

                    for i in range(GB - 1):
                        load(0, i)
                    for i in range(ahead):
                        maxima(0, i, 0)
                        if i < ahead - 1:
                            maxima(0, i, 1)

                    def step(b, i, left):
                        g = b * GB + i
                        if left >= ahead - 1:
                            maxima(*after(b, i, ahead - 1), 1)
                        if left >= GB - 1:
                            sp.wait_ge(s_pv, NPS + g * NST)
                            load(*after(b, i, GB - 1))
                        if left >= ahead:
                            maxima(*after(b, i, ahead), 0)
                        sp.wait_ge(s_u, 2 + 2 * g + 2)
                        sp.dma_start(o_dst[bass.ds(g, 1)].rearrange("a h w r t -> (a h w r) t"),
                                     u_[:, i % 2]).then_inc(us[i % 2], 16)

                    steps(sp, step)
                    for i in range(2):
                        sp.wait_ge(us[i], 16 * (G // 2 + 1))
                    barrier(sp, stage)

                @block.gpsimd
                def _(g):
                    barrier(g, stage)

                @block.vector
                def _(v):
                    nc.vector.memset(stk[R:RM], -1.0).then_inc(s_set, 1)

                    def item(b, i, n):
                        g = b * GB + i
                        kind, m = ring[n]
                        src = bank[MX_BANKS[n % 3]]
                        v.wait_ge(s_mxf, g * NMX + n + 1)
                        if kind == "t":
                            nc.vector.tensor_copy(mrow[:, i % 2, m], src[0:32, 0:P // 2].bitcast(BF16)).then_inc(s_mxe, 1)
                            return
                        half, k, r, h0, hb, _, w, _ = mx_units[m]
                        nc.vector.tensor_reduce(pm[:, k, h0:h0 + hb, r],
                                                src[:, 0:hb * w].rearrange("p (h w) -> p h w", h=hb),
                                                AX, ALU.max).then_inc(s_mxe, 1)
                        if m == n_half - 1 or m == len(mx_units) - 1:
                            parts_of_max(g, half, n)

                    def parts_of_max(g, c, n):
                        v.wait_ge(s_mxe, 3 + g * NMX + n + 1)
                        m = pm[:, c].rearrange("p h r -> p (h r)")
                        if causal and c:
                            nc.vector.tensor_tensor(mxv[:], m, pm[:, 2].rearrange("p h r -> p (h r)"),
                                                    ALU.max).then_inc(s_cmb, 1)
                            v.wait_ge(s_cmb, NC * g + 2)
                            m = mxv[:]
                        nc.vector.tensor_copy(mt[:, c, 0], m).then_inc(s_cmb, 1)
                        v.wait_ge(s_cmb, NC * g + (NC if c else 1))
                        nc.vector.tensor_tensor(mt[:, c, 1], m, mt[:, c, 0], ALU.subtract).then_inc(s_mt, 1)

                    def step(b, i, left):
                        if left >= ahead - 1:
                            item(*after(b, i, ahead - 1), NMX - 1)
                        if left >= ahead:
                            for n in range(NMX - 1):
                                item(*after(b, i, ahead), n)

                    for n in range(ahead * NMX - 1):
                        item(0, n // NMX, n % NMX)
                    steps(v, step)
                    barrier(v, stage)

                @block.scalar
                def _(a):
                    def outputs(b, i, c):
                        g = b * GB + i
                        if c == 0:
                            a.wait_ge(us[i % 2], 16 * (2 * b + i // 2 + 1))
                        a.wait_ge(s_pv, NPS + g * NST + half_end[c])
                        nc.scalar.activation(u_[:, i % 2, c * 512:(c + 1) * 512], bank[PV_BANKS[c]][:],
                                             ACT.Identity).then_inc(s_u, 1)

                    def step(b, i, left):
                        g = b * GB + i
                        for u, (half, kt, h0, hb, q0, n, diag) in enumerate(st_units):
                            a.wait_ge(s_st, g * NST + u + 1)
                            a.wait_ge(s_pv, g * NST + reused(u, NST, NPS))
                            nc.scalar.activation(prob[:, u % NPS, 0:hb * n], bank[ST_BANKS[u % 3]][0:KP, 0:hb * n],
                                                 ACT.Exp).then_inc(s_ex, 1)
                            if u == min(half_end[0] + LAG + 2, NST - 2):
                                outputs(b, i, 0)
                        outputs(b, i, 1)

                    steps(a, step)
                    barrier(a, stage)

                @block.tensor
                def _(t):
                    def item(b, i, n):
                        g = b * GB + i
                        kind, m = ring[n]
                        dst = bank[MX_BANKS[n % 3]]
                        if n == 0:
                            t.wait_ge(ld[i], 16 * NLD * (b + 1))
                        t.wait_ge(s_mxe, g * NMX + reused(n, NMX, 3))
                        if kind == "t":
                            t.wait_ge(s_mt, 2 * g + m + 1)
                            nc.tensor.transpose(dst[0:32, 0:P // 2].bitcast(BF16),
                                                mt[:, m].rearrange("p t m -> p (t m)"), identb[:]).then_inc(s_mxf, 1)
                            return
                        half, k, r, h0, hb, k0, w, diag = mx_units[m]
                        qt = 4 * half + r
                        for h in range(hb):
                            mm = nc.tensor.matmul(dst[:, h * w:(h + 1) * w],
                                                  stq[0:R, i, half, h0 + h, r * P:(r + 1) * P],
                                                  stk[0:R, i, h0 + h, k0:k0 + w],
                                                  start=(h == 0), stop=(causal and not diag), skip_group_check=True)
                        if not causal:
                            mm = nc.tensor.matmul(dst[:, 0:hb * w], mk[:, i, qt * P:(qt + 1) * P],
                                                  negid[:].rearrange("k h l -> k (h l)"),
                                                  start=False, stop=True, skip_group_check=True)
                        elif diag:
                            mm = nc.tensor.matmul(dst[:, 0:hb * w].rearrange("p (h w) -> p h w", h=hb)[:, :, w - P:w],
                                                  identb[:], tri_q[:, 0:hb], start=False, stop=True,
                                                  skip_group_check=True)
                        mm.then_inc(s_mxf, 1)

                    def scores(b, i, u):
                        g = b * GB + i
                        half, kt, h0, hb, q0, n, diag = st_units[u]
                        if u == 0 or u == half_end[0]:
                            t.wait_ge(md[i % 2][half], 32 * (2 * b + i // 2 + 1))
                        t.wait_ge(s_ex, g * NST + reused(u, NST, 3))
                        dst = bank[ST_BANKS[u % 3]]
                        q = half * 512 + q0
                        for h in range(hb):
                            mm = nc.tensor.matmul(dst[0:KP, h * n:(h + 1) * n],
                                                  stk[0:RM, i, h0 + h, kt * KP:(kt + 1) * KP],
                                                  stq[0:RM, i, half, h0 + h, q0:q0 + n],
                                                  start=(h == 0), stop=(causal and not diag), skip_group_check=True)
                        if not causal:
                            mm = nc.tensor.matmul(dst[0:KP, 0:n], negid[:, 0], mk[:, i, q:q + n],
                                                  start=False, stop=True, skip_group_check=True)
                        elif diag:
                            mm = nc.tensor.matmul(dst[:, 0:hb * n].rearrange("p (h n) -> p h n", h=hb)[:, :, 0:P],
                                                  identb[:], tri_k[:, 0:hb], start=False, stop=True,
                                                  skip_group_check=True)
                        mm.then_inc(s_st, 1)

                    def products(b, i, s):
                        g = b * GB + i
                        half, kt, first, end, fresh, last, q0, n, hb = sets[s]
                        if fresh:
                            t.wait_ge(s_u, 2 * g + half + 1)
                        t.wait_ge(s_ex, 3 + g * NST + end)
                        for h in range(HG):
                            mm = nc.tensor.matmul(bank[PV_BANKS[half]][h * VW:(h + 1) * VW, q0:512],
                                                  va[:, i, kt, h * VW:(h + 1) * VW],
                                                  prob[:, (first + h // hb) % NPS, (h % hb) * n:(h % hb + 1) * n],
                                                  start=fresh, stop=last)
                            if h % hb == hb - 1:
                                mm.then_inc(s_pv, 1)

                    def step(b, i, left):
                        for what in plan:
                            if what[0] == "s":
                                scores(b, i, what[1])
                            elif what[0] == "p":
                                products(b, i, what[1])
                            elif left >= what[2]:
                                item(*after(b, i, what[2]), what[1])

                    t.wait_ge(s_set, 1)
                    for n in range(ahead * NMX - 1):
                        item(0, n // NMX, n % NMX)
                    steps(t, step)
                    barrier(t, stage)

        def load_self(sp, g, stq, stk, ld):
            for slot, part in enumerate(Q_PARTS):
                for c in range(2):
                    sp.dma_start(stq[HD * slot:HD * (slot + 1), c],
                                 qk3[0, part, bass.ds(g, 1), :, c * 512:(c + 1) * 512]
                                 .rearrange("a (h r) t -> (a r) h t", h=HG)).then_inc(ld, 16)
            for slot, part in enumerate(K_PARTS):
                sp.dma_start(stk[HD * slot:HD * (slot + 1)],
                             qk3[1, part, bass.ds(g, 1)].rearrange("a (h r) t -> (a r) h t", h=HG)).then_inc(ld, 16)

        def load_cross(sp, g, stq, stk, ld):
            for c in range(2):
                sp.dma_start(stq[0:R, c], xqs[:, bass.ds(g * HG, HG), c * 512:(c + 1) * 512]).then_inc(ld, 16)
            sp.dma_start(stk[0:R], xks[:, bass.ds(g * HG, HG)]).then_inc(ld, 16)

        attention(3, "self_", True, 1, load_self, 2 * len(Q_PARTS) + len(K_PARTS), vs, None, od)

        def chunk_loads(sp, o_src, r_src, b, u, oin, din, ld):
            for k in range(KT):
                sp.dma_start(oin[:, u, k], o_src[bass.ds(b * GB + 2 * k, 2), :, 0, :, u * CH:(u + 1) * CH]
                             .rearrange("g h r t -> (g h) r t")).then_inc(ld, 16)
                sp.dma_start(din[:, u, k], r_src[bass.ds(b * H + HP * k, HP), None, u * CH:(u + 1) * CH]
                             .to_broadcast([HP, HD, CH])).then_inc(ld, 16)

        with ExitStack() as st:
            scope[0] = st
            oin = sb("c_oin", [P, 2, KT, CH])
            din = sb("c_din", [P, 2, KT, CH])
            den = sb("c_den", [P, CH])
            xin = sb("c_xin", [P, 2, J, D])
            min_ = sb("c_min", [P, 2, J, S2], U8)
            x1 = sb("c_x1", [P, 2, J, D])
            stat = sb("c_stat", [P, 2, J, 6])
            mom = sb("c_mom", [P, 2, 6, J])
            ve = sb("c_ve", [P, 2, J])
            rstd = sb("c_rstd", [P, 2, J])
            allm = sb("c_allm", [P, 2, J])
            live = sb("c_live", [P, 2, J])
            meff = sb("c_meff", [P, 2, J, SK], BF16)
            xn = sb("c_xn", [P, 2, J, D])
            xnt = sb("c_xnt", [P, 2, KT, CH])
            parts = sb("c_parts", [P, 2, KT, 3, CH], BF16)
            rest = sb("c_rest", [P, KT, CH])
            mtr = sb("c_mtr", [SK, 2, CH], BF16)

            ld = [sem(f"c_ld{u}") for u in range(2)]
            s_den = sem("c_den_")
            s_rd = sem("c_rd")
            s_on = sem("c_on")
            s_xb = sem("c_xb")
            s_op = sem("c_op")
            s_x1 = sem("c_x1_")
            x1o = [sem(f"c_x1o{u}") for u in range(2)]
            s_sum = sem("c_sum")
            s_pow = sem("c_pow")
            s_all = sem("c_all")
            s_sc = sem("c_sc")
            s_me = sem("c_me")
            s_xn = sem("c_xn_")
            s_mtp = sem("c_mtp")
            s_mts = sem("c_mts")
            mo = [sem(f"c_mo{u}") for u in range(2)]
            s_tr = sem("c_tr")
            s_xt = sem("c_xt")
            s_q = sem("c_q")
            s_hi = sem("c_hi")
            s_r = sem("c_r")
            s_m = sem("c_m")
            s_lo = sem("c_lo")
            so = [[sem(f"c_so{n}{u}") for u in range(2)] for n in range(KT)]
            OB, TB, QB, MB = (0, 1), (2, 3), (4, 5), 6
            NSO = 16 * len(Q_PARTS)

            block = st.enter_context(nc.Block())

            def store_queries(eng, b, u, n):
                c = 2 * b + u
                eng.wait_ge(s_lo, 2 + 2 * c + n + 1)
                for slot, part in enumerate(Q_PARTS):
                    eng.dma_start(xqs[HD * slot:HD * (slot + 1), bass.ds(b * H + HP * n, HP), u * CH:(u + 1) * CH]
                                  .rearrange("r h t -> h r t"), parts[:, u, n, part]).then_inc(so[n][u], 16)

            @block.sync
            def _(sp):
                for s_, n in ((s_on, 2), (s_op, 4), (s_x1, 2), (s_me, 4), (s_xn, 8), (s_mtp, 2), (s_mts, 1),
                              (s_tr, 4), (s_xt, 2), (s_q, 4), (s_r, 2), (s_lo, 2)):
                    sp.sem_inc(s_, n)
                for u in range(2):
                    sp.sem_inc(x1o[u], 16)
                    sp.sem_inc(mo[u], 64)
                    for n in range(KT):
                        sp.sem_inc(so[n][u], NSO)

                def load(b, u):
                    c = 2 * b + u
                    chunk_loads(sp, od, rdn, b, u, oin, din, ld[u])
                    sp.dma_start(xin[:, u], xv[bass.ds(c, 1)].rearrange("a p j d -> (a p) j d")).then_inc(ld[u], 16)
                    sp.dma_start(min_[:, u], mv[bass.ds(c, 1)].rearrange("a p j k -> (a p) j k")).then_inc(ld[u], 16)

                def used(b, u):
                    c = 2 * b + u
                    sp.wait_ge(s_x1, 2 + 2 * c + 2)
                    sp.wait_ge(s_me, 4 + 4 * c + 4)

                sp.dma_start(den[:], od[:, :, 1, 0].rearrange("g h (c t) -> (g h) c t", c=2)).then_inc(s_den, 16)
                sp.wait_ge(s_rd, 1)
                sp.dma_start(rdn.rearrange("h (c t) -> (h c) t", c=2), den[:]).then_inc(s_den, 16)
                sp.wait_ge(s_den, 32)
                load(0, 0)
                load(0, 1)

                def chunk(b, u, more):
                    c = 2 * b + u
                    if not isinstance(b, int) or c + 3 < NCH:
                        used(b + u, 1 - u)
                        load(b + u + 1, 1 - u)
                    sp.wait_ge(s_x1, 2 + 2 * c + 2)
                    sp.dma_start(x1s[bass.ds(c, 1)].rearrange("a p j d -> (a p) j d"), x1[:, u]).then_inc(x1o[u], 16)
                    sp.wait_ge(s_mts, 1 + c + 1)
                    sp.dma_start(mts[bass.ds(b * GB, GB), :, u * CH:(u + 1) * CH].rearrange("g k t -> k g t"),
                                 mtr[:, u:u + 1].to_broadcast([SK, GB, CH])).then_inc(mo[u], 64)
                    store_queries(sp, b, u, 0)

                used(0, 0)
                load(1, 0)
                sweep(sp, chunk, 2)
                for u in range(2):
                    sp.wait_ge(x1o[u], 16 * (B + 1))
                    sp.wait_ge(mo[u], 64 * (B + 1))
                    for n in range(KT):
                        sp.wait_ge(so[n][u], NSO * (B + 1))
                barrier(sp, 4)

            @block.gpsimd
            def _(g):
                def bias(b, u):
                    c = 2 * b + u
                    g.wait_ge(ld[u], 96 * (b + 1))
                    nc.gpsimd.tensor_tensor(xin[:, u], xin[:, u], bo_b[:, None, :].to_broadcast([P, J, D]),
                                            ALU.add).then_inc(s_xb, 1)

                def power(b, u):
                    c = 2 * b + u
                    g.wait_ge(s_sum, NSUM * (c + 1))
                    g.wait_ge(s_xn, J * c + J)
                    nc.gpsimd.tensor_tensor(rstd[:, u], ve[:, u], mhalf[:], ALU.pow).then_inc(s_pow, 1)

                def low(b, u, n):
                    c = 2 * b + u
                    g.wait_ge(s_m, 2 * c + n + 1)
                    nc.gpsimd.tensor_tensor(parts[:, u, n, 2], rest[:, n], parts[:, u, n, 1],
                                            ALU.subtract).then_inc(s_lo, 1)

                def chunk(b, u, more):
                    if again(b):
                        bias(b + 1, u)
                    low(b, u, 0)
                    low(b, u, 1)
                    if again(b):
                        power(b + 1, u)

                bias(0, 0)
                bias(0, 1)
                power(0, 0)
                power(0, 1)
                sweep(g, chunk)
                barrier(g, 4)

            @block.vector
            def _(v):
                for u in range(2):
                    nc.vector.memset(meff[:, u, :, S2:SK], 1.0)
                v.wait_ge(s_den, 16)
                nc.vector.reciprocal(den[:], den[:]).then_inc(s_rd, 1)

                def quotients(b, u):
                    c = 2 * b + u
                    v.wait_ge(ld[u], 96 * (b + 1))
                    nc.vector.tensor_tensor(oin[:, u], oin[:, u], din[:, u], ALU.mult).then_inc(s_on, 1)

                def masks(b, u):
                    c = 2 * b + u
                    v.wait_ge(ld[u], 96 * (b + 1))
                    v.wait_ge(s_mtp, c + 1)
                    nc.vector.tensor_reduce(allm[:, u], min_[:, u], AX, ALU.min).then_inc(s_all, 1)
                    v.wait_ge(s_all, 2 * c + 1)
                    nc.vector.tensor_scalar(live[:, u], allm[:, u], -1.0, 1.0, ALU.mult, ALU.add).then_inc(s_all, 1)
                    v.wait_ge(s_all, 2 * c + 2)
                    for j in range(J):
                        nc.vector.tensor_scalar(meff[:, u, j, 0:S2], min_[:, u, j], live[:, u, j:j + 1], None,
                                                ALU.mult).then_inc(s_me, 1)

                def sums(b, u):
                    c = 2 * b + u
                    v.wait_ge(s_xb, c + 1)
                    v.wait_ge(x1o[u], 16 * (b + 1))
                    for w in range(2):
                        v.wait_ge(s_op, 4 + 2 * c + w + 1)
                        nc.vector.tensor_tensor(x1[:, u, 2 * w:2 * w + 2].rearrange("p j d -> p (j d)"), bank[OB[w]][:],
                                                xin[:, u, 2 * w:2 * w + 2].rearrange("p j d -> p (j d)"),
                                                ALU.add).then_inc(s_x1, 1)
                    v.wait_ge(s_x1, 2 + 2 * c + 2)
                    moments(v, s_sum, c, x1[:, u], stat[:, u], mom[:, u], ve[:, u])

                def normalise(b, u):
                    c = 2 * b + u
                    v.wait_ge(s_pow, c + 1)
                    nc.vector.tensor_tensor(rstd[:, u], rstd[:, u], live[:, u], ALU.mult).then_inc(s_sc, 1)
                    v.wait_ge(s_sc, c + 1)
                    v.wait_ge(s_tr, 2 * c + 2)
                    for j in range(J):
                        nc.vector.tensor_scalar(xn[:, u, j], x1[:, u, j], mom[:, u, 0, j:j + 1], rstd[:, u, j:j + 1],
                                                ALU.subtract, ALU.mult).then_inc(s_xn, 1)

                def split(b, u, n):
                    c = 2 * b + u
                    v.wait_ge(s_hi, 2 * c + n + 1)
                    v.wait_ge(s_lo, 2 * c + n + 1)
                    nc.vector.scalar_tensor_tensor(rest[:, n], bank[QB[n]][:], SCALE,
                                                   parts[:, u, n, 0], ALU.mult, ALU.subtract).then_inc(s_r, 1)
                    v.wait_ge(s_r, 2 + 2 * c + n + 1)
                    nc.vector.tensor_copy(parts[:, u, n, 1], rest[:, n]).then_inc(s_m, 1)

                def chunk(b, u, more):
                    if again(b):
                        quotients(b + 1, u)
                    if more:
                        normalise(b + u, 1 - u)
                    split(b, u, 0)
                    split(b, u, 1)
                    if again(b):
                        sums(b + 1, u)
                        masks(b + 1, u)

                quotients(0, 0)
                quotients(0, 1)
                sums(0, 0)
                masks(0, 0)
                normalise(0, 0)
                sums(0, 1)
                masks(0, 1)
                sweep(v, chunk)
                barrier(v, 4)

            @block.scalar
            def _(a):
                def turned(b, u):
                    c = 2 * b + u
                    a.wait_ge(s_q, 2 * c + 2)
                    for k in range(KT):
                        a.wait_ge(s_tr, 4 + 2 * c + k + 1)
                        nc.scalar.activation(xnt[:, u, k], bank[TB[k]][:], ACT.Identity).then_inc(s_xt, 1)
                    a.wait_ge(s_mtp, 2 + c + 1)
                    a.wait_ge(mo[u], 64 * (b + 1))
                    nc.scalar.activation(mtr[:, u], bank[MB][0:SK, 0:CH // 2].bitcast(BF16), ACT.Identity).then_inc(s_mts, 1)

                def chunk(b, u, more):
                    c = 2 * b + u
                    for n in range(KT):
                        a.wait_ge(so[n][u], NSO * (b + 1))
                        a.wait_ge(s_q, 4 + 2 * c + n + 1)
                        nc.scalar.activation(parts[:, u, n, 0], bank[QB[n]][:], ACT.Identity, scale=SCALE).then_inc(s_hi, 1)
                    if more:
                        turned(b + u, 1 - u)
                    store_queries(a, b, u, 1)

                turned(0, 0)
                sweep(a, chunk)
                barrier(a, 4)

            @block.tensor
            def _(t):
                def project(b, u):
                    c = 2 * b + u
                    t.wait_ge(s_on, 2 + c + 1)
                    for w in range(2):
                        t.wait_ge(s_x1, 2 * c + w + 1)
                        for i in range(2):
                            for k in range(KT):
                                mm = nc.tensor.matmul(bank[OB[w]][:, i * D:(i + 1) * D],
                                                      oin[:, u, k, (2 * w + i) * P:(2 * w + i + 1) * P], wo_t[:, k],
                                                      start=(k == 0), stop=(k == KT - 1))
                        mm.then_inc(s_op, 1)

                def turn(b, u):
                    c = 2 * b + u
                    t.wait_ge(s_xn, 8 + 4 * c + 4)
                    for k in range(KT):
                        t.wait_ge(s_xt, 2 * c + k + 1)
                        for j in range(J):
                            mm = nc.tensor.transpose(bank[TB[k]][:, j * P:(j + 1) * P],
                                                     xn[:, u, j, k * P:(k + 1) * P], ident[:])
                        mm.then_inc(s_tr, 1)
                    t.wait_ge(s_me, 4 + 4 * c + 4)
                    t.wait_ge(s_mts, c + 1)
                    for j in range(J):
                        mm = nc.tensor.transpose(bank[MB][0:SK, j * P // 2:(j + 1) * P // 2].bitcast(BF16),
                                                 meff[:, u, j], identb[:])
                    mm.then_inc(s_mtp, 1)

                def chunk(b, u, more):
                    c = 2 * b + u
                    t.wait_ge(s_xt, 2 + 2 * c + 2)
                    for n in range(KT):
                        t.wait_ge(s_r, 2 * c + n + 1)
                        for k in range(KT):
                            mm = nc.tensor.matmul(bank[QB[n]][:], xwq[:, k, n * P:(n + 1) * P], xnt[:, u, k],
                                                  start=(k == 0), stop=(k == KT - 1))
                        mm.then_inc(s_q, 1)
                    if again(b):
                        project(b + 1, u)
                    if more:
                        turn(b + u, 1 - u)

                project(0, 0)
                project(0, 1)
                turn(0, 0)
                sweep(t, chunk)
                barrier(t, 4)

        attention(5, "cross_", False, 2, load_cross, 3, xvs, mts, od2)

        with ExitStack() as st:
            scope[0] = st
            oin = sb("e_oin", [P, 2, KT, CH])
            din = sb("e_din", [P, 2, KT, CH])
            den = sb("e_den", [P, CH])
            xin = sb("e_xin", [P, 2, J, D])
            x2 = sb("e_x2", [P, 2, J, D])
            yo = sb("e_yo", [P, 2, J, D])
            stat = sb("e_stat", [P, 2, J, 6])
            mom = sb("e_mom", [P, 2, 6, J])
            ve = sb("e_ve", [P, 2, J])
            rstd = sb("e_rstd", [P, 2, J])
            xn = sb("e_xn", [P, 2, J, D])
            xnt = sb("e_xnt", [P, 2, 2, KT, CH], F32R)
            sg = sb("e_sg", [P, 2, CH])
            hf = sb("e_hf", [P, 2, CH])
            ht = sb("e_ht", [P, 2, 2, HT, CH], F32R)

            ld = [sem(f"e_ld{u}") for u in range(2)]
            s_den = sem("e_den_")
            s_rd = sem("e_rd")
            s_on = sem("e_on")
            s_op = sem("e_op")
            s_x2 = sem("e_x2_")
            s_sum = sem("e_sum")
            s_pow = sem("e_pow")
            s_xn = sem("e_xn_")
            s_tr = sem("e_tr")
            s_xh = sem("e_xh")
            s_xt = sem("e_xt")
            s_gu = sem("e_gu")
            s_sg = sem("e_sg_")
            s_h = sem("e_h")
            s_hh = sem("e_hh")
            s_hl = sem("e_hl")
            s_y = sem("e_y")
            s_yo = sem("e_yo_")
            yd = [sem(f"e_yd{u}") for u in range(2)]
            OB, TB = (0, 1), (2, 3)

            block = st.enter_context(nc.Block())

            @block.sync
            def _(sp):
                for s_, n in ((s_on, 2), (s_op, 4), (s_xn, 8), (s_tr, 4), (s_xt, 2), (s_gu, 12), (s_sg, 2),
                              (s_h, 2), (s_hl, 2), (s_y, 4), (s_yo, 4)):
                    sp.sem_inc(s_, n)
                for u in range(2):
                    sp.sem_inc(yd[u], 16)

                def load(b, u):
                    c = 2 * b + u
                    chunk_loads(sp, od2, rdn2, b, u, oin, din, ld[u])
                    sp.dma_start(xin[:, u], x1s[bass.ds(c, 1)].rearrange("a p j d -> (a p) j d")).then_inc(ld[u], 16)

                sp.dma_start(den[:], od2[:, :, 1, 0].rearrange("g h (c t) -> (g h) c t", c=2)).then_inc(s_den, 16)
                sp.wait_ge(s_rd, 1)
                sp.dma_start(rdn2.rearrange("h (c t) -> (h c) t", c=2), den[:]).then_inc(s_den, 16)
                sp.wait_ge(s_den, 32)
                load(0, 0)
                load(0, 1)

                def chunk(b, u, more):
                    c = 2 * b + u
                    if again(b):
                        sp.wait_ge(s_x2, 2 * c + 2)
                        load(b + 1, u)
                    sp.wait_ge(s_yo, 4 + 2 * c + 2)
                    sp.dma_start(ov[bass.ds(c, 1)].rearrange("a p j d -> (a p) j d"), yo[:, u]).then_inc(yd[u], 16)

                sweep(sp, chunk)
                for u in range(2):
                    sp.wait_ge(yd[u], 16 * (B + 1))
                barrier(sp, 6)

            @block.gpsimd
            def _(g):
                def quotients(b, u):
                    c = 2 * b + u
                    g.wait_ge(ld[u], 80 * (b + 1))
                    nc.gpsimd.tensor_tensor(oin[:, u], oin[:, u], din[:, u], ALU.mult).then_inc(s_on, 1)

                def power(b, u):
                    c = 2 * b + u
                    g.wait_ge(s_sum, NSUM * (c + 1))
                    g.wait_ge(s_xn, J * c + J)
                    nc.gpsimd.tensor_tensor(rstd[:, u], ve[:, u], mhalf[:], ALU.pow).then_inc(s_pow, 1)

                def hidden_low(b, u, h):
                    c = 2 * b + u
                    g.wait_ge(s_hh, HT * c + h + 1)
                    nc.gpsimd.tensor_tensor(ht[:, u, 1, h], hf[:, h % 2], ht[:, u, 0, h].bitcast(F32),
                                            ALU.subtract).then_inc(s_hl, 1)

                def chunk(b, u, more):
                    if more:
                        power(b + u, 1 - u)
                    hidden_low(b, u, 2)
                    hidden_low(b, u, 3)
                    hidden_low(b, u, 4)
                    if again(b):
                        quotients(b + 1, u)
                    hidden_low(b, u, 5)
                    if more:
                        hidden_low(b + u, 1 - u, 0)
                        hidden_low(b + u, 1 - u, 1)

                quotients(0, 0)
                quotients(0, 1)
                power(0, 0)
                hidden_low(0, 0, 0)
                hidden_low(0, 0, 1)
                sweep(g, chunk)
                barrier(g, 6)

            @block.vector
            def _(v):
                def sums(b, u):
                    c = 2 * b + u
                    for w in range(2):
                        v.wait_ge(s_op, 4 + 2 * c + w + 1)
                        nc.vector.tensor_tensor(x2[:, u, 2 * w:2 * w + 2].rearrange("p j d -> p (j d)"), bank[OB[w]][:],
                                                xin[:, u, 2 * w:2 * w + 2].rearrange("p j d -> p (j d)"),
                                                ALU.add).then_inc(s_x2, 1)

                def row_stats(b, u, part):
                    c = 2 * b + u
                    if part == 0:
                        v.wait_ge(s_x2, 2 * c + 2)
                    moments(v, s_sum, c, x2[:, u], stat[:, u], mom[:, u], ve[:, u], (part,))

                def normalise(b, u):
                    c = 2 * b + u
                    v.wait_ge(s_pow, c + 1)
                    v.wait_ge(s_tr, 2 * c + 2)
                    for j in range(J):
                        nc.vector.tensor_scalar(xn[:, u, j], x2[:, u, j], mom[:, u, 0, j:j + 1], rstd[:, u, j:j + 1],
                                                ALU.subtract, ALU.mult).then_inc(s_xn, 1)

                def hidden(b, u, h):
                    c = 2 * b + u
                    if h == 0:
                        v.wait_ge(s_y, 2 * c + 2)
                    v.wait_ge(s_sg, 2 + HT * c + h + 1)
                    v.wait_ge(s_hl, HT * c + h + 1)
                    nc.vector.tensor_tensor(hf[:, h % 2], bank[5 + 2 * (h % 2)][:], sg[:, h % 2], ALU.mult).then_inc(s_h, 1)
                    v.wait_ge(s_h, 2 + HT * c + h + 1)
                    nc.vector.tensor_copy(ht[:, u, 0, h], hf[:, h % 2]).then_inc(s_hh, 1)

                def turned_low(b, u):
                    c = 2 * b + u
                    for k in range(KT):
                        v.wait_ge(s_xh, 2 * c + k + 1)
                        nc.vector.tensor_tensor(xnt[:, u, 1, k], bank[TB[k]][:], xnt[:, u, 0, k].bitcast(F32),
                                                ALU.subtract).then_inc(s_xt, 1)

                def chunk(b, u, more):
                    c = 2 * b + u
                    nb, nu = b + u, 1 - u
                    if more:
                        sums(nb, nu)
                        row_stats(nb, nu, 0)
                        row_stats(nb, nu, 1)
                    hidden(b, u, 2)
                    hidden(b, u, 3)
                    if more:
                        normalise(nb, nu)
                    hidden(b, u, 4)
                    if more:
                        turned_low(nb, nu)
                    hidden(b, u, 5)
                    if more:
                        hidden(nb, nu, 0)
                        hidden(nb, nu, 1)
                    v.wait_ge(yd[u], 16 * (b + 1))
                    for w in range(2):
                        v.wait_ge(s_y, 4 + 2 * c + w + 1)
                        nc.vector.tensor_tensor(yo[:, u, 2 * w:2 * w + 2].rearrange("p j d -> p (j d)"), bank[OB[w]][:],
                                                x2[:, u, 2 * w:2 * w + 2].rearrange("p j d -> p (j d)"),
                                                ALU.add).then_inc(s_yo, 1)

                v.wait_ge(s_den, 16)
                nc.vector.reciprocal(den[:], den[:]).then_inc(s_rd, 1)
                sums(0, 0)
                row_stats(0, 0, 0)
                row_stats(0, 0, 1)
                normalise(0, 0)
                turned_low(0, 0)
                hidden(0, 0, 0)
                hidden(0, 0, 1)
                sweep(v, chunk)
                barrier(v, 6)

            @block.scalar
            def _(a):
                def turned(b, u):
                    c = 2 * b + u
                    a.wait_ge(s_gu, HT * c + HT)
                    for k in range(KT):
                        a.wait_ge(s_tr, 4 + 2 * c + k + 1)
                        nc.scalar.activation(xnt[:, u, 0, k], bank[TB[k]][:], ACT.Identity).then_inc(s_xh, 1)

                def silu(b, u, h):
                    c = 2 * b + u
                    a.wait_ge(s_gu, 2 * HT + HT * c + h + 1)
                    a.wait_ge(s_h, HT * c + h + 1)
                    nc.scalar.activation(sg[:, h % 2], bank[4 + 2 * (h % 2)][:], ACT.Silu).then_inc(s_sg, 1)

                def chunk(b, u, more):
                    for h in range(2, HT - 1):
                        silu(b, u, h)
                    if more:
                        turned(b + u, 1 - u)
                    silu(b, u, HT - 1)
                    if more:
                        silu(b + u, 1 - u, 0)
                        silu(b + u, 1 - u, 1)

                turned(0, 0)
                silu(0, 0, 0)
                silu(0, 0, 1)
                sweep(a, chunk)
                barrier(a, 6)

            @block.tensor
            def _(t):
                def project(b, u):
                    c = 2 * b + u
                    t.wait_ge(s_on, 2 + c + 1)
                    for w in range(2):
                        t.wait_ge(s_yo, 2 * c + w + 1)
                        for i in range(2):
                            for k in range(KT):
                                mm = nc.tensor.matmul(bank[OB[w]][:, i * D:(i + 1) * D],
                                                      oin[:, u, k, (2 * w + i) * P:(2 * w + i + 1) * P], xwo[:, k],
                                                      start=(k == 0), stop=(k == KT - 1))
                        mm.then_inc(s_op, 1)

                def turn(b, u):
                    c = 2 * b + u
                    t.wait_ge(s_xn, 8 + 4 * c + 4)
                    for k in range(KT):
                        t.wait_ge(s_xt, 2 * c + k + 1)
                        for j in range(J):
                            mm = nc.tensor.transpose(bank[TB[k]][:, j * P:(j + 1) * P],
                                                     xn[:, u, j, k * P:(k + 1) * P], ident[:])
                        mm.then_inc(s_tr, 1)

                def gate_up(b, u, h):
                    c = 2 * b + u
                    if h == 0:
                        t.wait_ge(s_xt, 2 + 2 * c + 2)
                    t.wait_ge(s_h, HT * c + h + 1)
                    for w_, o in ((wg_t, 4), (wu_t, 5)):
                        mm = cut_products(bank[o + 2 * (h % 2)][:],
                                          [(w_[:, :, k, h * P:(h + 1) * P], xnt[:, u, :, k]) for k in range(KT)])
                    mm.then_inc(s_gu, 1)

                def down(b, u, more):
                    c = 2 * b + u
                    t.wait_ge(s_hl, 2 + HT * (c + 1))
                    if more:
                        t.wait_ge(s_x2, 2 * (c + 1) + 2)
                    for w in range(2):
                        for i in range(2):
                            tok = slice((2 * w + i) * P, (2 * w + i + 1) * P)
                            mm = cut_products(bank[OB[w]][:, i * D:(i + 1) * D],
                                              [(ht[:, u, :, h, tok], wd_t[:, :, h]) for h in range(HT)])
                        mm.then_inc(s_y, 1)

                def chunk(b, u, more):
                    if more:
                        project(b + u, 1 - u)
                    for h in range(2, HT - 1):
                        gate_up(b, u, h)
                    if more:
                        turn(b + u, 1 - u)
                    gate_up(b, u, HT - 1)
                    if more:
                        gate_up(b + u, 1 - u, 0)
                        gate_up(b + u, 1 - u, 1)
                    down(b, u, more)

                project(0, 0)
                turn(0, 0)
                gate_up(0, 0, 0)
                gate_up(0, 0, 1)
                sweep(t, chunk)
                barrier(t, 6)


_INS = ["x", "ctx_1024", "mask_BxSxS2_bk1", "L0_attn_Wq", "L0_attn_bq", "L0_attn_Wk", "L0_attn_bk",
        "L0_attn_Wv", "L0_attn_bv", "L0_attn_Wo", "L0_attn_bo", "L0_attn_W_cross",
        "L0_attn_shift_weights", "L0_attn_gate", "L0_xattn_Wq", "L0_xattn_Wk", "L0_xattn_Wv",
        "L0_xattn_Wo", "L0_ffn_w_gate", "L0_ffn_w_up", "L0_ffn_w_down"]


def kernel(**inputs):
    import numpy as np
    import concourse.bacc as bacc
    from concourse.bass_utils import run_bass_kernel_spmd

    nc = bacc.Bacc("TRN2", target_bir_lowering=False, num_devices=1)
    arrays, args = {}, []
    for name in _INS:
        a = np.ascontiguousarray(inputs[name])
        arrays[name] = a
        args.append(nc.dram_tensor(name, a.shape, mybir.dt.from_np(a.dtype), kind="ExternalInput").ap())
    out = nc.dram_tensor("out", inputs["x"].shape, F32, kind="ExternalOutput").ap()
    program(nc, *args, out)
    r = run_bass_kernel_spmd(nc, [arrays], core_ids=[0])
    return r.results[0]["out"]
```

```python
from contextlib import ExitStack

import concourse.bass as bass
from concourse import mybir

F32 = mybir.dt.float32
F32R = mybir.dt.float32r
BF16 = mybir.dt.bfloat16
I32 = mybir.dt.int32
U8 = mybir.dt.uint8
ALU = mybir.AluOpType
ACT = mybir.ActivationFunctionType
AX = mybir.AxisListType.X

P = 128
NEG = -1.0e30
EPS = 1e-5
HG = 4
Q_PARTS = (0, 1, 2, 0, 1, 0)
K_PARTS = (0, 0, 0, 1, 1, 2)
Q_RUNS = ((0, 3), (3, 2), (5, 1))
MX_BANKS, ST_BANKS, PV_BANKS = (0, 1, 2), (3, 4, 5), (6, 7)


def program(nc, x, ctxt, mask, Wq, bq, Wk, bk, Wv, bv, Wo, bo, W_cross, shift_w, gate,
            xWq, xWk, xWv, xWo, w_gate, w_up, w_down, out):
    B, S, D = x.shape
    S2 = ctxt.shape[1]
    H, HD = W_cross.shape[0], W_cross.shape[1]
    MS = shift_w.shape[1]
    HID = w_gate.shape[0]
    KT = D // P
    HT = HID // P
    CH = 512
    J = CH // P
    G = B * H // HG
    GB = H // HG
    HP = P // HD
    SK = 96
    R = len(Q_PARTS) * HD
    RM = R + 2
    VW = 2 * HD
    SCALE = float(HD) ** -0.5
    WSCALE = 1.0 / 127.0
    NCH = B * S // CH
    assert (D, HD, S, S2 <= SK, HG * VW, NCH) == (256, 16, 1024, True, P, 2 * B)

    def dram(name, shape, dt):
        return nc.dram_tensor(name, shape, dt, kind="Internal").ap()

    qk3 = dram("qk3", (2, 3, G, HG * HD, S), BF16)
    vs = dram("vs", (G, P, S // P, HG * VW), F32)
    od = dram("od", (G, HG, 2, HD, S), F32)
    x1s = dram("x1s", (NCH, P, J, D), F32)
    xqs = dram("xqs", (B, KT, len(Q_PARTS), HD, HP, S), BF16)
    xk3 = dram("xk3", (3, G * HG, HD, SK), BF16)
    xks = dram("xks", (R, G * HG, SK), BF16)
    xvs = dram("xvs", (G, SK, 1, HG * VW), F32)
    mts = dram("mts", (G, SK, S), BF16)
    rdn = dram("rdn", (G * HG, S), F32)
    rdn2 = dram("rdn2", (G * HG, S), F32)
    od2 = dram("od2", (G, HG, 2, HD, S), F32)

    xv = x.rearrange("b (h j p) d -> (b h) p j d", j=J, p=P)
    ov = out.rearrange("b (h j p) d -> (b h) p j d", j=J, p=P)
    mv = mask.rearrange("b (h j p) k -> (b h) p j k", j=J, p=P)

    root = ExitStack()
    with root:
        scope = [root]

        side = ["left"]

        def sb(name, shape, dt=F32):
            return scope[0].enter_context(nc.sbuf_tensor(name, shape, dt, side=side[0]))

        def sem(name):
            return root.enter_context(nc.semaphore(name))

        bank = [root.enter_context(nc.psum_tensor(f"bank{i}", [P, 512], F32)) for i in range(8)]
        s_phase = sem("s_phase")

        def arrive(eng):
            eng.drain().then_inc(s_phase, 1)

        def barrier(eng, n):
            arrive(eng)
            eng.wait_ge(s_phase, 5 * n)

        ident = sb("ident", [P, P])
        identb = sb("identb", [P, P], BF16)
        tri_q = sb("tri_q", [P, HG, P], BF16)
        tri_k = sb("tri_k", [P, HG, P], BF16)
        negid = sb("negid", [SK, HG, SK], BF16)
        wq_t = sb("wq_t", [P, 2, KT, D], F32R)
        wk_t = sb("wk_t", [P, 2, KT, D], F32R)
        wv_t = sb("wv_t", [P, 2, KT, D], F32R)
        wo_t = sb("wo_t", [P, KT, D])
        xwq = sb("xwq", [P, KT, D])
        xwo = sb("xwo", [P, KT, D])
        qkb = sb("qkb", [P, 2, KT])
        bv_b = sb("bv_b", [P, H, HD])
        bo_b = sb("bo_b", [P, D])
        wg_t = sb("wg_t", [P, 2, KT, HID], F32R)
        wu_t = sb("wu_t", [P, 2, KT, HID], F32R)
        wd_t = sb("wd_t", [P, 2, HT, D], F32R)
        mhalf = sb("mhalf", [P, J])
        oin = sb("oin", [P, 2, KT, CH])
        din = sb("din", [P, 2, KT, CH])
        rin = sb("rin", [P, 2, J, D])
        min_ = sb("min_", [P, 2, J, S2], U8)
        den = sb("den", [P, B, S * H // P])

        def again(b):
            return not (isinstance(b, int) and b == B - 1)

        def sweep(eng, chunk, peeled=1):
            with eng.Fori(0, B - peeled) as b:
                chunk(b, 0, True)
                chunk(b, 1, True)
            for b in range(B - peeled, B):
                chunk(b, 0, True)
                chunk(b, 1, b < B - 1)

        def moments(v, s_sum, c, src, stat, mom, ve):
            for j in range(J):
                nc.vector.bn_stats(stat[:, j], src[:, j]).then_inc(s_sum, 1)
            v.wait_ge(s_sum, NSUM * c + J)
            even, odd = stat[:, :, 1], stat[:, :, 4]
            nc.vector.tensor_tensor(mom[:, 1], even, odd, ALU.add).then_inc(s_sum, 1)
            nc.vector.tensor_tensor(mom[:, 2], even, odd, ALU.subtract).then_inc(s_sum, 1)
            nc.vector.tensor_tensor(mom[:, 3], stat[:, :, 2], stat[:, :, 5], ALU.add).then_inc(s_sum, 1)
            v.wait_ge(s_sum, NSUM * c + J + 3)
            nc.vector.tensor_scalar(mom[:, 0], mom[:, 1], 0.5, None, ALU.mult).then_inc(s_sum, 1)
            nc.vector.scalar_tensor_tensor(mom[:, 4], mom[:, 2], 0.25, mom[:, 2], ALU.mult, ALU.mult).then_inc(s_sum, 1)
            nc.vector.tensor_scalar(mom[:, 5], mom[:, 3], 1.0 / D, EPS, ALU.mult, ALU.add).then_inc(s_sum, 1)
            v.wait_ge(s_sum, NSUM * c + J + 6)
            nc.vector.tensor_tensor(ve, mom[:, 4], mom[:, 5], ALU.add).then_inc(s_sum, 1)

        NSUM = J + 7

        def cut_products(dst, terms):
            n = 0
            for a, b in terms:
                for i, j in ((0, 0), (0, 1), (1, 0)):
                    mm = nc.tensor.matmul(dst, a[:, i], b[:, j], start=(n == 0), stop=(n == 3 * len(terms) - 1))
                    n += 1
            return mm

        opening = root.enter_context(ExitStack())
        scope[0] = opening
        xin = sb("a_xin", [P, 2, J, D])
        stat = sb("a_stat", [P, 2, J, 6])
        mom = sb("a_mom", [P, 2, 6, J])
        ve = sb("a_ve", [P, 2, J])
        rstd = sb("a_rstd", [P, 2, J])
        xn = sb("a_xn", [P, 2, J, D])
        k3 = sb("k3", [P, KT, 3, B, SK], BF16)
        vx = sb("vx", [SK, B, H, VW])

        ld = [sem(f"a_ld{u}") for u in range(2)]
        s_sum = sem("a_sum")
        s_pow = sem("a_pow")
        s_xn = sem("a_xn_")
        s_tr = sem("a_tr")
        s_k = sem("w_k")
        s_vx = sem("w_vx")
        s_out = sem("w_out")
        s_stk = sem("w_stk")

        def stats1(v, b, u):
            c = 2 * b + u
            v.wait_ge(ld[u], 16 * (b + 1))
            moments(v, s_sum, c, xin[:, u], stat[:, u], mom[:, u], ve[:, u])

        def normalise1(v, b, u):
            c = 2 * b + u
            v.wait_ge(s_pow, c + 1)
            v.wait_ge(s_tr, 2 * c + 2)
            for j in range(J):
                nc.vector.tensor_scalar(xn[:, u, j], xin[:, u, j], mom[:, u, 0, j:j + 1], rstd[:, u, j:j + 1],
                                        ALU.subtract, ALU.mult).then_inc(s_xn, 1)

        def power1(g, b, u):
            c = 2 * b + u
            g.wait_ge(s_sum, NSUM * (c + 1))
            g.wait_ge(s_xn, J * c + J)
            nc.gpsimd.tensor_tensor(rstd[:, u], ve[:, u], mhalf[:], ALU.pow).then_inc(s_pow, 1)

        with ExitStack() as st:
            scope[0] = st
            n_q = sb("n_q", [P, KT, D])
            n_k = sb("n_k", [P, KT, D])
            n_v = sb("n_v", [P, KT, D])
            n_o = sb("n_o", [P, KT, D])
            ig = sb("ig", [P, HT, D], I32)
            iu = sb("iu", [P, HT, D], I32)
            idn = sb("idn", [P, KT, HID], I32)
            fg = sb("fg", [P, HT, D])
            fu = sb("fu", [P, HT, D])
            fd = sb("fd", [P, KT, HID])
            xwk = sb("xwk", [P, KT, D])
            xwv = sb("xwv", [P, KT, D])
            n_xq = sb("n_xq", [P, KT, D])
            bq_c = sb("bq_c", [P, KT])
            wc = sb("wc", [P, KT, HD])
            sw = sb("sw", [P, KT, MS])
            gt = sb("gt", [P, KT])
            ge = sb("ge", [P, KT])
            gs = sb("gs", [P, 2, KT])
            blk = sb("blk", [P, P])
            tau = sb("tau", [P, MS, P])
            mm_ = sb("mm_", [P, KT, P])
            ablk = sb("ablk", [P, KT, P])
            cn = sb("cn", [S2, B, D])
            c_t = sb("c_t", [P, KT, B, S2])
            kr = sb("kr", [P, B, S2])
            trif = sb("trif", [P, 2, P])

            s_in = sem("w_in")
            s_in2 = sem("w_in2")
            s_g = sem("w_g")
            s_v = sem("w_v")
            s_a = sem("w_a")
            s_ab = sem("w_ab")
            s_f = sem("w_f")
            s_t = sem("w_t")
            s_e = sem("w_e")
            s_el = sem("w_el")
            s_kh = sem("w_kh")

            def cols(a):
                return a.rearrange("(t p) -> p t", p=P)

            N_IN, N_IN2 = 5 + 2 + 2 * KT + 4, 8
            jobs = []

            def turned(src, dst, nk, no):
                for k in range(nk):
                    for o in range(0, no, 4):
                        n = min(4, no - o)
                        jobs.append(([src[:, o + i, k * P:(k + 1) * P] for i in range(n)],
                                     [d[:, k, o * P:(o + n) * P] for d in dst]))

            def both(w):
                return w[:, 0], w[:, 1]

            turned(n_k, both(wk_t), KT, KT)
            turned(n_v, both(wv_t), KT, KT)
            turned(n_o, (wo_t,), KT, KT)
            n_small = len(jobs)
            turned(fg, both(wg_t), KT, HT)
            turned(fu, both(wu_t), KT, HT)
            turned(fd, both(wd_t), HT, KT)
            NJ = len(jobs)
            cut = [n for n in range(NJ + KT) if n >= NJ or len(jobs[n][1]) == 2]
            N_FOLD = NJ + KT
            N_BIAS = N_FOLD + 1
            N_CTX = N_BIAS + KT
            N_XK = N_CTX + KT
            NB = 8

            block = st.enter_context(nc.Block())

            @block.sync
            def _(sp):
                sp.sem_inc(s_xn, 2 * J)
                sp.sem_inc(s_tr, 4)
                for dst, src in ((n_q, Wq), (n_k, Wk), (n_v, Wv), (n_o, Wo)):
                    sp.dma_start(dst[:], src.rearrange("(t p) n -> p t n", p=P)).then_inc(s_in, 16)
                sp.dma_start(wc[:], W_cross.rearrange("(t h) f g -> (h f) t g", t=KT)).then_inc(s_in, 16)
                with nc.allow_non_contiguous_dma(reason="biases on partitions, a few hundred words"):
                    sp.dma_start(bq_c[:], cols(bq)).then_inc(s_in, 16)
                    sp.dma_start(qkb[:, 1, :], cols(bk)).then_inc(s_in, 16)
                    for t in range(KT):
                        hs = slice(t * HP, (t + 1) * HP)
                        sp.dma_start(sw[:, t, :], shift_w[hs, None, :].to_broadcast([HP, HD, MS])).then_inc(s_in, 16)
                        sp.dma_start(gt[:, t:t + 1],
                                     gate[hs].rearrange("(h a b) -> h a b", a=1, b=1).to_broadcast([HP, HD, 1])).then_inc(s_in, 16)
                sp.dma_start(bv_b[:], bv.rearrange("(a n) -> a n", a=1).to_broadcast([P, D])).then_inc(s_in, 16)
                sp.dma_start(bo_b[:], bo.rearrange("(a n) -> a n", a=1).to_broadcast([P, D])).then_inc(s_in, 16)
                sp.dma_start(n_xq[:], xWq.rearrange("(t p) n -> p t n", p=P)).then_inc(s_in, 16)
                sp.dma_start(xwo[:], xWo.rearrange("(t p) n -> p t n", p=P)).then_inc(s_in, 16)
                sp.dma_start(xin[:, 0], xv[0]).then_inc(ld[0], 16)
                for dst, src in ((ig, w_gate), (iu, w_up), (idn, w_down), (xwk, xWk), (xwv, xWv)):
                    sp.dma_start(dst[:], src.rearrange("(t p) n -> p t n", p=P)).then_inc(s_in2, 16)
                sp.dma_start(cn[:], ctxt.rearrange("b s d -> s b d")).then_inc(s_in2, 16)
                sp.dma_start(xin[:, 1], xv[1]).then_inc(ld[1], 16)
                sp.wait_ge(s_in, 16 * N_IN)
                sp.wait_ge(s_in2, 16 * 6)
                barrier(sp, 1)

            @block.gpsimd
            def _(g):
                nc.gpsimd.memset(ident[:], 0.0).then_inc(s_g, 1)
                nc.gpsimd.memset(trif[:], 0.0).then_inc(s_g, 1)
                nc.gpsimd.memset(blk[:], 1.0).then_inc(s_g, 1)
                nc.gpsimd.memset(tau[:], 0.0).then_inc(s_g, 1)
                g.wait_ge(s_g, 4)
                nc.gpsimd.affine_select(out=ident[:], in_=ident[:], compare_op=ALU.not_equal, fill=1.0,
                                        base=0, pattern=[[-1, P]], channel_multiplier=1).then_inc(s_g, 1)
                nc.gpsimd.affine_select(out=blk[:], in_=blk[:], compare_op=ALU.is_ge, fill=0.0,
                                        base=0, pattern=[[-HD, HP], [0, HD]], channel_multiplier=1).then_inc(s_g, 1)
                g.wait_ge(s_g, 6)
                nc.gpsimd.affine_select(out=blk[:], in_=blk[:], compare_op=ALU.is_ge, fill=0.0,
                                        base=HD - 1, pattern=[[HD, HP], [0, HD]], channel_multiplier=-1).then_inc(s_g, 1)
                nc.gpsimd.affine_select(out=tau[:], in_=tau[:], compare_op=ALU.not_equal, fill=1.0,
                                        base=0, pattern=[[-1, MS], [1, P]], channel_multiplier=-1).then_inc(s_g, 1)
                nc.gpsimd.affine_select(out=trif[:, 0, :], in_=trif[:, 0, :], compare_op=ALU.is_ge, fill=NEG,
                                        base=0, pattern=[[-1, P]], channel_multiplier=1).then_inc(s_g, 1)
                nc.gpsimd.affine_select(out=trif[:, 1, :], in_=trif[:, 1, :], compare_op=ALU.is_ge, fill=NEG,
                                        base=0, pattern=[[1, P]], channel_multiplier=-1).then_inc(s_g, 1)
                nc.gpsimd.memset(mhalf[:], -0.5).then_inc(s_g, 1)
                nc.gpsimd.memset(k3[:], 0.0).then_inc(s_g, 1)
                nc.gpsimd.memset(vx[:], 0.0).then_inc(s_g, 1)
                g.wait_ge(s_g, 13)
                nc.gpsimd.memset(vx[:, :, :, HD:VW], 1.0).then_inc(s_g, 1)
                for h in range(HG):
                    nc.gpsimd.tensor_copy(tri_q[:, h, :], trif[:, 0, :])
                    nc.gpsimd.tensor_copy(tri_k[:, h, :], trif[:, 1, :])
                    nc.gpsimd.tensor_scalar(negid[:, h, :], ident[0:SK, 0:SK], NEG, None, ALU.mult)
                nc.gpsimd.tensor_copy(identb[:], ident[:])
                g.wait_ge(s_g, 14)
                power1(g, 0, 0)
                power1(g, 0, 1)
                barrier(g, 1)

            @block.vector
            def _(v):
                made = [0]

                def low(upto):
                    for n in cut[made[0]:upto]:
                        v.wait_ge(s_e, n + 1)
                        if n < NJ:
                            blocks, (hi, lo) = jobs[n]
                            w = len(blocks) * P
                        else:
                            hi, lo, w = wq_t[:, 0, n - NJ], wq_t[:, 1, n - NJ], D
                        nc.vector.tensor_tensor(lo, bank[n % NB][:, 0:w], hi.bitcast(F32), ALU.subtract).then_inc(s_el, 1)
                    made[0] = upto

                v.wait_ge(s_in, 16 * N_IN)
                v.wait_ge(s_a, 1)
                nc.vector.tensor_scalar(ge[:], ge[:], 1.0, None, ALU.add).then_inc(s_v, 1)
                v.wait_ge(s_v, 1)
                nc.vector.reciprocal(ge[:], ge[:]).then_inc(s_v, 1)
                v.wait_ge(s_v, 2)
                nc.vector.tensor_scalar(gs[:, 0, :], ge[:], SCALE, None, ALU.mult).then_inc(s_v, 1)
                nc.vector.tensor_scalar(gs[:, 1, :], ge[:], -SCALE, SCALE, ALU.mult, ALU.add).then_inc(s_v, 1)
                v.wait_ge(s_g, 10)
                n = 4
                for t in range(KT):
                    v.wait_ge(s_v, n)
                    nc.vector.tensor_scalar(mm_[:, t, :], tau[:, 0, :], sw[:, t, 0:1], None, ALU.mult).then_inc(s_v, 1)
                    n += 1
                    for s in range(1, MS):
                        v.wait_ge(s_v, n)
                        nc.vector.scalar_tensor_tensor(mm_[:, t, :], tau[:, s, :], sw[:, t, s:s + 1],
                                                       mm_[:, t, :], ALU.mult, ALU.add).then_inc(s_v, 1)
                        n += 1
                    v.wait_ge(s_v, n)
                    nc.vector.tensor_scalar(mm_[:, t, :], mm_[:, t, :], gs[:, 1, t:t + 1], None, ALU.mult).then_inc(s_v, 1)
                    n += 1
                    v.wait_ge(s_v, n)
                    nc.vector.scalar_tensor_tensor(
                        ablk[:, t, :].rearrange("p (h g) -> p h g", h=HP),
                        wc[:, t:t + 1, :].to_broadcast([P, HP, HD]), gs[:, 0, t:t + 1],
                        mm_[:, t, :].rearrange("p (h g) -> p h g", h=HP), ALU.mult, ALU.add).then_inc(s_v, 1)
                    n += 1
                    v.wait_ge(s_v, n)
                    nc.vector.tensor_tensor(ablk[:, t, :], ablk[:, t, :], blk[:], ALU.mult).then_inc(s_ab, 1)
                for t in range(KT):
                    nc.vector.tensor_copy(xwq[:, :, t * P:(t + 1) * P].rearrange("p k (r h) -> p k r h", r=HD),
                                          n_xq[:, :, t * P:(t + 1) * P].rearrange("p k (h r) -> p k r h", r=HD))
                stats1(v, 0, 0)
                normalise1(v, 0, 0)
                low(len(cut))
                v.wait_ge(s_g, 14)
                for t in range(KT):
                    ps = bank[(N_CTX + t) % NB][:, 0:B * S2].rearrange("p (b s) -> p b s", b=B)
                    v.wait_ge(s_kh, t + 1)
                    if t:
                        v.wait_ge(s_k, 3 * t)
                    nc.vector.tensor_tensor(kr[:], ps, k3[:, t, 0, :, 0:S2], ALU.subtract).then_inc(s_k, 1)
                    v.wait_ge(s_k, 3 * t + 1)
                    nc.vector.tensor_copy(k3[:, t, 1, :, 0:S2], kr[:]).then_inc(s_k, 1)
                    v.wait_ge(s_k, 3 * t + 2)
                    nc.vector.tensor_tensor(k3[:, t, 2, :, 0:S2], kr[:], k3[:, t, 1, :, 0:S2], ALU.subtract).then_inc(s_k, 1)
                stats1(v, 0, 1)
                barrier(v, 1)

            @block.scalar
            def _(a):
                a.wait_ge(s_in, 16 * N_IN)
                nc.scalar.activation(ge[:], gt[:], ACT.Exp, scale=-1.0).then_inc(s_a, 1)

                def empty(n, dst, src, **kw):
                    a.wait_ge(s_t, n + 1)
                    nc.scalar.activation(dst, src, ACT.Identity, **kw).then_inc(s_e, 1)

                for n, (blocks, dst) in enumerate(jobs):
                    if n == n_small:
                        a.wait_ge(s_in2, 16 * 6)
                        for f, i in ((fg, ig), (fu, iu), (fd, idn)):
                            nc.scalar.activation(f[:], i[:], ACT.Identity, scale=WSCALE).then_inc(s_f, 1)
                    empty(n, dst[0], bank[n % NB][:, 0:len(blocks) * P])
                for k in range(KT):
                    empty(NJ + k, wq_t[:, 0, k, :], bank[(NJ + k) % NB][:, 0:D])
                empty(N_FOLD, qkb[:, 0, :], bank[N_FOLD % NB][:, 0:KT])
                for k in range(KT):
                    empty(N_BIAS + k, c_t[:, k], bank[(N_BIAS + k) % NB][:, 0:B * S2].rearrange("p (b s) -> p b s", b=B))
                a.wait_ge(s_g, 14)
                for t in range(KT):
                    a.wait_ge(s_t, N_CTX + t + 1)
                    nc.scalar.activation(k3[:, t, 0, :, 0:S2],
                                         bank[(N_CTX + t) % NB][:, 0:B * S2].rearrange("p (b s) -> p b s", b=B),
                                         ACT.Identity).then_inc(s_kh, 1)
                nc.scalar.activation(gt[0:1, 0:1], gt[0:1, 0:1], ACT.Identity).then_inc(s_vx, 1)
                for b in range(B):
                    n = N_XK + b
                    a.wait_ge(s_t, n + 1)
                    nc.scalar.activation(vx[0:S2, b, :, 0:HD],
                                         bank[n % NB][0:S2, 0:D].rearrange("p (h d) -> p h d", h=H),
                                         ACT.Identity).then_inc(s_vx, 1)
                barrier(a, 1)

            @block.tensor
            def _(t_):
                t_.wait_ge(s_in, 16 * N_IN)
                t_.wait_ge(s_g, 5)

                def free(n):
                    if n >= NB:
                        t_.wait_ge(s_e, n - NB + 1)
                        if n - NB in cut:
                            t_.wait_ge(s_el, cut.index(n - NB) + 1)

                for n, (blocks, dst) in enumerate(jobs):
                    free(n)
                    if n >= n_small:
                        t_.wait_ge(s_f, 3)
                    for i, b_ in enumerate(blocks):
                        m = nc.tensor.transpose(bank[n % NB][:, i * P:(i + 1) * P], b_, ident[:])
                    m.then_inc(s_t, 1)
                t_.wait_ge(s_ab, KT)
                for k in range(KT):
                    free(NJ + k)
                    for o in range(KT):
                        m = nc.tensor.matmul(bank[(NJ + k) % NB][:, o * P:(o + 1) * P],
                                             n_q[:, o, k * P:(k + 1) * P], ablk[:, o, :], start=True, stop=True)
                    m.then_inc(s_t, 1)
                free(N_FOLD)
                for o in range(KT):
                    m = nc.tensor.matmul(bank[N_FOLD % NB][:, o:o + 1], ablk[:, o, :], bq_c[:, o:o + 1],
                                         start=True, stop=True)
                m.then_inc(s_t, 1)
                t_.wait_ge(s_in2, 16 * 6)
                for k in range(KT):
                    free(N_BIAS + k)
                    for b in range(B):
                        m = nc.tensor.transpose(bank[(N_BIAS + k) % NB][:, b * S2:(b + 1) * S2],
                                                cn[:, b, k * P:(k + 1) * P], ident[0:S2, 0:S2])
                    m.then_inc(s_t, 1)
                t_.wait_ge(s_e, N_CTX)
                t_.wait_ge(s_el, len(cut))
                for o in range(KT):
                    for k in range(KT):
                        m = nc.tensor.matmul(bank[(N_CTX + o) % NB][:, 0:B * S2],
                                             xwk[:, k, o * P:(o + 1) * P],
                                             c_t[:, k].rearrange("p b s -> p (b s)"),
                                             start=(k == 0), stop=(k == KT - 1))
                    m.then_inc(s_t, 1)
                for b in range(B):
                    for k in range(KT):
                        m = nc.tensor.matmul(bank[(N_XK + b) % NB][0:S2, 0:D], c_t[:, k, b, :], xwv[:, k, :],
                                             start=(k == 0), stop=(k == KT - 1))
                    m.then_inc(s_t, 1)
                barrier(t_, 1)

        def attention(stage, name, causal, ahead, ops, o_dst, following):
            KW = S if causal else SK
            KP = P if causal else SK
            NKT = S // P if causal else 1
            NPS = 12
            mx_units = []
            for half in range(2):
                for r in range(4):
                    if not causal:
                        mx_units.append((half, half, r, 0, HG, 0, KW, False))
                        continue
                    if half:
                        mx_units += [(half, 1, r, h, 1, 0, 512, False) for h in range(HG)]
                    hb = HG // (r + 1)
                    mx_units += [(half, 2 * half, r, h, hb, half * 512, (r + 1) * P, True)
                                 for h in range(0, HG, hb)]
            n_half = sum(1 for m in mx_units if m[0] == 0)
            st_units, sets = [], []
            for half in range(2):
                kts = range(4 * half + 4) if causal else range(1)
                for kt in kts:
                    diag = causal and kt >= 4 * half
                    q0 = (kt % 4) * P if diag else 0
                    n = 512 - q0
                    hb = max(1, (512 // n) // 2 * 2)
                    first = len(st_units)
                    st_units += [(half, kt, h, hb, q0, n, diag) for h in range(0, HG, hb)]
                    sets.append((half, kt, first, len(st_units), kt == kts[0], kt == kts[-1], q0, n, hb))
            NST = len(st_units)
            half_end = [max(s[3] for s in sets if s[0] == h) for h in range(2)]
            ring = [("m", i) for i in range(len(mx_units))]
            ring.insert(min(n_half + (4 if causal else 2), len(ring)), ("t", 0))
            ring.append(("t", 1))
            NMX = len(ring)
            NC = 3 if causal else 2
            LAG = 3
            LATE = 3 if causal else 0

            def reused(u, count, slots):
                last = max(w for w in range(count) if w % slots == u % slots) if u < slots else None
                return slots - count + last + 1 if u < slots else u + 1

            plan, at = [], 0
            for u in range(NST):
                plan.append(("s", u))
                plan += [("p", s) for s, x in enumerate(sets) if x[3] - 1 == u - LAG]
                if u == LATE:
                    plan.append(("r", NMX - 1, ahead - 1))
                upto = max(0, u - LATE + 1) * (NMX - 1) // (NST - LATE)
                plan += [("r", n, ahead) for n in range(at, upto)]
                at = upto
            plan += [("p", s) for s, x in enumerate(sets) if x[3] - 1 > NST - 1 - LAG]
            early_at = plan.index(("s", NST - 3))
            pm = sb(name + "pm", [P, 3, HG, 4])
            mxv = sb(name + "mxv", [P, HG * 4])
            mt = sb(name + "mt", [P, 2, 2, HG * 4], BF16)
            mrow = sb(name + "mrow", [2 * HG * 4, 2, 2, P], BF16)

            s_set = sem(name + "s_set")
            first_placed = len(ops.stq)
            s_mxf = sem(name + "s_mxf")
            s_mxe = sem(name + "s_mxe")
            s_cmb = sem(name + "s_cmb")
            s_mt = sem(name + "s_mt")
            md = [[sem(f"{name}md{i}{c}") for c in range(2)] for i in range(2)]
            s_st = sem(name + "s_st")
            s_ex = sem(name + "s_ex")
            s_pv = sem(name + "s_pv")
            s_u = sem(name + "s_u")
            us = [sem(f"{name}us{i}") for i in range(2)]
            stq, stk, va, mk, ld, NLD = ops.stq, ops.stk, ops.va, ops.mk, ops.ld, ops.n_loads

            def steps(eng, step):
                with eng.Fori(0, B - 1) as b:
                    for i in range(GB):
                        step(b, i, GB)
                for i in range(GB):
                    step(B - 1, i, GB - 1 - i)

            def after(b, i, n):
                return b + (i + n) // GB, (i + n) % GB

            def sync(sp, first):
                def maxima(b, i, c):
                    sp.wait_ge(s_mxe, 3 + (b * GB + i) * NMX + ring.index(("t", c)) + 1)
                    for t in range(2):
                        sp.dma_start(stq[i][R + t:R + t + 1, c].rearrange("a h q -> a (h q)"),
                                     mrow[16 * t:16 * (t + 1), i % 2, c]).then_inc(md[i % 2][c], 16)

                if first:
                    for i in range(ahead):
                        maxima(0, i, 0)
                        if i < ahead - 1:
                            maxima(0, i, 1)
                    return

                def step(b, i, left):
                    g = b * GB + i
                    if left >= ahead - 1:
                        maxima(*after(b, i, ahead - 1), 1)
                    if left >= GB - 1:
                        sp.wait_ge(s_pv, NPS + g * NST)
                        load_group(sp, ops, *after(b, i, GB - 1))
                    if left >= ahead:
                        maxima(*after(b, i, ahead), 0)
                    if isinstance(b, int):
                        following.early_sync(sp, i, us)
                    sp.wait_ge(s_u, 2 + 2 * g + 2)
                    sp.dma_start(o_dst[bass.ds(g, 1)].rearrange("a h w r t -> (a h w r) t"),
                                 ops.u[:, i % 2]).then_inc(us[i % 2], 16)

                steps(sp, step)
                barrier(sp, stage)
                for i in range(2):
                    sp.wait_ge(us[i], 16 * (G // 2 + 1))

            def gpsimd(g, first):
                if first:
                    for stk_i in stk[:first_placed]:
                        nc.gpsimd.memset(stk_i[R:RM], -1.0).then_inc(s_set, 1)
                    return
                for stk_i in stk[first_placed:]:
                    nc.gpsimd.memset(stk_i[R:RM], -1.0).then_inc(s_set, 1)
                following.early_gpsimd(g)
                barrier(g, stage)

            def vector(v, first):
                def item(b, i, n):
                    g = b * GB + i
                    kind, m = ring[n]
                    src = bank[MX_BANKS[n % 3]]
                    v.wait_ge(s_mxf, g * NMX + n + 1)
                    if kind == "t":
                        nc.vector.tensor_copy(mrow[:, i % 2, m], src[0:32, 0:P // 2].bitcast(BF16)).then_inc(s_mxe, 1)
                        return
                    half, k, r, h0, hb, _, w, _ = mx_units[m]
                    nc.vector.tensor_reduce(pm[:, k, h0:h0 + hb, r],
                                            src[:, 0:hb * w].rearrange("p (h w) -> p h w", h=hb),
                                            AX, ALU.max).then_inc(s_mxe, 1)
                    if m == n_half - 1 or m == len(mx_units) - 1:
                        parts_of_max(g, half, n)

                def parts_of_max(g, c, n):
                    v.wait_ge(s_mxe, 3 + g * NMX + n + 1)
                    m = pm[:, c].rearrange("p h r -> p (h r)")
                    if causal and c:
                        nc.vector.tensor_tensor(mxv[:], m, pm[:, 2].rearrange("p h r -> p (h r)"),
                                                ALU.max).then_inc(s_cmb, 1)
                        v.wait_ge(s_cmb, NC * g + 2)
                        m = mxv[:]
                    nc.vector.tensor_copy(mt[:, c, 0], m).then_inc(s_cmb, 1)
                    v.wait_ge(s_cmb, NC * g + (NC if c else 1))
                    nc.vector.tensor_tensor(mt[:, c, 1], m, mt[:, c, 0], ALU.subtract).then_inc(s_mt, 1)

                def step(b, i, left):
                    if left >= ahead - 1:
                        item(*after(b, i, ahead - 1), NMX - 1)
                    if left >= ahead:
                        for n in range(NMX - 1):
                            item(*after(b, i, ahead), n)
                    if isinstance(b, int) and i == 1:
                        following.reciprocals(v, 0)
                        following.reciprocals(v, 1)

                if first:
                    for n in range(ahead * NMX - 1):
                        item(0, n // NMX, n % NMX)
                    return

                steps(v, step)
                following.early_vector(v)
                barrier(v, stage)

            def scalar(a):
                def outputs(b, i, c):
                    g = b * GB + i
                    if c == 0:
                        a.wait_ge(us[i % 2], 16 * (2 * b + i // 2 + 1))
                    a.wait_ge(s_pv, NPS + g * NST + half_end[c])
                    nc.scalar.activation(ops.u[:, i % 2, c * 512:(c + 1) * 512], bank[PV_BANKS[c]][:],
                                         ACT.Identity).then_inc(s_u, 1)

                def step(b, i, left):
                    g = b * GB + i
                    for u, (half, kt, h0, hb, q0, n, diag) in enumerate(st_units):
                        a.wait_ge(s_st, g * NST + u + 1)
                        a.wait_ge(s_pv, g * NST + reused(u, NST, NPS))
                        nc.scalar.activation(ops.prob[:, u % NPS, 0:hb * n], bank[ST_BANKS[u % 3]][0:KP, 0:hb * n],
                                             ACT.Exp).then_inc(s_ex, 1)
                        if u == min(half_end[0] + LAG + 2, NST - 2):
                            outputs(b, i, 0)
                    outputs(b, i, 1)

                steps(a, step)
                barrier(a, stage)

            def tensor(t, first):
                def item(b, i, n):
                    g = b * GB + i
                    kind, m = ring[n]
                    dst = bank[MX_BANKS[n % 3]]
                    if n == 0:
                        t.wait_ge(ld[i], 16 * NLD * (b + 1))
                    t.wait_ge(s_mxe, g * NMX + reused(n, NMX, 3))
                    if kind == "t":
                        t.wait_ge(s_mt, 2 * g + m + 1)
                        nc.tensor.transpose(dst[0:32, 0:P // 2].bitcast(BF16),
                                            mt[:, m].rearrange("p t m -> p (t m)"), identb[:]).then_inc(s_mxf, 1)
                        return
                    half, k, r, h0, hb, k0, w, diag = mx_units[m]
                    qt = 4 * half + r
                    for h in range(hb):
                        mm = nc.tensor.matmul(dst[:, h * w:(h + 1) * w],
                                              stq[i][0:R, half, h0 + h, r * P:(r + 1) * P],
                                              stk[i][0:R, h0 + h, k0:k0 + w],
                                              start=(h == 0), stop=(causal and not diag), skip_group_check=True)
                    if not causal:
                        mm = nc.tensor.matmul(dst[:, 0:hb * w], mk[i][:, qt * P:(qt + 1) * P],
                                              negid[:].rearrange("k h l -> k (h l)"),
                                              start=False, stop=True, skip_group_check=True)
                    elif diag:
                        mm = nc.tensor.matmul(dst[:, 0:hb * w].rearrange("p (h w) -> p h w", h=hb)[:, :, w - P:w],
                                              identb[:], tri_q[:, 0:hb], start=False, stop=True,
                                              skip_group_check=True)
                    mm.then_inc(s_mxf, 1)

                def scores(b, i, u):
                    g = b * GB + i
                    half, kt, h0, hb, q0, n, diag = st_units[u]
                    if u == 0 or u == half_end[0]:
                        t.wait_ge(md[i % 2][half], 32 * (2 * b + i // 2 + 1))
                    t.wait_ge(s_ex, g * NST + reused(u, NST, 3))
                    dst = bank[ST_BANKS[u % 3]]
                    q = half * 512 + q0
                    for h in range(hb):
                        mm = nc.tensor.matmul(dst[0:KP, h * n:(h + 1) * n],
                                              stk[i][0:RM, h0 + h, kt * KP:(kt + 1) * KP],
                                              stq[i][0:RM, half, h0 + h, q0:q0 + n],
                                              start=(h == 0), stop=(causal and not diag), skip_group_check=True)
                    if not causal:
                        mm = nc.tensor.matmul(dst[0:KP, 0:n], negid[:, 0], mk[i][:, q:q + n],
                                              start=False, stop=True, skip_group_check=True)
                    elif diag:
                        mm = nc.tensor.matmul(dst[:, 0:hb * n].rearrange("p (h n) -> p h n", h=hb)[:, :, 0:P],
                                              identb[:], tri_k[:, 0:hb], start=False, stop=True,
                                              skip_group_check=True)
                    mm.then_inc(s_st, 1)

                def products(b, i, s):
                    g = b * GB + i
                    half, kt, first, end, fresh, last, q0, n, hb = sets[s]
                    if fresh:
                        t.wait_ge(s_u, 2 * g + half + 1)
                    t.wait_ge(s_ex, 3 + g * NST + end)
                    for h in range(HG):
                        mm = nc.tensor.matmul(bank[PV_BANKS[half]][h * VW:(h + 1) * VW, q0:512],
                                              va[i][:, kt, h * VW:(h + 1) * VW],
                                              ops.prob[:, (first + h // hb) % NPS, (h % hb) * n:(h % hb + 1) * n],
                                              start=fresh, stop=last)
                        if h % hb == hb - 1:
                            mm.then_inc(s_pv, 1)

                def step(b, i, left):
                    for n, what in enumerate(plan):
                        if left == 0 and n == early_at:
                            t.wait_ge(s_mxe, 3 + G * NMX)
                            following.early_tensor(t)
                        if what[0] == "s":
                            scores(b, i, what[1])
                        elif what[0] == "p":
                            products(b, i, what[1])
                        elif left >= what[2]:
                            item(*after(b, i, what[2]), what[1])

                if first:
                    for n in range(ahead * NMX - 1):
                        item(0, n // NMX, n % NMX)
                    return

                t.wait_ge(s_set, GB)
                steps(t, step)
                barrier(t, stage)

            def credits(sp):
                sp.sem_inc(s_mxe, 3)
                sp.sem_inc(s_ex, 3)
                sp.sem_inc(s_pv, NPS)
                sp.sem_inc(s_u, 2)
                for i in range(2):
                    sp.sem_inc(us[i], 16)

            def place():
                ops.prob = sb(name + "prob", [KP, NPS, 512])
                side[0] = "right"
                ops.u = sb(name + "u", [P, 2, S])
                side[0] = "left"

            return credits, place, sync, gpsimd, vector, scalar, tensor

        def chunk_loads(sp, o_src, r_src, b, u, oin, din, ld):
            for k in range(KT):
                sp.dma_start(oin[:, u, k], o_src[bass.ds(b * GB + 2 * k, 2), :, 0, :, u * CH:(u + 1) * CH]
                             .rearrange("g h r t -> (g h) r t")).then_inc(ld, 16)
                sp.dma_start(din[:, u, k], r_src[bass.ds(b * H + HP * k, HP), None, u * CH:(u + 1) * CH]
                             .to_broadcast([HP, HD, CH])).then_inc(ld, 16)

        class Operands:

            def __init__(self, name, kw, kp, nkt, load_qk, n_qk, v_src, m_src):
                self.name, self.kw, self.kp, self.nkt = name, kw, kp, nkt
                self.stq, self.stk, self.va, self.mk = [], [], [], []
                self.load_qk, self.v_src, self.m_src = load_qk, v_src, m_src
                self.ld = [sem(f"{name}ld{i}") for i in range(GB)]
                self.n_loads = n_qk + (1 if m_src is None else 2)

            def place(self, n):
                for i in range(len(self.stq), len(self.stq) + n):
                    self.stq.append(sb(f"{self.name}stq{i}", [P, 2, HG, 512], BF16))
                    self.stk.append(sb(f"{self.name}stk{i}", [P, HG, self.kw], BF16))
                    self.va.append(sb(f"{self.name}va{i}", [self.kp, self.nkt, HG * VW]))
                    if self.m_src is not None:
                        self.mk.append(sb(f"{self.name}mk{i}", [SK, S], BF16))

        def load_group(sp, ops, b, i):
            g = b * GB + i
            ops.load_qk(sp, b, i, ops.stq[i], ops.stk[i], ops.ld[i])
            sp.dma_start(ops.va[i][:], ops.v_src[bass.ds(g, 1)].rearrange("a p n c -> (a p) n c")).then_inc(ops.ld[i], 16)
            if ops.m_src is not None:
                sp.dma_start(ops.mk[i][:], ops.m_src[bass.ds(g, 1)].rearrange("a k t -> (a k) t")).then_inc(ops.ld[i], 16)

        class ChunkInputs:

            def __init__(self, name, o_src, r_dst, x_src, m_src, early_pool):
                self.o_src, self.r_dst, self.x_src, self.m_src = o_src, r_dst, x_src, m_src
                self.early_pool = early_pool
                self.ld = [sem(f"{name}ld{u}") for u in range(2)]
                self.s_den = sem(name + "den_")
                self.s_rd = sem(name + "rd")
                self.s_inv = sem(name + "inv")
                self.s_on = sem(name + "on")
                self.n_loads = 16 * (2 * KT + (1 if m_src is None else 2))

            def denominators(self, sp, b):
                sp.dma_start(den[:, b], self.o_src[b * GB:(b + 1) * GB, :, 1, 0]
                             .rearrange("g h (c t) -> (g h) c t", t=S * H // P)).then_inc(self.s_den, 16)

            def reciprocals(self, v, b):
                v.wait_ge(self.s_den, 16 * (b + 2 - b % 2))
                nc.vector.reciprocal(den[:, b], den[:, b]).then_inc(self.s_rd, 1)

            def inverses(self, sp, b):
                sp.wait_ge(self.s_rd, b + 1)
                sp.dma_start(self.r_dst[b * H:(b + 1) * H].rearrange("h (c t) -> (h c) t", t=S * H // P),
                             den[:, b]).then_inc(self.s_inv, 16)

            def load(self, sp, b, u):
                c = 2 * b + u
                chunk_loads(sp, self.o_src, self.r_dst, b, u, oin, din, self.ld[u])
                sp.dma_start(rin[:, u], self.x_src[bass.ds(c, 1)].rearrange("a p j d -> (a p) j d")).then_inc(self.ld[u], 16)
                if self.m_src is not None:
                    sp.dma_start(min_[:, u], self.m_src[bass.ds(c, 1)].rearrange("a p j k -> (a p) j k")).then_inc(self.ld[u], 16)

            def quotients(self, eng, b, u):
                eng.wait_ge(self.ld[u], self.n_loads * (b + 1))
                eng.tensor_tensor(oin[:, u], oin[:, u], din[:, u], ALU.mult).then_inc(self.s_on, 1)

            def early_sync(self, sp, i, us):
                if i == 0:
                    for w in range(2):
                        sp.wait_ge(us[w], 16 * (1 + 2 * 2))
                    self.denominators(sp, 0)
                    self.denominators(sp, 1)
                if i == 1:
                    self.inverses(sp, 0)
                    self.inverses(sp, 1)
                if i == 2:
                    sp.wait_ge(self.s_inv, 32)
                    self.load(sp, 0, 0)
                if i == 3:
                    self.load(sp, 0, 1)

            def early_vector(self, v):
                if self.early_pool:
                    sums3(v, 0, 0)
                    normalise3(v, 0, 0)
                else:
                    self.quotients(v, 0, 0)
                    self.quotients(v, 0, 1)

            def early_tensor(self, t):
                if self.early_pool:
                    project3(t, 0, 0)
                else:
                    project2(t, 0, 0)

            def early_gpsimd(self, g):
                for u in range(2):
                    if self.early_pool:
                        self.quotients(g, 0, u)
                    else:
                        residual_bias(g, 0, u)
                    if self.early_pool and u == 0:
                        power3(g, 0, 0)

        def residual_bias(g, b, u):
            g.wait_ge(middle_in.ld[u], middle_in.n_loads * (b + 1))
            nc.gpsimd.tensor_tensor(rin[:, u], rin[:, u], bo_b[:, None, :].to_broadcast([P, J, D]),
                                    ALU.add).then_inc(s_xb, 1)

        def load_self(sp, b, i, stq, stk, ld):
            g = b * GB + i
            for slot, part in enumerate(Q_PARTS):
                for c in range(2):
                    sp.dma_start(stq[HD * slot:HD * (slot + 1), c],
                                 qk3[0, part, bass.ds(g, 1), :, c * 512:(c + 1) * 512]
                                 .rearrange("a (h r) t -> (a r) h t", h=HG)).then_inc(ld, 16)
            for slot, part in enumerate(K_PARTS):
                sp.dma_start(stk[HD * slot:HD * (slot + 1)],
                             qk3[1, part, bass.ds(g, 1)].rearrange("a (h r) t -> (a r) h t", h=HG)).then_inc(ld, 16)

        def load_cross(sp, b, i, stq, stk, ld):
            g = b * GB + i
            heads = slice(i % 2 * HG, (i % 2 + 1) * HG)
            for c in range(2):
                sp.dma_start(stq[0:R, c], xqs[bass.ds(b, 1), i // 2, :, :, heads, c * 512:(c + 1) * 512]
                             .rearrange("a s r h t -> (a s r) h t")).then_inc(ld, 16)
            sp.dma_start(stk[0:R], xks[:, bass.ds(g * HG, HG)]).then_inc(ld, 16)

        beside_qkv = root.enter_context(ExitStack())
        scope[0], side[0] = beside_qkv, "right"
        s_xb = sem("c_xb")
        s_op2 = sem("c_op")
        s_x12 = sem("c_x1_")

        def project2(t, b, u):
            c = 2 * b + u
            t.wait_ge(middle_in.s_on, 2 + c + 1)
            for w in range(2):
                t.wait_ge(s_x12, 2 * c + w + 1)
                for i in range(2):
                    for k in range(KT):
                        mm = nc.tensor.matmul(bank[w][:, i * D:(i + 1) * D],
                                              oin[:, u, k, (2 * w + i) * P:(2 * w + i + 1) * P], wo_t[:, k],
                                              start=(k == 0), stop=(k == KT - 1))
                mm.then_inc(s_op2, 1)

        middle_in = ChunkInputs("c_", od, rdn, xv, mv, False)
        ffn_in = ChunkInputs("e_", od2, rdn2, x1s, None, True)
        self_ops = Operands("self_", S, P, S // P, load_self, 2 * len(Q_PARTS) + len(K_PARTS), vs, None)
        self_ops.place(1)
        (self_credits, self_place, self_sync, self_gpsimd, self_vector, self_scalar,
         self_tensor) = attention(3, "self_", True, 1, self_ops, od, middle_in)
        side[0] = "left"

        with ExitStack() as st:
            scope[0] = st
            xnt = sb("a_xnt", [P, 2, 2, KT, CH], F32R)
            parts = sb("a_parts", [P, 2, 4, 3, CH], BF16)
            rest = sb("a_rest", [P, 4, CH])
            vst = sb("a_vst", [P, 2, GB, J, HG, VW])

            s_xh = sem("a_xh")
            s_xt = sem("a_xt")
            s_qk = sem("a_qk")
            s_hi = sem("a_hi")
            s_r = sem("a_r")
            s_m = sem("a_m")
            s_lo = sem("a_lo")
            so = [sem(f"a_so{u}") for u in range(2)]
            s_vm = sem("a_vm")
            s_ve = sem("a_ve_")
            vo = [sem(f"a_vo{u}") for u in range(2)]
            QKB, VB = (2, 3, 4, 5), (6, 7)

            st.close()
            opening.close()
            self_ops.place(GB - 1)
            self_place()
            block = st.enter_context(nc.Block())

            @block.sync
            def _(sp):
                sp.sem_inc(s_xt, 2)
                sp.sem_inc(s_r, 4)
                sp.sem_inc(s_lo, 4)
                sp.sem_inc(s_vm, 4)
                sp.sem_inc(s_ve, 2)
                for u in range(2):
                    sp.sem_inc(so[u], 64)
                    sp.sem_inc(vo[u], 16)
                sp.wait_ge(s_xn, 2 * J + J)
                sp.dma_start(xin[:, 0], xv[2]).then_inc(ld[0], 16)
                sp.wait_ge(s_k, 3 * KT)
                for t in range(KT):
                    for b in range(B):
                        sp.dma_start(
                            xk3[:, b * H + HP * t:b * H + HP * (t + 1)].rearrange("c h r k -> (h r) c k"),
                            k3[:, t, :, b, :]).then_inc(s_out, 16)
                sp.wait_ge(s_vx, 1 + B)
                for b in range(B):
                    sp.dma_start(xvs[b * GB:(b + 1) * GB].rearrange("g k a c -> (k a) g c"),
                                 vx[:, b].rearrange("k h c -> k (h c)").rearrange("k (g c) -> k g c", g=GB)).then_inc(s_out, 16)

                def chunk(b, u, more):
                    c = 2 * b + u
                    if isinstance(b, int) and c == NCH - 4:
                        self_credits(sp)
                        sp.sem_inc(middle_in.s_on, 2)
                        sp.sem_inc(s_op2, 4)
                        sp.sem_inc(s_x12, 2)
                        sp.wait_ge(s_out, 16 * (KT * B + B))
                        for slot, part in enumerate(K_PARTS):
                            sp.dma_start(xks[HD * slot:HD * (slot + 1)],
                                         xk3[part].rearrange("h r k -> r h k")).then_inc(s_stk, 16)
                    if not isinstance(b, int) or c + 3 < NCH:
                        sp.wait_ge(s_xn, 2 * J + J * (c + 1) + J)
                        sp.dma_start(xin[:, 1 - u], xv[bass.ds(c + 3, 1)].rearrange("a p j d -> (a p) j d")).then_inc(ld[1 - u], 16)
                    if isinstance(b, int) and c == NCH - 2:
                        for w in range(2):
                            sp.wait_ge(so[w], 64 * 2)
                            sp.wait_ge(vo[w], 16 * 2)
                        load_group(sp, self_ops, 0, 0)
                    for n in range(4):
                        sp.wait_ge(s_lo, 4 + 4 * c + n + 1)
                        sp.dma_start(
                            qk3[n // 2, :, bass.ds(b * GB + 2 * (n % 2), 2), :, u * CH:(u + 1) * CH]
                            .rearrange("c g r t -> (g r) c t"),
                            parts[:, u, n]).then_inc(so[u], 16)
                    sp.wait_ge(s_ve, 2 + 2 * c + 2)
                    sp.dma_start(vs[bass.ds(b * GB, GB), :, u * J:(u + 1) * J, :].rearrange("g p j c -> p g (j c)"),
                                 vst[:, u].rearrange("p g j h c -> p g (j h c)")).then_inc(vo[u], 16)

                sweep(sp, chunk, 2)
                sp.wait_ge(s_stk, 16 * len(K_PARTS))
                for u in range(2):
                    sp.wait_ge(so[u], 64 * (B + 1))
                    sp.wait_ge(vo[u], 16 * (B + 1))
                barrier(sp, 2)
                load_group(sp, self_ops, 0, 1)
                self_sync(sp, True)
                load_group(sp, self_ops, 0, 2)
                self_sync(sp, False)

            @block.vector
            def _(v):
                nc.vector.memset(vst[:].rearrange("p u g j h c -> p (u g j h) c")[:, :, HD:VW], 1.0)

                def turned_low(b, u):
                    c = 2 * b + u
                    for k in range(KT):
                        v.wait_ge(s_xh, 2 * c + k + 1)
                        nc.vector.tensor_tensor(xnt[:, u, 1, k], bank[k][:], xnt[:, u, 0, k].bitcast(F32),
                                                ALU.subtract).then_inc(s_xt, 1)

                def split(b, u, n):
                    c = 2 * b + u
                    v.wait_ge(s_hi, 4 * c + n + 1)
                    v.wait_ge(s_lo, 4 * c + n + 1)
                    nc.vector.scalar_tensor_tensor(rest[:, n], bank[QKB[n]][:], qkb[:, n // 2, n % 2:n % 2 + 1],
                                                   parts[:, u, n, 0], ALU.add, ALU.subtract).then_inc(s_r, 1)

                def chunk(b, u, more):
                    c = 2 * b + u
                    nb, nu = b + u, 1 - u
                    if more:
                        normalise1(v, nb, nu)
                    split(b, u, 0)
                    split(b, u, 1)
                    if more:
                        turned_low(nb, nu)
                    if again(b):
                        stats1(v, b + 1, u)
                    split(b, u, 2)
                    split(b, u, 3)
                    v.wait_ge(vo[u], 16 * (b + 1))
                    for w in range(2):
                        v.wait_ge(s_vm, 4 + 2 * c + w + 1)
                        for i in range(2):
                            m = nc.vector.tensor_tensor(
                                vst[:, u, :, 2 * w + i, :, 0:HD],
                                bank[VB[w]][:, i * D:(i + 1) * D].rearrange("p (g h d) -> p g h d", g=GB, h=HG),
                                bv_b[:].rearrange("p (g h) d -> p g h d", g=GB), ALU.add)
                        m.then_inc(s_ve, 1)

                turned_low(0, 0)
                sweep(v, chunk)
                arrive(v)
                self_vector(v, True)
                v.wait_ge(s_phase, 5 * 2)
                self_vector(v, False)

            @block.gpsimd
            def _(g):
                def low(b, u, n):
                    c = 2 * b + u
                    g.wait_ge(s_m, 4 * c + n + 1)
                    nc.gpsimd.tensor_tensor(parts[:, u, n, 2], rest[:, n], parts[:, u, n, 1],
                                            ALU.subtract).then_inc(s_lo, 1)

                def chunk(b, u, more):
                    low(b, u, 0)
                    low(b, u, 1)
                    if again(b):
                        power1(g, b + 1, u)
                    low(b, u, 2)
                    low(b, u, 3)

                sweep(g, chunk)
                g.wait_ge(s_lo, 4 + 4 * NCH)
                self_gpsimd(g, True)
                barrier(g, 2)
                self_gpsimd(g, False)

            @block.scalar
            def _(a):
                def turned(b, u):
                    c = 2 * b + u
                    a.wait_ge(s_vm, 2 * c + 2)
                    for k in range(KT):
                        a.wait_ge(s_tr, 4 + 2 * c + k + 1)
                        nc.scalar.activation(xnt[:, u, 0, k], bank[k][:], ACT.Identity).then_inc(s_xh, 1)

                def high(b, u, n):
                    a.wait_ge(s_qk, 4 * (2 * b + u) + n + 1)
                    nc.scalar.activation(parts[:, u, n, 0], bank[QKB[n]][:], ACT.Identity,
                                         bias=qkb[:, n // 2, n % 2:n % 2 + 1]).then_inc(s_hi, 1)

                def middle(b, u, n):
                    a.wait_ge(s_r, 4 + 4 * (2 * b + u) + n + 1)
                    nc.scalar.activation(parts[:, u, n, 1], rest[:, n], ACT.Identity).then_inc(s_m, 1)

                def chunk(b, u, more):
                    c = 2 * b + u
                    a.wait_ge(so[u], 64 * (b + 1))
                    high(b, u, 0)
                    high(b, u, 1)
                    middle(b, u, 0)
                    if more:
                        turned(b + u, 1 - u)
                    high(b, u, 2)
                    middle(b, u, 1)
                    high(b, u, 3)
                    middle(b, u, 2)
                    middle(b, u, 3)

                turned(0, 0)
                sweep(a, chunk)
                barrier(a, 2)
                self_scalar(a)

            @block.tensor
            def _(t):
                def turn(b, u):
                    c = 2 * b + u
                    t.wait_ge(s_xn, 2 * J + J * c + J)
                    for k in range(KT):
                        t.wait_ge(s_xt, 2 * c + k + 1)
                        for j in range(J):
                            m = nc.tensor.transpose(bank[k][:, j * P:(j + 1) * P],
                                                    xn[:, u, j, k * P:(k + 1) * P], ident[:])
                        m.then_inc(s_tr, 1)

                def values(b, u, w):
                    c = 2 * b + u
                    t.wait_ge(s_ve, 2 * c + w + 1)
                    for i in range(2):
                        tok = slice((2 * w + i) * P, (2 * w + i + 1) * P)
                        m = cut_products(bank[VB[w]][:, i * D:(i + 1) * D],
                                         [(xnt[:, u, :, k, tok], wv_t[:, :, k]) for k in range(KT)])
                    m.then_inc(s_vm, 1)

                def chunk(b, u, more):
                    c = 2 * b + u
                    t.wait_ge(s_xt, 2 + 2 * c + 2)
                    for n in range(4):
                        t.wait_ge(s_r, 4 * c + n + 1)
                        w_ = (wq_t, wk_t)[n // 2]
                        m = cut_products(bank[QKB[n]][:],
                                         [(w_[:, :, k, (n % 2) * P:(n % 2 + 1) * P], xnt[:, u, :, k]) for k in range(KT)])
                        m.then_inc(s_qk, 1)
                        if n == 1 and more:
                            turn(b + u, 1 - u)
                    values(b, u, 0)
                    values(b, u, 1)

                turn(0, 0)
                sweep(t, chunk)
                t.wait_ge(s_xt, 2 + 2 * NCH)
                t.wait_ge(s_r, 4 + 4 * NCH)
                arrive(t)
                self_tensor(t, True)
                t.wait_ge(s_phase, 5 * 2)
                self_tensor(t, False)

        beside_qkv.close()

        across = root.enter_context(ExitStack())
        scope[0] = across
        cross_ops = Operands("cross_", SK, SK, 1, load_cross, 3, xvs, mts)
        cross_ops.place(GB)
        (cross_credits, cross_place, cross_sync, cross_gpsimd, cross_vector, cross_scalar,
         cross_tensor) = attention(5, "cross_", False, 2, cross_ops, od2, ffn_in)

        with ExitStack() as st:
            scope[0] = st
            x1 = sb("c_x1", [P, 2, J, D])
            stat = sb("c_stat", [P, 2, J, 6])
            mom = sb("c_mom", [P, 2, 6, J])
            ve = sb("c_ve", [P, 2, J])
            rstd = sb("c_rstd", [P, 2, J])
            allm = sb("c_allm", [P, 2, J])
            live = sb("c_live", [P, 2, J])
            meff = sb("c_meff", [P, 2, J, SK], BF16)
            xn = sb("c_xn", [P, 2, J, D])
            xnt = sb("c_xnt", [P, 2, KT, CH])
            parts = sb("c_parts", [P, 2, KT, 3, CH], BF16)
            rest = sb("c_rest", [P, KT, CH])
            mtr = sb("c_mtr", [SK, 2, CH], BF16)

            x1o = [sem(f"c_x1o{u}") for u in range(2)]
            s_sum = sem("c_sum")
            s_pow = sem("c_pow")
            s_all = sem("c_all")
            s_sc = sem("c_sc")
            s_me = sem("c_me")
            s_xn = sem("c_xn_")
            s_mtp = sem("c_mtp")
            s_mts = sem("c_mts")
            mo = [sem(f"c_mo{u}") for u in range(2)]
            s_tr = sem("c_tr")
            s_xt = sem("c_xt")
            s_q = sem("c_q")
            s_hi = sem("c_hi")
            s_r = sem("c_r")
            s_m = sem("c_m")
            s_lo = sem("c_lo")
            so = [[sem(f"c_so{n}{u}") for u in range(2)] for n in range(KT)]
            OB, TB, QB, MB = (0, 1), (2, 3), (4, 5), 6
            NSO = 16 * len(Q_RUNS)

            block = st.enter_context(nc.Block())

            def store_queries(eng, b, u, n):
                c = 2 * b + u
                eng.wait_ge(s_lo, 2 + 2 * c + n + 1)
                for slot, number in Q_RUNS:
                    eng.dma_start(xqs[bass.ds(b, 1), n, slot:slot + number, :, :, u * CH:(u + 1) * CH]
                                  .rearrange("a s r h t -> (a r h) s t"),
                                  parts[:, u, n, 0:number]).then_inc(so[n][u], 16)

            @block.sync
            def _(sp):
                for s_, n in ((s_me, 4), (s_xn, 8), (s_mtp, 2), (s_mts, 1),
                              (s_tr, 4), (s_xt, 2), (s_q, 4), (s_r, 2), (s_lo, 2)):
                    sp.sem_inc(s_, n)
                for u in range(2):
                    sp.sem_inc(x1o[u], 16)
                    sp.sem_inc(mo[u], 64)
                    for n in range(KT):
                        sp.sem_inc(so[n][u], NSO)

                def used(b, u):
                    c = 2 * b + u
                    sp.wait_ge(s_x12, 2 + 2 * c + 2)
                    sp.wait_ge(s_me, 4 + 4 * c + 4)

                cross_credits(sp)
                middle_in.denominators(sp, 2)
                middle_in.denominators(sp, 3)

                def store_sums(b, u):
                    c = 2 * b + u
                    sp.wait_ge(s_x12, 2 + 2 * c + 2)
                    sp.dma_start(x1s[bass.ds(c, 1)].rearrange("a p j d -> (a p) j d"), x1[:, u]).then_inc(x1o[u], 16)

                def chunk(b, u, more):
                    c = 2 * b + u
                    if more:
                        store_sums(b + u, 1 - u)
                    if not isinstance(b, int) or c + 3 < NCH:
                        used(b + u, 1 - u)
                        middle_in.load(sp, b + u + 1, 1 - u)
                    sp.wait_ge(s_mts, 1 + c + 1)
                    sp.dma_start(mts[bass.ds(b * GB, GB), :, u * CH:(u + 1) * CH].rearrange("g k t -> k g t"),
                                 mtr[:, u:u + 1].to_broadcast([SK, GB, CH])).then_inc(mo[u], 64)
                    if isinstance(b, int) and b == B - 1 and u == 0:
                        for w in range(2):
                            sp.wait_ge(mo[w], 64 * 2)
                            for n in range(KT):
                                sp.wait_ge(so[n][w], NSO * 2)
                        load_group(sp, cross_ops, 0, 0)
                        load_group(sp, cross_ops, 0, 1)
                    store_queries(sp, b, u, 0)

                store_sums(0, 0)
                used(0, 0)
                middle_in.load(sp, 1, 0)
                middle_in.inverses(sp, 2)
                middle_in.inverses(sp, 3)
                sp.wait_ge(middle_in.s_inv, 16 * B)
                sweep(sp, chunk, 2)
                cross_sync(sp, True)
                load_group(sp, cross_ops, 0, 2)
                for u in range(2):
                    sp.wait_ge(x1o[u], 16 * (B + 1))
                    sp.wait_ge(mo[u], 64 * (B + 1))
                    for n in range(KT):
                        sp.wait_ge(so[n][u], NSO * (B + 1))
                barrier(sp, 4)

            @block.gpsimd
            def _(g):
                def power(b, u):
                    c = 2 * b + u
                    g.wait_ge(s_sum, NSUM * (c + 1))
                    g.wait_ge(s_xn, J * c + J)
                    nc.gpsimd.tensor_tensor(rstd[:, u], ve[:, u], mhalf[:], ALU.pow).then_inc(s_pow, 1)

                def low(b, u, n):
                    c = 2 * b + u
                    g.wait_ge(s_m, 2 * c + n + 1)
                    nc.gpsimd.tensor_tensor(parts[:, u, n, 2], rest[:, n], parts[:, u, n, 1],
                                            ALU.subtract).then_inc(s_lo, 1)

                def chunk(b, u, more):
                    if again(b):
                        residual_bias(g, b + 1, u)
                    low(b, u, 0)
                    low(b, u, 1)
                    if again(b):
                        power(b + 1, u)

                power(0, 0)
                power(0, 1)
                sweep(g, chunk)
                g.wait_ge(s_lo, 2 + 2 * NCH)
                cross_gpsimd(g, True)
                barrier(g, 4)

            @block.vector
            def _(v):
                for u in range(2):
                    nc.vector.memset(meff[:, u, :, S2:SK], 1.0)

                def masks(b, u):
                    c = 2 * b + u
                    v.wait_ge(middle_in.ld[u], 96 * (b + 1))
                    v.wait_ge(s_mtp, c + 1)
                    nc.vector.tensor_reduce(allm[:, u], min_[:, u], AX, ALU.min).then_inc(s_all, 1)
                    v.wait_ge(s_all, 2 * c + 1)
                    nc.vector.tensor_scalar(live[:, u], allm[:, u], -1.0, 1.0, ALU.mult, ALU.add).then_inc(s_all, 1)
                    v.wait_ge(s_all, 2 * c + 2)
                    for j in range(J):
                        nc.vector.tensor_scalar(meff[:, u, j, 0:S2], min_[:, u, j], live[:, u, j:j + 1], None,
                                                ALU.mult).then_inc(s_me, 1)

                def sums(b, u):
                    c = 2 * b + u
                    v.wait_ge(s_xb, c + 1)
                    v.wait_ge(x1o[u], 16 * (b + 1))
                    for w in range(2):
                        v.wait_ge(s_op2, 4 + 2 * c + w + 1)
                        nc.vector.tensor_tensor(x1[:, u, 2 * w:2 * w + 2].rearrange("p j d -> p (j d)"), bank[OB[w]][:],
                                                rin[:, u, 2 * w:2 * w + 2].rearrange("p j d -> p (j d)"),
                                                ALU.add).then_inc(s_x12, 1)
                    v.wait_ge(s_x12, 2 + 2 * c + 2)
                    moments(v, s_sum, c, x1[:, u], stat[:, u], mom[:, u], ve[:, u])

                def normalise(b, u):
                    c = 2 * b + u
                    v.wait_ge(s_pow, c + 1)
                    nc.vector.tensor_tensor(rstd[:, u], rstd[:, u], live[:, u], ALU.mult).then_inc(s_sc, 1)
                    v.wait_ge(s_sc, c + 1)
                    v.wait_ge(s_tr, 2 * c + 2)
                    for j in range(J):
                        nc.vector.tensor_scalar(xn[:, u, j], x1[:, u, j], mom[:, u, 0, j:j + 1], rstd[:, u, j:j + 1],
                                                ALU.subtract, ALU.mult).then_inc(s_xn, 1)

                def split(b, u, n):
                    c = 2 * b + u
                    v.wait_ge(s_hi, 2 * c + n + 1)
                    v.wait_ge(s_lo, 2 * c + n + 1)
                    nc.vector.scalar_tensor_tensor(rest[:, n], bank[QB[n]][:], SCALE,
                                                   parts[:, u, n, 0], ALU.mult, ALU.subtract).then_inc(s_r, 1)
                    v.wait_ge(s_r, 2 + 2 * c + n + 1)
                    nc.vector.tensor_copy(parts[:, u, n, 1], rest[:, n]).then_inc(s_m, 1)

                def chunk(b, u, more):
                    if more:
                        normalise(b + u, 1 - u)
                    split(b, u, 0)
                    split(b, u, 1)
                    if again(b):
                        sums(b + 1, u)
                    if not isinstance(b, int) or 2 * b + u + 3 < NCH:
                        middle_in.quotients(v, b + 1 + u, 1 - u)
                    if again(b):
                        masks(b + 1, u)

                sums(0, 0)
                masks(0, 0)
                normalise(0, 0)
                sums(0, 1)
                masks(0, 1)
                middle_in.reciprocals(v, 2)
                middle_in.reciprocals(v, 3)
                middle_in.quotients(v, 1, 0)
                sweep(v, chunk, 2)
                arrive(v)
                cross_vector(v, True)
                v.wait_ge(s_phase, 5 * 4)

            @block.scalar
            def _(a):
                def turned(b, u):
                    c = 2 * b + u
                    a.wait_ge(s_q, 2 * c + 2)
                    for k in range(KT):
                        a.wait_ge(s_tr, 4 + 2 * c + k + 1)
                        nc.scalar.activation(xnt[:, u, k], bank[TB[k]][:], ACT.Identity).then_inc(s_xt, 1)
                    a.wait_ge(s_mtp, 2 + c + 1)
                    a.wait_ge(mo[u], 64 * (b + 1))
                    nc.scalar.activation(mtr[:, u], bank[MB][0:SK, 0:CH // 2].bitcast(BF16), ACT.Identity).then_inc(s_mts, 1)

                def chunk(b, u, more):
                    c = 2 * b + u
                    for n in range(KT):
                        a.wait_ge(so[n][u], NSO * (b + 1))
                        a.wait_ge(s_q, 4 + 2 * c + n + 1)
                        nc.scalar.activation(parts[:, u, n, 0], bank[QB[n]][:], ACT.Identity, scale=SCALE).then_inc(s_hi, 1)
                    if more:
                        turned(b + u, 1 - u)
                    store_queries(a, b, u, 1)

                turned(0, 0)
                sweep(a, chunk)
                barrier(a, 4)

            @block.tensor
            def _(t):
                def turn(b, u):
                    c = 2 * b + u
                    t.wait_ge(s_xn, 8 + 4 * c + 4)
                    for k in range(KT):
                        t.wait_ge(s_xt, 2 * c + k + 1)
                        for j in range(J):
                            mm = nc.tensor.transpose(bank[TB[k]][:, j * P:(j + 1) * P],
                                                     xn[:, u, j, k * P:(k + 1) * P], ident[:])
                        mm.then_inc(s_tr, 1)
                    t.wait_ge(s_me, 4 + 4 * c + 4)
                    t.wait_ge(s_mts, c + 1)
                    for j in range(J):
                        mm = nc.tensor.transpose(bank[MB][0:SK, j * P // 2:(j + 1) * P // 2].bitcast(BF16),
                                                 meff[:, u, j], identb[:])
                    mm.then_inc(s_mtp, 1)

                def chunk(b, u, more):
                    c = 2 * b + u
                    t.wait_ge(s_xt, 2 + 2 * c + 2)
                    for n in range(KT):
                        t.wait_ge(s_r, 2 * c + n + 1)
                        for k in range(KT):
                            mm = nc.tensor.matmul(bank[QB[n]][:], xwq[:, k, n * P:(n + 1) * P], xnt[:, u, k],
                                                  start=(k == 0), stop=(k == KT - 1))
                        mm.then_inc(s_q, 1)
                    if again(b):
                        project2(t, b + 1, u)
                    if more:
                        turn(b + u, 1 - u)

                project2(t, 0, 1)
                turn(0, 0)
                sweep(t, chunk)
                t.wait_ge(s_x12, 2 + 2 * NCH)
                t.wait_ge(s_xt, 2 + 2 * NCH)
                arrive(t)
                cross_tensor(t, True)
                t.wait_ge(s_phase, 5 * 4)

        beside_cross = root.enter_context(ExitStack())
        scope[0], side[0] = beside_cross, "right"
        x2 = sb("e_x2", [P, 2, J, D])
        stat = sb("e_stat", [P, 2, J, 6])
        mom = sb("e_mom", [P, 2, 6, J])
        ve = sb("e_ve", [P, 2, J])
        rstd = sb("e_rstd", [P, 2, J])
        xn = sb("e_xn", [P, 2, J, D])

        s_op = sem("e_op")
        s_x2 = sem("e_x2_")
        s_sum = sem("e_sum")
        s_pow = sem("e_pow")
        s_xn = sem("e_xn_")
        s_tr = sem("e_tr")
        s_xh = sem("e_xh")
        s_xt = sem("e_xt")
        s_gu = sem("e_gu")
        s_sg = sem("e_sg_")
        s_h = sem("e_h")
        s_hh = sem("e_hh")
        s_hl = sem("e_hl")
        s_y = sem("e_y")
        s_yo = sem("e_yo_")
        yd = [sem(f"e_yd{u}") for u in range(2)]
        OB, TB = (0, 1), (2, 3)

        def credits3(sp):
            for s_, n in ((ffn_in.s_on, 2), (s_op, 4), (s_xn, 8), (s_tr, 4), (s_xt, 2), (s_gu, 12), (s_sg, 2),
                          (s_h, 2), (s_hl, 2), (s_y, 4), (s_yo, 4)):
                sp.sem_inc(s_, n)
            for u in range(2):
                sp.sem_inc(yd[u], 16)

        def power3(g, b, u):
            c = 2 * b + u
            g.wait_ge(s_sum, NSUM * (c + 1))
            g.wait_ge(s_xn, J * c + J)
            nc.gpsimd.tensor_tensor(rstd[:, u], ve[:, u], mhalf[:], ALU.pow).then_inc(s_pow, 1)

        def sums3(v, b, u):
            c = 2 * b + u
            for w in range(2):
                v.wait_ge(s_op, 4 + 2 * c + w + 1)
                nc.vector.tensor_tensor(x2[:, u, 2 * w:2 * w + 2].rearrange("p j d -> p (j d)"), bank[OB[w]][:],
                                        rin[:, u, 2 * w:2 * w + 2].rearrange("p j d -> p (j d)"),
                                        ALU.add).then_inc(s_x2, 1)
            v.wait_ge(s_x2, 2 * c + 2)
            moments(v, s_sum, c, x2[:, u], stat[:, u], mom[:, u], ve[:, u])

        def normalise3(v, b, u):
            c = 2 * b + u
            v.wait_ge(s_pow, c + 1)
            v.wait_ge(s_tr, 2 * c + 2)
            for j in range(J):
                nc.vector.tensor_scalar(xn[:, u, j], x2[:, u, j], mom[:, u, 0, j:j + 1], rstd[:, u, j:j + 1],
                                        ALU.subtract, ALU.mult).then_inc(s_xn, 1)

        def project3(t, b, u):
            c = 2 * b + u
            t.wait_ge(ffn_in.s_on, 2 + c + 1)
            for w in range(2):
                t.wait_ge(s_yo, 2 * c + w + 1)
                for i in range(2):
                    for k in range(KT):
                        mm = nc.tensor.matmul(bank[OB[w]][:, i * D:(i + 1) * D],
                                              oin[:, u, k, (2 * w + i) * P:(2 * w + i + 1) * P], xwo[:, k],
                                              start=(k == 0), stop=(k == KT - 1))
                mm.then_inc(s_op, 1)

        side[0] = "left"

        with ExitStack() as st:
            scope[0] = st
            cross_place()
            block = st.enter_context(nc.Block())

            @block.sync
            def _(sp):
                credits3(sp)
                cross_sync(sp, False)

            @block.gpsimd
            def _(g):
                cross_gpsimd(g, False)

            @block.vector
            def _(v):
                cross_vector(v, False)

            @block.scalar
            def _(a):
                cross_scalar(a)

            @block.tensor
            def _(t):
                cross_tensor(t, False)
        across.close()

        with ExitStack() as st:
            scope[0] = st
            yo = sb("e_yo", [P, 2, J, D])
            xnt = sb("e_xnt", [P, 2, 2, KT, CH], F32R)
            sg = sb("e_sg", [P, 2, CH])
            hf = sb("e_hf", [P, 2, CH])
            ht = sb("e_ht", [P, 2, 2, HT, CH], F32R)


            block = st.enter_context(nc.Block())

            @block.sync
            def _(sp):

                ffn_in.denominators(sp, 2)
                ffn_in.denominators(sp, 3)
                ffn_in.inverses(sp, 2)
                ffn_in.inverses(sp, 3)
                sp.wait_ge(ffn_in.s_inv, 16 * B)

                def chunk(b, u, more):
                    c = 2 * b + u
                    if again(b):
                        sp.wait_ge(s_x2, 2 * c + 2)
                        ffn_in.load(sp, b + 1, u)
                    sp.wait_ge(s_yo, 4 + 2 * c + 2)
                    sp.dma_start(ov[bass.ds(c, 1)].rearrange("a p j d -> (a p) j d"), yo[:, u]).then_inc(yd[u], 16)

                sweep(sp, chunk)
                for u in range(2):
                    sp.wait_ge(yd[u], 16 * (B + 1))
                barrier(sp, 6)

            @block.gpsimd
            def _(g):
                def hidden_low(b, u, h):
                    c = 2 * b + u
                    g.wait_ge(s_hh, HT * c + h + 1)
                    nc.gpsimd.tensor_tensor(ht[:, u, 1, h], hf[:, h % 2], ht[:, u, 0, h].bitcast(F32),
                                            ALU.subtract).then_inc(s_hl, 1)

                def chunk(b, u, more):
                    if more:
                        power3(g, b + u, 1 - u)
                    hidden_low(b, u, 2)
                    hidden_low(b, u, 3)
                    hidden_low(b, u, 4)
                    if again(b):
                        ffn_in.quotients(g, b + 1, u)
                    hidden_low(b, u, 5)
                    if more:
                        hidden_low(b + u, 1 - u, 0)
                        hidden_low(b + u, 1 - u, 1)

                hidden_low(0, 0, 0)
                hidden_low(0, 0, 1)
                sweep(g, chunk)
                barrier(g, 6)

            @block.vector
            def _(v):
                def hidden(b, u, h):
                    c = 2 * b + u
                    if h == 0:
                        v.wait_ge(s_y, 2 * c + 2)
                    v.wait_ge(s_sg, 2 + HT * c + h + 1)
                    v.wait_ge(s_hl, HT * c + h + 1)
                    nc.vector.tensor_tensor(hf[:, h % 2], bank[5 + 2 * (h % 2)][:], sg[:, h % 2], ALU.mult).then_inc(s_h, 1)
                    v.wait_ge(s_h, 2 + HT * c + h + 1)
                    nc.vector.tensor_copy(ht[:, u, 0, h], hf[:, h % 2]).then_inc(s_hh, 1)

                def turned_low(b, u):
                    c = 2 * b + u
                    for k in range(KT):
                        v.wait_ge(s_xh, 2 * c + k + 1)
                        nc.vector.tensor_tensor(xnt[:, u, 1, k], bank[TB[k]][:], xnt[:, u, 0, k].bitcast(F32),
                                                ALU.subtract).then_inc(s_xt, 1)

                def chunk(b, u, more):
                    c = 2 * b + u
                    nb, nu = b + u, 1 - u
                    if more:
                        sums3(v, nb, nu)
                    hidden(b, u, 2)
                    if more:
                        normalise3(v, nb, nu)
                    hidden(b, u, 3)
                    hidden(b, u, 4)
                    if more:
                        turned_low(nb, nu)
                    hidden(b, u, 5)
                    if more:
                        hidden(nb, nu, 0)
                        hidden(nb, nu, 1)
                    v.wait_ge(yd[u], 16 * (b + 1))
                    for w in range(2):
                        v.wait_ge(s_y, 4 + 2 * c + w + 1)
                        nc.vector.tensor_tensor(yo[:, u, 2 * w:2 * w + 2].rearrange("p j d -> p (j d)"), bank[OB[w]][:],
                                                x2[:, u, 2 * w:2 * w + 2].rearrange("p j d -> p (j d)"),
                                                ALU.add).then_inc(s_yo, 1)

                turned_low(0, 0)
                ffn_in.reciprocals(v, 2)
                ffn_in.reciprocals(v, 3)
                hidden(0, 0, 0)
                hidden(0, 0, 1)
                sweep(v, chunk)
                barrier(v, 6)

            @block.scalar
            def _(a):
                def turned(b, u):
                    c = 2 * b + u
                    a.wait_ge(s_gu, HT * c + HT)
                    for k in range(KT):
                        a.wait_ge(s_tr, 4 + 2 * c + k + 1)
                        nc.scalar.activation(xnt[:, u, 0, k], bank[TB[k]][:], ACT.Identity).then_inc(s_xh, 1)

                def silu(b, u, h):
                    c = 2 * b + u
                    a.wait_ge(s_gu, 2 * HT + HT * c + h + 1)
                    a.wait_ge(s_h, HT * c + h + 1)
                    nc.scalar.activation(sg[:, h % 2], bank[4 + 2 * (h % 2)][:], ACT.Silu).then_inc(s_sg, 1)

                def chunk(b, u, more):
                    for h in range(2, HT - 1):
                        silu(b, u, h)
                    if more:
                        turned(b + u, 1 - u)
                    silu(b, u, HT - 1)
                    if more:
                        silu(b + u, 1 - u, 0)
                        silu(b + u, 1 - u, 1)

                turned(0, 0)
                silu(0, 0, 0)
                silu(0, 0, 1)
                sweep(a, chunk)
                barrier(a, 6)

            @block.tensor
            def _(t):
                def turn(b, u):
                    c = 2 * b + u
                    t.wait_ge(s_xn, 8 + 4 * c + 4)
                    for k in range(KT):
                        t.wait_ge(s_xt, 2 * c + k + 1)
                        for j in range(J):
                            mm = nc.tensor.transpose(bank[TB[k]][:, j * P:(j + 1) * P],
                                                     xn[:, u, j, k * P:(k + 1) * P], ident[:])
                        mm.then_inc(s_tr, 1)

                def gate_up(b, u, h):
                    c = 2 * b + u
                    if h == 0:
                        t.wait_ge(s_xt, 2 + 2 * c + 2)
                    t.wait_ge(s_h, HT * c + h + 1)
                    for w_, o in ((wg_t, 4), (wu_t, 5)):
                        mm = cut_products(bank[o + 2 * (h % 2)][:],
                                          [(w_[:, :, k, h * P:(h + 1) * P], xnt[:, u, :, k]) for k in range(KT)])
                    mm.then_inc(s_gu, 1)

                def down(b, u, more):
                    c = 2 * b + u
                    t.wait_ge(s_hl, 2 + HT * (c + 1))
                    if more:
                        t.wait_ge(s_x2, 2 * (c + 1) + 2)
                    for w in range(2):
                        for i in range(2):
                            tok = slice((2 * w + i) * P, (2 * w + i + 1) * P)
                            mm = cut_products(bank[OB[w]][:, i * D:(i + 1) * D],
                                              [(ht[:, u, :, h, tok], wd_t[:, :, h]) for h in range(HT)])
                        mm.then_inc(s_y, 1)

                def chunk(b, u, more):
                    if more:
                        project3(t, b + u, 1 - u)
                    for h in range(2, HT - 1):
                        gate_up(b, u, h)
                    if more:
                        turn(b + u, 1 - u)
                    gate_up(b, u, HT - 1)
                    if more:
                        gate_up(b + u, 1 - u, 0)
                        gate_up(b + u, 1 - u, 1)
                    down(b, u, more)

                turn(0, 0)
                gate_up(0, 0, 0)
                gate_up(0, 0, 1)
                sweep(t, chunk)
                barrier(t, 6)


_INS = ["x", "ctx_1024", "mask_BxSxS2_bk1", "L0_attn_Wq", "L0_attn_bq", "L0_attn_Wk", "L0_attn_bk",
        "L0_attn_Wv", "L0_attn_bv", "L0_attn_Wo", "L0_attn_bo", "L0_attn_W_cross",
        "L0_attn_shift_weights", "L0_attn_gate", "L0_xattn_Wq", "L0_xattn_Wk", "L0_xattn_Wv",
        "L0_xattn_Wo", "L0_ffn_w_gate", "L0_ffn_w_up", "L0_ffn_w_down"]


def kernel(**inputs):
    import numpy as np
    import concourse.bacc as bacc
    from concourse.bass_utils import run_bass_kernel_spmd

    nc = bacc.Bacc("TRN2", target_bir_lowering=False, num_devices=1)
    arrays, args = {}, []
    for name in _INS:
        a = np.ascontiguousarray(inputs[name])
        arrays[name] = a
        args.append(nc.dram_tensor(name, a.shape, mybir.dt.from_np(a.dtype), kind="ExternalInput").ap())
    out = nc.dram_tensor("out", inputs["x"].shape, F32, kind="ExternalOutput").ap()
    program(nc, *args, out)
    r = run_bass_kernel_spmd(nc, [arrays], core_ids=[0])
    return r.results[0]["out"]
```
